# Optimizing a Trainium2 kernel written in Bass

```python
import numpy as np
import jax
import jax.numpy as jnp

def _softmax(x, axis=-1):
    return jax.nn.softmax(x, axis=axis)

def _gelu(x):
    return jax.nn.gelu(x, approximate=True)

def _silu(x):
    return jax.nn.silu(x)

def _sigmoid(x):
    return jax.nn.sigmoid(x)

def _layernorm(x, axis=-1, eps=1e-05):
    m = jnp.mean(x, axis=axis, keepdims=True)
    v = jnp.var(x, axis=axis, keepdims=True)
    return (x - m) / jnp.sqrt(v + eps)

def _scatter_add(tgt, idx, src, axis=0):
    return tgt.at[idx].add(src)

def _segment_sum(src, seg, n):
    return jax.ops.segment_sum(src, seg, n)
kernel_name = 'mk_hybrid_d1_jaxref_r4_deb990'

def setup_inputs(seed: int=0):
    np.random.seed(seed)
    _w = jnp.asarray

    def _L0_attn_a_setup():
        import jax, jax.numpy as jnp
        import numpy as np
        NUM_BUCKETS = 63

        def _rp_bucket(N):
            rel = jnp.arange(N)[None, :] - jnp.arange(N)[:, None]
            half = NUM_BUCKETS // 2
            return (jnp.clip(rel, -half, half) + half).astype(jnp.int32)
        key = jax.random.key(seed)
        ks = jax.random.split(key, 7)
        B, N, C, H = (4, 256, 256, 16)
        hd = C // H
        g = lambda k, shp, sc: jax.random.normal(k, shp, jnp.float32) * sc
        return {'x': g(ks[0], (B, N, C), 1.0), 'w_qkv': g(ks[1], (3 * C, C), C ** (-0.5)), 'w_proj': g(ks[2], (C, C), C ** (-0.5)), 'b_proj': jnp.zeros((C,), jnp.float32), 'rpe_q_table': g(ks[3], (H, hd, NUM_BUCKETS), 0.02), 'rpe_k_table': g(ks[4], (H, hd, NUM_BUCKETS), 0.02), 'rpe_v_table': g(ks[5], (H, NUM_BUCKETS, hd), 0.02)}
    _L0_attn_a_in = _L0_attn_a_setup()

    def _L0_attn_b_setup():
        import jax, jax.numpy as jnp
        import numpy as np
        B, T, DIM = (2, 512, 256)
        N_HEADS, HEAD_DIM, WINDOW = (16, 64, 128)
        EPS = 0.01

        def _rmsnorm(x, gamma, eps):
            rms = jnp.sqrt(jnp.mean(jnp.square(x), axis=-1, keepdims=True) + eps)
            return x / rms * gamma
        key = jax.random.key(seed)
        ks = jax.random.split(key, 5)
        s = 1.0 / np.sqrt(DIM)
        return {'x': jax.random.normal(ks[0], (B, T, DIM), jnp.float32), 'wq': jax.random.normal(ks[1], (N_HEADS * HEAD_DIM, DIM), jnp.float32) * s, 'wk': jax.random.normal(ks[2], (N_HEADS * HEAD_DIM, DIM), jnp.float32) * s, 'wv': jax.random.normal(ks[3], (N_HEADS * HEAD_DIM, DIM), jnp.float32) * s, 'wo': jax.random.normal(ks[4], (DIM, N_HEADS * HEAD_DIM), jnp.float32) * s, 'q_gamma': jnp.ones((N_HEADS * HEAD_DIM,), jnp.float32), 'k_gamma': jnp.ones((N_HEADS * HEAD_DIM,), jnp.float32)}
    _L0_attn_b_in = _L0_attn_b_setup()

    def _L0_ffn_setup():
        import jax, jax.numpy as jnp
        import numpy as np
        E = 16
        F_C = 2.0
        D = 256
        I = 4 * D
        IS = 2 * D
        B, S = (4, 256)
        key = jax.random.key(seed)
        ks = jax.random.split(key, 8)
        w = 0.02
        return {'hidden_states': jax.random.normal(ks[0], (B, S, D), dtype=jnp.float32), 'gate_w': jax.random.normal(ks[1], (E, D), dtype=jnp.float32) * w, 'Wg': jax.random.normal(ks[2], (E, I, D), dtype=jnp.float32) * w, 'Wu': jax.random.normal(ks[3], (E, I, D), dtype=jnp.float32) * w, 'Wd': jax.random.normal(ks[4], (E, D, I), dtype=jnp.float32) * w, 'Sg': jax.random.normal(ks[5], (IS, D), dtype=jnp.float32) * w, 'Su': jax.random.normal(ks[6], (IS, D), dtype=jnp.float32) * w, 'Sd': jax.random.normal(ks[7], (D, IS), dtype=jnp.float32) * w}
    _L0_ffn_in = _L0_ffn_setup()
    _d = {'L0_attn_a_x': _L0_attn_a_in['x'], 'L0_attn_a_w_qkv': _L0_attn_a_in['w_qkv'], 'L0_attn_a_w_proj': _L0_attn_a_in['w_proj'], 'L0_attn_a_b_proj': _L0_attn_a_in['b_proj'], 'L0_attn_a_rpe_q_table': _L0_attn_a_in['rpe_q_table'], 'L0_attn_a_rpe_k_table': _L0_attn_a_in['rpe_k_table'], 'L0_attn_a_rpe_v_table': _L0_attn_a_in['rpe_v_table'], 'L0_attn_b_wq': _L0_attn_b_in['wq'], 'L0_attn_b_wk': _L0_attn_b_in['wk'], 'L0_attn_b_wv': _L0_attn_b_in['wv'], 'L0_attn_b_wo': _L0_attn_b_in['wo'], 'L0_attn_b_q_gamma': _L0_attn_b_in['q_gamma'], 'L0_attn_b_k_gamma': _L0_attn_b_in['k_gamma'], 'L0_ffn_gate_w': _L0_ffn_in['gate_w'], 'L0_ffn_Wg': _L0_ffn_in['Wg'], 'L0_ffn_Wu': _L0_ffn_in['Wu'], 'L0_ffn_Wd': _L0_ffn_in['Wd'], 'L0_ffn_Sg': _L0_ffn_in['Sg'], 'L0_ffn_Su': _L0_ffn_in['Su'], 'L0_ffn_Sd': _L0_ffn_in['Sd']}
    _x0 = _d['L0_attn_a_x']
    _d['L0_attn_a_x'] = jax.random.normal(jax.random.fold_in(jax.random.key(seed), 1), (8, 512, 256), dtype=_x0.dtype)
    del _x0
    return _d

def reference(L0_attn_a_x, L0_attn_a_w_qkv, L0_attn_a_w_proj, L0_attn_a_b_proj, L0_attn_a_rpe_q_table, L0_attn_a_rpe_k_table, L0_attn_a_rpe_v_table, L0_attn_b_wq, L0_attn_b_wk, L0_attn_b_wv, L0_attn_b_wo, L0_attn_b_q_gamma, L0_attn_b_k_gamma, L0_ffn_gate_w, L0_ffn_Wg, L0_ffn_Wu, L0_ffn_Wd, L0_ffn_Sg, L0_ffn_Su, L0_ffn_Sd):

    def _L0_attn_a_ref(x, w_qkv, w_proj, b_proj, rpe_q_table, rpe_k_table, rpe_v_table):
        import jax, jax.numpy as jnp
        import numpy as np
        NUM_BUCKETS = 63

        def _rp_bucket(N):
            rel = jnp.arange(N)[None, :] - jnp.arange(N)[:, None]
            half = NUM_BUCKETS // 2
            return (jnp.clip(rel, -half, half) + half).astype(jnp.int32)
        B, N, C = x.shape
        H = rpe_k_table.shape[0]
        hd = C // H
        scale = hd ** (-0.5)
        qkv = (x @ w_qkv.T).reshape(B, N, 3, H, hd).transpose(2, 0, 3, 1, 4)
        q, k, v = (qkv[0] * scale, qkv[1], qkv[2])
        attn = jnp.einsum('bhid,bhjd->bhij', q, k)
        rp = _rp_bucket(N)
        idx = rp[None, None]
        qL = jnp.einsum('bhid,hdm->bhim', q, rpe_k_table)
        attn = attn + jnp.take_along_axis(qL, idx, axis=-1)
        kL = jnp.einsum('bhjd,hdm->bhjm', k * scale, rpe_q_table)
        attn = attn + jnp.swapaxes(jnp.take_along_axis(kL, idx, axis=-1), 2, 3)
        attn = jax.nn.softmax(attn, axis=-1)
        out = jnp.einsum('bhij,bhjd->bhid', attn, v)
        a_t = attn.transpose(2, 3, 0, 1)
        S = jax.vmap(lambda a, seg: jax.ops.segment_sum(a, seg, num_segments=NUM_BUCKETS))(a_t, rp)
        out = out + jnp.einsum('inbh,hnd->bhid', S, rpe_v_table)
        x_out = out.transpose(0, 2, 1, 3).reshape(B, N, C)
        return x_out @ w_proj.T + b_proj

    def _L0_attn_b_ref(x, wq, wk, wv, wo, q_gamma, k_gamma):
        import jax, jax.numpy as jnp
        import numpy as np
        B, T, DIM = (2, 512, 256)
        N_HEADS, HEAD_DIM, WINDOW = (16, 64, 128)
        EPS = 0.01

        def _rmsnorm(x, gamma, eps):
            rms = jnp.sqrt(jnp.mean(jnp.square(x), axis=-1, keepdims=True) + eps)
            return x / rms * gamma
        Bx, Tx, _ = x.shape
        H, D = (N_HEADS, HEAD_DIM)
        q = x @ wq.T
        k = x @ wk.T
        v = (x @ wv.T).reshape(Bx, Tx, H, D).transpose(0, 2, 1, 3)
        q = _rmsnorm(q, q_gamma, 1e-06).reshape(Bx, Tx, H, D).transpose(0, 2, 1, 3)
        k = _rmsnorm(k, k_gamma, 1e-06).reshape(Bx, Tx, H, D).transpose(0, 2, 1, 3)
        scale = 1.0 / np.sqrt(D)
        scores = jnp.einsum('bhqd,bhkd->bhqk', q, k) * scale
        slopes = jnp.asarray([2.0 ** (-8.0 / H * (h + 1)) for h in range(H)], jnp.float32)
        pos = jnp.arange(Tx)
        dist = (pos[None, :] - pos[:, None]).astype(jnp.float32)
        scores = scores + slopes[None, :, None, None] * dist[None, None]
        j_minus_i = pos[None, :] - pos[:, None]
        mask = (j_minus_i > 0) | (j_minus_i < -WINDOW)
        scores = jnp.where(mask[None, None], -1000000000.0, scores)
        attn = jax.nn.softmax(scores, axis=-1)
        out = jnp.einsum('bhqk,bhkd->bhqd', attn, v)
        out = out.transpose(0, 2, 1, 3).reshape(Bx, Tx, H * D)
        return out @ wo.T

    def _L0_ffn_ref(hidden_states, gate_w, Wg, Wu, Wd, Sg, Su, Sd):
        import jax, jax.numpy as jnp
        import numpy as np
        E = 16
        F_C = 2.0
        D = 256
        I = 4 * D
        IS = 2 * D
        B, S = (4, 256)
        b, s, d = hidden_states.shape
        T = b * s
        C = int(T * F_C / E)
        flat_x = hidden_states.reshape(T, d)
        logits = flat_x @ gate_w.T
        scores = jax.nn.softmax(logits, axis=-1).T
        topk_weight, topk_idx = jax.lax.top_k(scores, C)
        xg = flat_x[topk_idx]
        g = jnp.einsum('ecd,eid->eci', xg, Wg)
        u = jnp.einsum('ecd,eid->eci', xg, Wu)
        h = jax.nn.gelu(g, approximate=False) * u
        eo = jnp.einsum('eci,edi->ecd', h, Wd)
        eo = eo * topk_weight[..., None]
        flat_out = jnp.zeros_like(flat_x).at[topk_idx.reshape(-1)].add(eo.reshape(-1, d))
        out = flat_out.reshape(b, s, d)
        sg = hidden_states @ Sg.T
        su = hidden_states @ Su.T
        shared = jax.nn.gelu(sg, approximate=False) * su @ Sd.T
        return out + shared
    x = L0_attn_a_x
    x = x + _L0_attn_a_ref(_layernorm(x, axis=-1), L0_attn_a_w_qkv, L0_attn_a_w_proj, L0_attn_a_b_proj, L0_attn_a_rpe_q_table, L0_attn_a_rpe_k_table, L0_attn_a_rpe_v_table)
    x = x + _L0_ffn_ref(_layernorm(x, axis=-1), L0_ffn_gate_w, L0_ffn_Wg, L0_ffn_Wu, L0_ffn_Wd, L0_ffn_Sg, L0_ffn_Su, L0_ffn_Sd)
    x = x + _L0_attn_b_ref(_layernorm(x, axis=-1), L0_attn_b_wq, L0_attn_b_wk, L0_attn_b_wv, L0_attn_b_wo, L0_attn_b_q_gamma, L0_attn_b_k_gamma)
    x = x + _L0_ffn_ref(_layernorm(x, axis=-1), L0_ffn_gate_w, L0_ffn_Wg, L0_ffn_Wu, L0_ffn_Wd, L0_ffn_Sg, L0_ffn_Su, L0_ffn_Sd)
    return x

_drawn_inputs = setup_inputs


def setup_inputs(seed=0):
    import zlib

    import numpy as np

    out = dict(_drawn_inputs(seed))
    spreads = {'L0_attn_a_b_proj': (0.0, 0.1),
     'L0_attn_b_q_gamma': (1.0, 0.2),
     'L0_attn_b_k_gamma': (1.0, 0.2)}
    factors = {'L0_attn_a_rpe_q_table': 7.088,
     'L0_attn_a_rpe_k_table': 8.0,
     'L0_ffn_gate_w': 7.517,
     'L0_ffn_Wg': 6.954,
     'L0_ffn_Wu': 6.765,
     'L0_ffn_Wd': 6.763,
     'L0_ffn_Sg': 4.279,
     'L0_ffn_Su': 4.076,
     'L0_ffn_Sd': 3.956}
    for name, (base, spread) in spreads.items():
        noise = np.random.default_rng([zlib.crc32(name.encode()), seed]).standard_normal(out[name].shape)
        drawn = base * np.exp(spread * noise) if base else spread * noise
        out[name] = jnp.asarray(drawn.astype(out[name].dtype))
    for name, factor in factors.items():
        out[name] = (out[name] * factor).astype(out[name].dtype)
    return out
```

```python
from contextlib import ExitStack, contextmanager

import numpy as np

import concourse.bass as bass
from concourse import mybir

F32 = mybir.dt.float32
I32 = mybir.dt.int32
ACT = mybir.ActivationFunctionType
ALU = mybir.AluOpType
AX = mybir.AxisListType
ds = bass.ds

P = 128
B, T, C = 8, 512, 256
NT = T // P
KC = C // P
LN_EPS = 1e-5

AH, AD = 16, 16
HG = 4
NG = AH // HG
BUCKETS = 63
HALF = BUCKETS // 2
XB = BUCKETS + 1
WIN = 192
A_SCALE = AD ** -0.5

BH, BD = 16, 64
BC = BH * BD
WINDOW = 128
RMS_EPS = 1e-6
B_SCALE = BD ** -0.5

E = 16
CAP = B * T * 2 // E
CT = CAP // P
I_E = 4 * C
I_S = 2 * C


class Chain:

    def __init__(self, engine, sem, start=0):
        self.engine, self.sem, self.start, self.n = engine, sem, start, 0

    def link(self, instruction):
        instruction.then_inc(self.sem, 1)
        self.n += 1
        self.engine.wait_ge(self.sem, self.start + self.n)

    def mark(self, instruction):
        instruction.then_inc(self.sem, 1)
        self.n += 1

    def settle(self):
        self.engine.wait_ge(self.sem, self.start + self.n)


def hold(engine, sem, value, held):
    engine.wait_ge(sem, value)
    engine.sem_inc(held, 1)


class Store:

    def __init__(self, nc, ctx, tag):
        self.nc, self.ctx, self.tag = nc, ctx, tag
        self.sems = []

    def sb(self, name, shape, dt=F32):
        return self.ctx.enter_context(self.nc.sbuf_tensor(f"{self.tag}_{name}", shape, dt))

    def ps(self, name, shape):
        return self.ctx.enter_context(self.nc.psum_tensor(f"{self.tag}_{name}", shape, F32))

    def sem(self, name):
        self.sems.append(self.ctx.enter_context(self.nc.semaphore(f"{self.tag}_{name}")))
        return self.sems[-1]

    @contextmanager
    def programs(self):
        with self.nc.Block() as block:
            yield block
        with self.nc.Block() as ending:
            @ending.gpsimd
            def _(pool):
                for sem in self.sems:
                    pool.sem_clear(sem)


def by_token(dram, n):
    return dram[ds(n, 1)].rearrange("a (t p) c -> p (a t) c", p=P)


def by_channel(dram, n):
    return dram[ds(n, 1)].rearrange("a p k t -> p (a k) t")


def norm_stage(nc, tag, ident_d, x_d, xnT_d, attn=None, x1_d=None, xn_d=None, gate=None, scores=None):
    with ExitStack() as ctx:
        s = Store(nc, ctx, tag)
        ident = s.sb("ident", [P, P])
        x = s.sb("x", [P, 2, NT, C])
        xn = s.sb("xn", [P, 2, NT, C])
        xnT = s.sb("xnT", [P, 2, KC, T])
        stats = s.sb("stats", [P, NT, 6])
        mv = s.sb("mv", [P, NT, 2])
        var = s.sb("var", [P, NT, 1])
        minus_half = s.sb("minus_half", [P, NT, 1])
        rstd = s.sb("rstd", [P, NT, 1])
        ps_xT = [s.ps(f"ps_xT{k}", [P, T]) for k in range(KC)]
        const_in = s.sem("const_in")
        x_in = [s.sem(f"x_in{p}") for p in range(2)]
        chain = s.sem("chain")
        held = s.sem("held")
        half_set = s.sem("half_set")
        mv_ready = s.sem("mv_ready")
        rstd_ready = s.sem("rstd_ready")
        xn_ready = s.sem("xn_ready")
        xT_ready = s.sem("xT_ready")
        xnT_ready = s.sem("xnT_ready")
        stored = [s.sem(f"stored{p}") for p in range(2)]
        n_const, n_store, n_load = 1, 1, 1
        if xn_d is not None:
            n_store += 1
        if attn:
            o_d, wT_d, bias_d = attn
            n_const += 2
            n_store += 1
            n_load += 1
            o = s.sb("o", [P, 2, NT, C])
            oT = s.sb("oT", [P, KC, T])
            wT = s.sb("wT", [P, KC, C])
            bias = s.sb("bias", [P, C])
            ps_oT = [s.ps(f"ps_oT{k}", [P, T]) for k in range(KC)]
            ps_y = [s.ps(f"ps_y{k}", [P, T]) for k in range(2)]
            oT_ready = s.sem("oT_ready")
            oT_copied = s.sem("oT_copied")
            y_ready = s.sem("y_ready")
        if gate is not None:
            n_const += 1
            gwT = s.sb("gwT", [P, KC, E])
            sm = s.sb("sm", [P, NT, E])
            mx = s.sb("mx", [P, NT, 1])
            total = s.sb("total", [P, NT, 1])
            ps_l = s.ps("ps_l", [P, NT, E])
            logits_ready = s.sem("logits_ready")
            shifted = s.sem("shifted")
            exped = s.sem("exped")
        block = ctx.enter_context(s.programs())

        @block.sync
        def _(sp):
            sp.dma_start(ident[:, :], ident_d).then_inc(const_in, 16)
            if attn:
                sp.dma_start(wT[:, :, :], wT_d).then_inc(const_in, 16)
                sp.dma_start(bias[:, :], bias_d).then_inc(const_in, 16)
            if gate is not None:
                sp.dma_start(gwT[:, :, :], gate).then_inc(const_in, 16)

            def load(n, p):
                sp.dma_start(x[:, p, :, :], by_token(x_d, n)).then_inc(x_in[p], 16)
                if attn:
                    sp.dma_start(o[:, p, :, :], by_token(o_d, n)).then_inc(x_in[p], 16)

            def store(i, p, more):
                n = 2 * i + p
                sp.wait_ge(xnT_ready, KC * n + 2 * KC)
                sp.dma_start(by_channel(xnT_d, n), xnT[:, p, :, :]).then_inc(stored[p], 16)
                if xn_d is not None:
                    sp.dma_start(by_token(xn_d, n), xn[:, p, :, :]).then_inc(stored[p], 16)
                if attn:
                    sp.dma_start(by_token(x1_d, n), x[:, p, :, :]).then_inc(stored[p], 16)
                if more:
                    sp.wait_ge(stored[p], 16 * n_store * i + 32 * n_store)
                    load(n + 2, p)

            for p in range(2):
                sp.sem_inc(stored[p], 16 * n_store)
            load(0, 0)
            load(1, 1)
            with nc.sync.Fori(0, B // 2 - 1) as i:
                store(i, 0, True)
                store(i, 1, True)
            for p in range(2):
                store(B // 2 - 1, p, False)
            for p in range(2):
                sp.wait_ge(stored[p], 16 * n_store * (B // 2 + 1))

        @block.tensor
        def _(pe):
            pe.wait_ge(const_in, 16 * n_const)
            with nc.tensor.Fori(0, B // 2) as i:
                for p in range(2):
                    n = 2 * i + p
                    if attn:
                        pe.wait_ge(x_in[p], 16 * n_load * i + 16 * n_load)
                        for k in range(KC):
                            for t in range(NT):
                                last = nc.tensor.transpose(ps_oT[k][:, t * P:(t + 1) * P],
                                                           o[:, p, t, k * P:(k + 1) * P], ident[:, :])
                            last.then_inc(oT_ready, 1)
                        pe.wait_ge(oT_copied, KC * n + KC)
                        for t in range(NT):
                            for k in range(KC):
                                last = nc.tensor.matmul(ps_y[t // 2][:, (t % 2) * C:(t % 2 + 1) * C],
                                                        oT[:, k, t * P:(t + 1) * P], wT[:, k, :],
                                                        start=(k == 0), stop=(k == KC - 1))
                            if t % 2:
                                last.then_inc(y_ready, 1)
                    pe.wait_ge(xn_ready, n + 1)
                    pe.wait_ge(xnT_ready, KC * n + KC)
                    for k in range(KC):
                        for t in range(NT):
                            last = nc.tensor.transpose(ps_xT[k][:, t * P:(t + 1) * P],
                                                       xn[:, p, t, k * P:(k + 1) * P], ident[:, :])
                        last.then_inc(xT_ready, 1)
                    if gate is not None:
                        pe.wait_ge(xnT_ready, KC * n + 2 * KC)
                        for t in range(NT):
                            for k in range(KC):
                                last = nc.tensor.matmul(ps_l[:, t, :], xnT[:, p, k, t * P:(t + 1) * P], gwT[:, k, :],
                                                        start=(k == 0), stop=(k == KC - 1))
                        last.then_inc(logits_ready, 1)

        @block.scalar
        def _(act):
            act.sem_inc(xnT_ready, KC)
            with nc.scalar.Fori(0, B // 2) as i:
                for p in range(2):
                    n = 2 * i + p
                    if attn:
                        for k in range(KC):
                            act.wait_ge(oT_ready, KC * n + k + 1)
                            nc.scalar.copy(oT[:, k, :], ps_oT[k][:, :]).then_inc(oT_copied, 1)
                    act.wait_ge(stored[p], 16 * n_store * i + 16 * n_store)
                    for k in range(KC):
                        act.wait_ge(xT_ready, KC * n + k + 1)
                        nc.scalar.copy(xnT[:, p, k, :], ps_xT[k][:, :]).then_inc(xnT_ready, 1)
                    if gate is not None:
                        act.wait_ge(shifted, n + 1)
                        nc.scalar.activation(sm[:, :, :], sm[:, :, :], ACT.Exp).then_inc(exped, 1)

        @block.gpsimd
        def _(pool):
            nc.gpsimd.memset(minus_half[:, :, :], -0.5).then_inc(half_set, 1)
            pool.wait_ge(half_set, 1)
            with nc.gpsimd.Fori(0, B) as n:
                pool.wait_ge(mv_ready, n + 1)
                nc.gpsimd.tensor_tensor(rstd[:, :, :], var[:, :, :], minus_half[:, :, :], ALU.pow).then_inc(rstd_ready, 1)

        @block.vector
        def _(dve):
            LINKS = 2 * NT + (1 if attn else 0) + (2 if attn else 0) + (3 if gate is not None else 0)
            if attn:
                dve.wait_ge(const_in, 16 * n_const)
            with nc.vector.Fori(0, B // 2) as i:
                for p in range(2):
                    n = 2 * i + p
                    ch = Chain(dve, chain, LINKS * n)
                    dve.wait_ge(x_in[p], 16 * n_load * i + 16 * n_load)
                    if attn:
                        ch.link(nc.vector.tensor_tensor(x[:, p, :, :], x[:, p, :, :],
                                                        bias[:, :].unsqueeze(1).to_broadcast([P, NT, C]), ALU.add))
                        for h in range(2):
                            dve.wait_ge(y_ready, 2 * n + h + 1)
                            xh = x[:, p, 2 * h:2 * h + 2, :]
                            ch.mark(nc.vector.tensor_tensor(xh, ps_y[h][:, :].rearrange("p (t c) -> p t c", c=C), xh, ALU.add))
                        ch.settle()
                    for t in range(NT):
                        ch.mark(nc.vector.bn_stats(stats[:, t, :], x[:, p, t, :]))
                    ch.settle()
                    dve.sem_inc(held, 1)
                    for t in range(NT):
                        ch.mark(nc.vector.bn_aggr(mv[:, t, :], stats[:, t, :]))
                    ch.settle()
                    nc.vector.tensor_scalar(var[:, :, :], mv[:, :, 1:2], LN_EPS, None, ALU.add).then_inc(mv_ready, 1)
                    dve.wait_ge(rstd_ready, n + 1)
                    dve.wait_ge(stored[p], 16 * n_store * i + 16 * n_store)
                    for t in range(NT):
                        last = nc.vector.tensor_scalar(xn[:, p, t, :], x[:, p, t, :], mv[:, t, 0:1], rstd[:, t, :],
                                                       ALU.subtract, ALU.mult)
                    last.then_inc(xn_ready, 1)
                    if gate is not None:
                        dve.wait_ge(logits_ready, n + 1)
                        ch.link(nc.vector.reduce_max(mx[:, :, :], ps_l[:, :, :], AX.X))
                        nc.vector.tensor_tensor(sm[:, :, :], ps_l[:, :, :], mx[:, :, :].to_broadcast([P, NT, E]),
                                                ALU.subtract).then_inc(shifted, 1)
                        dve.wait_ge(exped, n + 1)
                        ch.link(nc.vector.reduce_sum(total[:, :, :], sm[:, :, :], AX.X))
                        ch.link(nc.vector.reciprocal(total[:, :, :], total[:, :, :]))
                        nc.vector.tensor_tensor(scores[:, :, ds(n, 1), :].rearrange("p t a e -> p (t a) e"), sm[:, :, :],
                                                total[:, :, :].to_broadcast([P, NT, E]), ALU.mult)
                    assert ch.n == LINKS


def route_stage(nc, tag, const, scores, slot_token, slot_weight):
    FLOOR = 2.0 ** -126
    EXPONENT = [2.0 ** (2 ** k) for k in range(6, -1, -1)]
    MANTISSA = [2.0 ** -k for k in range(1, 24)]
    ROUNDS = 1 + len(EXPONENT) + len(MANTISSA)
    with ExitStack() as ctx:
        s = Store(nc, ctx, tag)
        ident = s.sb("ident", [P, P])
        same = s.sb("same", [P, P])
        before = s.sb("before", [P, P])
        iota = s.sb("iota", [P, P])
        token = s.sb("token", [P, NT * B])
        st = s.sb("st", [P, T])
        work = s.sb("work", [P, T])
        equal = s.sb("equal", [P, T])
        sel = s.sb("sel", [P, T])
        ones = s.sb("ones", [P, T])
        pos = s.sb("pos", [P, T])
        posi = s.sb("posi", [P, 2, T], I32)
        parts = s.sb("parts", [P, 2, T])
        partsT = s.sb("partsT", [P, 2, NT, P])
        thr = s.sb("thr", [P, 1])
        expo = s.sb("expo", [P, 1])
        cand = s.sb("cand", [P, 1])
        count = s.sb("count", [P, 1])
        got = s.sb("got", [P, 1])
        need = s.sb("need", [P, 1])
        offset = s.sb("offset", [P, 1])
        hit = s.sb("hit", [P, NT * P, CT])
        value = s.sb("value", [P, NT * P, CT, 2])
        onehot = s.sb("onehot", [P, 2, NT * B, P])
        found = s.sb("found", [P, E, CT, 2])
        ps_t = [s.ps(f"ps_t{k}", [P, T]) for k in range(2)]
        ps_c = s.ps("ps_c", [P, 1])
        ps_f = [s.ps(f"ps_f{k}", [P, CT * 2]) for k in range(2)]
        const_in = s.sem("const_in")
        t_ready = s.sem("t_ready")
        chain = s.sem("chain")
        counted = s.sem("counted")
        summed = s.sem("summed")
        parts_ready = s.sem("parts_ready")
        parts_T = s.sem("parts_T")
        hot_ready = s.sem("hot_ready")
        found_ready = s.sem("found_ready")
        taken = s.sem("taken")
        block = ctx.enter_context(s.programs())

        @block.sync
        def _(sp):
            for tile, dram in ((ident, "ident"), (same, "same"), (before, "before"), (iota, "iota"), (token, "token")):
                sp.dma_start(tile[:, :], const[dram]).then_inc(const_in, 16)

        @block.tensor
        def _(pe):
            pe.wait_ge(const_in, 16 * 5)
            for t in range(NT):
                last = nc.tensor.transpose(ps_t[0][:, t * P:(t + 1) * P], scores[:, t, :, :].rearrange("p b e -> p (b e)"), ident[:, :])
            last.then_inc(t_ready, 1)
            for r in range(ROUNDS + 3):
                pe.wait_ge(counted, r + 1)
                table = same if r <= ROUNDS else before
                nc.tensor.matmul(ps_c[:, :], table[:, :], count[:, :], start=True, stop=True).then_inc(summed, 1)
            pe.wait_ge(parts_ready, 1)
            for k in range(2):
                for t in range(NT):
                    last = nc.tensor.transpose(ps_t[k][:, t * P:(t + 1) * P], parts[:, k, t * P:(t + 1) * P], ident[:, :])
            last.then_inc(parts_T, 1)
            with nc.tensor.Fori(0, E // 2) as i:
                for q in range(2):
                    e = 2 * i + q
                    pe.wait_ge(hot_ready, e + 1)
                    pe.wait_ge(taken, e + 1)
                    for m in range(NT * B):
                        last = nc.tensor.matmul(ps_f[q][:, :], onehot[:, q, m, :],
                                                value[:, ds(m * E + e, 1), :, :].rearrange("p a c v -> p (a c v)"),
                                                start=(m == 0), stop=(m == NT * B - 1))
                    last.then_inc(found_ready, 1)

        @block.vector
        def _(dve):
            ch = Chain(dve, chain)
            rounds = [0]

            def total(count_of, op, scalar):
                nc.vector.tensor_scalar(work[:, :], count_of, scalar, None, op, op1=ALU.add, accum_out=count[:, :]).then_inc(counted, 1)
                rounds[0] += 1
                dve.wait_ge(summed, rounds[0])

            dve.sem_inc(taken, 2)
            nc.vector.memset(ones[:, :], 1.0)
            ch.mark(nc.vector.memset(cand[:, :], FLOOR))
            dve.wait_ge(const_in, 16 * 5)
            dve.wait_ge(t_ready, 1)
            ch.mark(nc.vector.tensor_copy(st[:, :], ps_t[0][:, :]))
            ch.settle()
            total(st[:, :], ALU.is_ge, cand[:, :])
            ch.link(nc.vector.tensor_scalar(thr[:, :], ps_c[:, :], CAP - 0.5, cand[:, :], ALU.is_ge, ALU.mult))

            def keep():
                ch.link(nc.vector.tensor_scalar(got[:, :], ps_c[:, :], CAP - 0.5, cand[:, :], ALU.is_ge, ALU.mult))
                ch.link(nc.vector.tensor_tensor(thr[:, :], thr[:, :], got[:, :], ALU.max))

            for f in EXPONENT:
                ch.link(nc.vector.tensor_scalar(cand[:, :], thr[:, :], f, None, ALU.mult))
                total(st[:, :], ALU.is_ge, cand[:, :])
                keep()
            ch.link(nc.vector.tensor_copy(expo[:, :], thr[:, :]))
            for f in MANTISSA:
                ch.link(nc.vector.scalar_tensor_tensor(cand[:, :], expo[:, :], f, thr[:, :], ALU.mult, ALU.add))
                total(st[:, :], ALU.is_ge, cand[:, :])
                keep()
            total(st[:, :], ALU.is_gt, thr[:, :])
            ch.link(nc.vector.tensor_scalar(need[:, :], ps_c[:, :], -1.0, float(CAP), ALU.mult, ALU.add))
            total(st[:, :], ALU.is_equal, thr[:, :])
            ch.link(nc.vector.tensor_copy(offset[:, :], ps_c[:, :]))
            ch.link(nc.vector.tensor_scalar(equal[:, :], st[:, :], thr[:, :], None, ALU.is_equal))
            ch.link(nc.vector.tensor_tensor_scan(pos[:, :], ones[:, :], equal[:, :], offset[:, :], ALU.mult, ALU.add))
            ch.link(nc.vector.scalar_tensor_tensor(equal[:, :], pos[:, :], need[:, :], equal[:, :], ALU.is_le, ALU.mult))
            ch.link(nc.vector.scalar_tensor_tensor(sel[:, :], st[:, :], thr[:, :], equal[:, :], ALU.is_gt, ALU.add))
            total(sel[:, :], ALU.mult, 1.0)
            ch.link(nc.vector.tensor_copy(offset[:, :], ps_c[:, :]))
            ch.link(nc.vector.tensor_tensor_scan(pos[:, :], ones[:, :], sel[:, :], offset[:, :], ALU.mult, ALU.add))
            ch.link(nc.vector.tensor_tensor(pos[:, :], pos[:, :], sel[:, :], ALU.mult))
            ch.link(nc.vector.tensor_scalar(pos[:, :], pos[:, :], -1.0, None, ALU.add))
            ch.link(nc.vector.tensor_copy(posi[:, 0, :], pos[:, :]))
            ch.link(nc.vector.tensor_single_scalar(posi[:, 1, :], posi[:, 0, :], P - 1, ALU.bitwise_and))
            ch.link(nc.vector.tensor_single_scalar(posi[:, 0, :], posi[:, 0, :], 7, ALU.arith_shift_right))
            nc.vector.tensor_copy(parts[:, :, :], posi[:, :, :]).then_inc(parts_ready, 1)
            dve.wait_ge(parts_T, 1)
            for k in range(2):
                ch.mark(nc.vector.tensor_copy(partsT[:, k, :, :].rearrange("p t r -> p (t r)"), ps_t[k][:, :]))
            ch.settle()
            slot_tile = partsT[:, 0, :, :].rearrange("p t r -> p (t r)")
            ch.link(nc.vector.tensor_tensor(hit[:, :, :], slot_tile.unsqueeze(2).to_broadcast([P, NT * P, CT]),
                                            iota[:, 0:CT].unsqueeze(1).to_broadcast([P, NT * P, CT]), ALU.is_equal))
            tok = token[:, :].unsqueeze(2).to_broadcast([P, NT * B, E * CT])
            by_tile = hit[:, :, :].rearrange("p (m e) c -> p m (e c)", e=E)
            ch.mark(nc.vector.tensor_tensor(value[:, :, :, 0].rearrange("p (m e) c -> p m (e c)", e=E), by_tile, tok, ALU.mult))
            sc = scores[:, :, :, :].rearrange("p t b e -> p (t b e)").unsqueeze(2).to_broadcast([P, NT * P, CT])
            ch.mark(nc.vector.tensor_tensor(value[:, :, :, 1], hit[:, :, :], sc, ALU.mult))
            ch.settle()
            with nc.vector.Fori(0, E // 2) as i:
                for q in range(2):
                    e = 2 * i + q
                    dve.wait_ge(taken, e + 1)
                    low = partsT[:, 1, :, :].rearrange("p t (b e) -> p (t b) e", e=E)[:, :, ds(e, 1)]
                    nc.vector.tensor_tensor(onehot[:, q, :, :], low.to_broadcast([P, NT * B, P]),
                                            iota[:, :].unsqueeze(1).to_broadcast([P, NT * B, P]), ALU.is_equal).then_inc(hot_ready, 1)
                    dve.wait_ge(found_ready, e + 1)
                    nc.vector.tensor_copy(found[:, ds(e, 1), :, :].rearrange("p a c v -> p (a c v)"), ps_f[q][:, :]).then_inc(taken, 1)
            dve.wait_ge(taken, E + 2)
            nc.vector.tensor_copy(slot_token[:, :, :], found[:, :, :, 0])
            nc.vector.tensor_copy(slot_weight[:, :, :], found[:, :, :, 1])


def hidden_pe(nc, pe, n, hidden, xT, gT, uT, ps_g, ps_u, gu_ready, h_ready):
    for j in range(hidden):
        q = j % 2
        pe.wait_ge(h_ready, hidden * n + j + 1)
        for ps, w in ((ps_g[q], gT), (ps_u[q], uT)):
            for k in range(KC):
                last = nc.tensor.matmul(ps[:, :], w[:, k, j * P:(j + 1) * P], xT[:, k, :], start=(k == 0), stop=(k == KC - 1))
        last.then_inc(gu_ready, 1)


def hidden_act(nc, act, n, hidden, ps_g, gelu, gu_ready, h_ready, gelu_ready):
    for j in range(hidden):
        act.wait_ge(gu_ready, hidden * n + j + 1)
        act.wait_ge(h_ready, hidden * n + j + 1)
        nc.scalar.activation(gelu[:, j % 2, :], ps_g[j % 2][:, :], ACT.Gelu).then_inc(gelu_ready, 1)


def hidden_dve(nc, dve, n, hidden, ps_u, gelu, hT, gelu_ready, h_ready):
    for j in range(hidden):
        dve.wait_ge(gelu_ready, hidden * n + j + 1)
        nc.vector.tensor_tensor(hT[:, j, :], gelu[:, j % 2, :], ps_u[j % 2][:, :], ALU.mult).then_inc(h_ready, 1)


def down_pe(nc, pe, n, hidden, hT, dT, ps_d, h_ready, d_ready, d_taken):
    pe.wait_ge(h_ready, hidden * n + hidden + 2)
    for t in range(NT):
        pe.wait_ge(d_taken, NT * n + t + 1)
        for j in range(hidden):
            last = nc.tensor.matmul(ps_d[t % 2][:, :], hT[:, j, t * P:(t + 1) * P], dT[:, j, :], start=(j == 0), stop=(j == hidden - 1))
        last.then_inc(d_ready, 1)


def shared_stage(nc, tag, xnT_d, x_d, gT_d, uT_d, dT_d, y_d):
    HB = I_S // P
    with ExitStack() as ctx:
        s = Store(nc, ctx, tag)
        gT = s.sb("gT", [P, KC, I_S])
        uT = s.sb("uT", [P, KC, I_S])
        dT = s.sb("dT", [P, HB, C])
        xT = s.sb("xT", [P, 2, KC, T])
        x = s.sb("x", [P, 2, NT, C])
        gelu = s.sb("gelu", [P, 2, T])
        hT = s.sb("hT", [P, 2, HB, T])
        ps_g = [s.ps(f"ps_g{q}", [P, T]) for q in range(2)]
        ps_u = [s.ps(f"ps_u{q}", [P, T]) for q in range(2)]
        ps_d = [s.ps(f"ps_d{q}", [P, C]) for q in range(2)]
        w_in = s.sem("w_in")
        xT_in = [s.sem(f"xT_in{p}") for p in range(2)]
        x_in = [s.sem(f"x_in{p}") for p in range(2)]
        gu_ready = s.sem("gu_ready")
        gelu_ready = s.sem("gelu_ready")
        h_ready = s.sem("h_ready")
        d_ready = s.sem("d_ready")
        d_taken = s.sem("d_taken")
        y_out = [s.sem(f"y_out{p}") for p in range(2)]
        block = ctx.enter_context(s.programs())

        @block.sync
        def _(sp):
            def load(n, p):
                sp.dma_start(xT[:, p, :, :], by_channel(xnT_d, n)).then_inc(xT_in[p], 16)
                sp.dma_start(x[:, p, :, :], by_token(x_d, n)).then_inc(x_in[p], 16)

            sp.dma_start(gT[:, :, :], gT_d).then_inc(w_in, 16)
            sp.dma_start(uT[:, :, :], uT_d).then_inc(w_in, 16)
            load(0, 0)
            load(1, 1)
            sp.dma_start(dT[:, :, :], dT_d).then_inc(w_in, 16)

            def store(i, p, more):
                n = 2 * i + p
                sp.wait_ge(d_taken, NT * n + NT + 2)
                sp.dma_start(by_token(y_d, n), x[:, p, :, :]).then_inc(y_out[p], 16)
                if more:
                    sp.wait_ge(y_out[p], 16 * i + 16)
                    load(n + 2, p)

            with nc.sync.Fori(0, B // 2 - 1) as i:
                store(i, 0, True)
                store(i, 1, True)
            store(B // 2 - 1, 0, False)
            store(B // 2 - 1, 1, False)
            for p in range(2):
                sp.wait_ge(y_out[p], 16 * (B // 2))

        @block.tensor
        def _(pe):
            pe.wait_ge(w_in, 16 * 3)
            with nc.tensor.Fori(0, B // 2) as i:
                for p in range(2):
                    pe.wait_ge(xT_in[p], 16 * i + 16)
                    hidden_pe(nc, pe, 2 * i + p, HB, xT[:, p, :, :], gT, uT, ps_g, ps_u, gu_ready, h_ready)
                    down_pe(nc, pe, 2 * i + p, HB, hT[:, p, :, :], dT, ps_d, h_ready, d_ready, d_taken)

        @block.scalar
        def _(act):
            with nc.scalar.Fori(0, B) as n:
                hidden_act(nc, act, n, HB, ps_g, gelu, gu_ready, h_ready, gelu_ready)

        @block.vector
        def _(dve):
            dve.sem_inc(h_ready, 2)
            dve.sem_inc(d_taken, 2)
            with nc.vector.Fori(0, B // 2) as i:
                for p in range(2):
                    n = 2 * i + p
                    hidden_dve(nc, dve, n, HB, ps_u, gelu, hT[:, p, :, :], gelu_ready, h_ready)
                    dve.wait_ge(x_in[p], 16 * i + 16)
                    for t in range(NT):
                        dve.wait_ge(d_ready, NT * n + t + 1)
                        nc.vector.tensor_tensor(x[:, p, t, :], x[:, p, t, :], ps_d[t % 2][:, :], ALU.add).then_inc(d_taken, 1)


def expert_stage(nc, tag, ident_d, xn_d, slot_token, slot_weight, gT_d, uT_d, dT_d, y_d):
    HB = I_E // P
    DONE = 16 * CT
    rows_xn = xn_d.rearrange("b t c -> (b t) c")
    rows_y = y_d.rearrange("b t c -> (b t) c")
    with ExitStack() as ctx:
        s = Store(nc, ctx, tag)
        ident = s.sb("ident", [P, P])
        gT = s.sb("gT", [P, 2, KC, I_E])
        uT = s.sb("uT", [P, 2, KC, I_E])
        dT = s.sb("dT", [P, 2, HB, C])
        index = s.sb("index", [P, 2, CT], I32)
        xg = s.sb("xg", [P, 2, CT, C])
        xT = s.sb("xT", [P, 2, KC, T])
        gelu = s.sb("gelu", [P, 2, T])
        hT = s.sb("hT", [P, HB, T])
        eo = s.sb("eo", [P, 2, CT, C])
        ps_x = [s.ps(f"ps_x{k}", [P, T]) for k in range(KC)]
        ps_g = [s.ps(f"ps_g{q}", [P, T]) for q in range(2)]
        ps_u = [s.ps(f"ps_u{q}", [P, T]) for q in range(2)]
        ps_d = [s.ps(f"ps_d{q}", [P, C]) for q in range(2)]
        ident_in = s.sem("ident_in")
        up_in = [s.sem(f"up_in{q}") for q in range(2)]
        down_in = [s.sem(f"down_in{q}") for q in range(2)]
        held = s.sem("held")
        index_ready = s.sem("index_ready")
        gathered = [s.sem(f"gathered{q}") for q in range(2)]
        x_T = s.sem("x_T")
        xT_ready = s.sem("xT_ready")
        gu_ready = s.sem("gu_ready")
        gelu_ready = s.sem("gelu_ready")
        h_ready = s.sem("h_ready")
        d_ready = s.sem("d_ready")
        d_taken = s.sem("d_taken")
        added = [s.sem(f"added{q}") for q in range(2)]
        block = ctx.enter_context(s.programs())

        @block.sync
        def _(sp):
            sp.dma_start(ident[:, :], ident_d).then_inc(ident_in, 16)

            def load(e, q):
                sp.dma_start(gT[:, q, :, :], gT_d[ds(e, 1)].rearrange("a p k i -> p (a k) i")).then_inc(up_in[q], 16)
                sp.dma_start(uT[:, q, :, :], uT_d[ds(e, 1)].rearrange("a p k i -> p (a k) i")).then_inc(up_in[q], 16)
                sp.dma_start(dT[:, q, :, :], dT_d[ds(e, 1)].rearrange("a p k i -> p (a k) i")).then_inc(down_in[q], 16)

            load(0, 0)
            load(1, 1)
            with nc.sync.Fori(0, E // 2 - 1) as i:
                for q in range(2):
                    sp.wait_ge(d_ready, CT * (2 * i + q) + CT)
                    load(2 * i + q + 2, q)

        @block.gpsimd
        def _(pool):
            def gather(e, q):
                nc.gpsimd.tensor_copy(index[:, q, :], slot_token[:, ds(e, 1), :].rearrange("p a c -> p (a c)")).then_inc(index_ready, 1)
                hold(pool, index_ready, e + 1, held)
                for t in range(CT):
                    nc.gpsimd.indirect_dma_start(xg[:, q, t, :], None, rows_xn, bass.IndirectOffsetOnAxis(index[:, q, t:t + 1], 0),
                                                 bounds_check=B * T - 1).then_inc(gathered[q], 16)

            def step(i, q, more, first=False):
                e = 2 * i + q
                if not first or q:
                    hold(pool, added[1 - q], DONE * (i + q), held)
                if more:
                    hold(pool, x_T, KC * e + KC, held)
                    gather(e + 1, 1 - q)
                for t in range(CT):
                    hold(pool, d_taken, CT * e + t + 3, held)
                    nc.gpsimd.indirect_dma_start(rows_y, bass.IndirectOffsetOnAxis(index[:, q, t:t + 1], 0), eo[:, q, t, :], None,
                                                 bounds_check=B * T - 1, compute_op=ALU.add).then_inc(added[q], 16)

            gather(0, 0)
            step(0, 0, True, first=True)
            step(0, 1, True, first=True)
            with nc.gpsimd.Fori(1, E // 2 - 1) as i:
                step(i, 0, True)
                step(i, 1, True)
            step(E // 2 - 1, 0, True)
            step(E // 2 - 1, 1, False)
            for q in range(2):
                pool.wait_ge(added[q], DONE * (E // 2))

        @block.tensor
        def _(pe):
            def transpose_rows(i, q, e):
                pe.wait_ge(gathered[q], DONE * i + DONE)
                for k in range(KC):
                    for t in range(CT):
                        last = nc.tensor.transpose(ps_x[k][:, t * P:(t + 1) * P], xg[:, q, t, k * P:(k + 1) * P], ident[:, :])
                    last.then_inc(x_T, 1)

            def step(i, q, more):
                e = 2 * i + q
                pe.wait_ge(xT_ready, KC * e + KC)
                pe.wait_ge(up_in[q], 32 * i + 32)
                hidden_pe(nc, pe, e, HB, xT[:, q, :, :], gT[:, q, :, :], uT[:, q, :, :], ps_g, ps_u, gu_ready, h_ready)
                if more:
                    transpose_rows(i + q, 1 - q, e + 1)
                pe.wait_ge(down_in[q], 16 * i + 16)
                down_pe(nc, pe, e, HB, hT, dT[:, q, :, :], ps_d, h_ready, d_ready, d_taken)

            pe.sem_inc(x_T, KC)
            pe.wait_ge(ident_in, 16)
            transpose_rows(0, 0, 0)
            with nc.tensor.Fori(0, E // 2 - 1) as i:
                step(i, 0, True)
                step(i, 1, True)
            step(E // 2 - 1, 0, True)
            step(E // 2 - 1, 1, False)

        @block.scalar
        def _(act):
            def copy_rows(e, q):
                for k in range(KC):
                    act.wait_ge(x_T, KC * e + k + 1 + KC)
                    nc.scalar.copy(xT[:, q, k, :], ps_x[k][:, :]).then_inc(xT_ready, 1)

            def step(i, q, more):
                hidden_act(nc, act, 2 * i + q, HB, ps_g, gelu, gu_ready, h_ready, gelu_ready)
                if more:
                    copy_rows(2 * i + q + 1, 1 - q)

            copy_rows(0, 0)
            with nc.scalar.Fori(0, E // 2 - 1) as i:
                step(i, 0, True)
                step(i, 1, True)
            step(E // 2 - 1, 0, True)
            step(E // 2 - 1, 1, False)

        @block.vector
        def _(dve):
            dve.sem_inc(h_ready, 2)
            dve.sem_inc(d_taken, 2)

            def step(i, q, first=False):
                e = 2 * i + q
                hidden_dve(nc, dve, e, HB, ps_u, gelu, hT, gelu_ready, h_ready)
                if not first:
                    dve.wait_ge(added[q], DONE * i)
                for t in range(CT):
                    dve.wait_ge(d_ready, CT * e + t + 1)
                    nc.vector.tensor_tensor(eo[:, q, t, :], ps_d[t % 2][:, :],
                                            slot_weight[:, ds(e, 1), t:t + 1].rearrange("p a c -> p (a c)").to_broadcast([P, C]),
                                            ALU.mult).then_inc(d_taken, 1)

            step(0, 0, first=True)
            step(0, 1, first=True)
            with nc.vector.Fori(1, E // 2) as i:
                step(i, 0)
                step(i, 1)


WINDOW_ORDER = [
    ("scores", 0), ("out_T", 0), ("out_T", 1), ("scores", 1), ("out", 0),
    ("probs_T", 0), ("q", 0), ("probs_T", 1), ("values", 0), ("q", 1),
    ("scores", 2), ("probs_T", 2), ("values", 1), ("k", 0), ("probs_T", 3), ("values", 2), ("k", 1),
    ("scores", 3), ("probs_T", 4), ("values", 3), ("v", 0), ("probs_T", 5), ("values", 4), ("v", 1),
    ("q_T", 0), ("probs_T", 6), ("values", 5), ("q_T", 1), ("k_T", 0), ("probs_T", 7), ("values", 6), ("k_T", 1), ("values", 7),
]
NEXT = ("q", "k", "v", "q_T", "k_T")
PAST = ("out_T", "out")


def window_stage(nc, tag, const, x_d, xnT_d, wqT_d, wkT_d, wvT_d, woT_d, gamma_d, bias_d, y_d):
    CH = BC // P
    HALVES = 2
    HW = BC // HALVES
    with ExitStack() as ctx:
        s = Store(nc, ctx, tag)
        ident = s.sb("ident", [P, P])
        wT = {"q": s.sb("wqT", [P, KC, BC]), "k": s.sb("wkT", [P, KC, BC]), "v": s.sb("wvT", [P, KC, BC])}
        woT = s.sb("woT", [P, CH, C])
        gamma = s.sb("gamma", [P, 2, BC])
        bias = s.sb("bias", [P, BH, 2 * P])
        minus_half = s.sb("minus_half", [P, 2])
        xT = s.sb("xT", [P, 2, KC, P])
        x = s.sb("x", [P, 2, C])
        raw = s.sb("raw", [P, 2, BC])
        square = s.sb("square", [P, HW])
        ss = s.sb("ss", [P, 2, HALVES])
        ms = s.sb("ms", [P, 2])
        rrms = s.sb("rrms", [P, 2])
        normed = s.sb("normed", [P, 2, BC])
        qT = s.sb("qT", [P, 2, CH, P])
        kT = s.sb("kT", [P, CH, T])
        v = s.sb("v", [P, NT, BC])
        score = s.sb("score", [P, 4, 2 * P])
        low = s.sb("low", [P, 4])
        prob = s.sb("prob", [P, 4, 2 * P])
        probT = s.sb("probT", [P, 2, 2, 2, P])
        rsum = s.sb("rsum", [P, 2, BH])
        rinv = s.sb("rinv", [P, 2, BH])
        o = s.sb("o", [P, 2, BC])
        oT = s.sb("oT", [P, CH, P])
        ps_s = [[s.ps(f"ps_s{q}{r}", [P, 2, 2 * P]) for r in range(2)] for q in range(2)]
        ps_p = [s.ps(f"ps_p{q}", [P, 2, 2, P]) for q in range(2)]
        ps_o = s.ps("ps_o", [P, HW])
        ps_w = s.ps("ps_w", [P, HW])
        const_in = s.sem("const_in")
        xT_in = [s.sem(f"xT_in{p}") for p in range(2)]
        x_in = [s.sem(f"x_in{p}") for p in range(2)]
        y_out = [s.sem(f"y_out{p}") for p in range(2)]
        chain = s.sem("chain")
        held = s.sem("held")
        half_set = s.sem("half_set")
        filled = s.sem("filled")
        emptied = s.sem("emptied")
        squared = s.sem("squared")
        ms_ready = s.sem("ms_ready")
        pow_ready = s.sem("pow_ready")
        normed_ready = s.sem("normed_ready")
        scored = s.sem("scored")
        biased = s.sem("biased")
        exped = s.sem("exped")
        transposed = s.sem("transposed")
        copied = s.sem("copied")
        valued = s.sem("valued")
        o_taken = s.sem("o_taken")
        block = ctx.enter_context(s.programs())

        PROLOGUE = 10
        UNIT = 13

        def sections_before(b, t):
            return PROLOGUE if isinstance(b, int) and b == 0 and t == 0 else UNIT * (NT * b + t) + PROLOGUE - 3

        def steps(b, t, first, last):
            n = sections_before(b, t)
            for kind, k in WINDOW_ORDER:
                if (kind in NEXT and last) or (kind in PAST and first):
                    continue
                yield kind, k, n
                if kind in NEXT or kind in PAST:
                    n = n + 1

        def units(engine, unit):
            for t in range(NT):
                unit(0, t, t == 0, False)
            with engine.Fori(1, B - 1) as b:
                for t in range(NT):
                    unit(b, t, False, False)
            for t in range(NT):
                unit(B - 1, t, False, t == NT - 1)

        def following(b, t):
            return (b, t + 1) if t < NT - 1 else (b + 1, 0)

        def preceding(b, t):
            return (b, t - 1) if t else (b - 1, NT - 1)

        def first_tile():
            n = 0
            for kind, k in WINDOW_ORDER:
                if kind in NEXT:
                    yield kind, k, n
                    n += 1

        def last_tile():
            n = sections_before(B - 1, NT - 1) + UNIT - PROLOGUE
            for kind, k in (("out_T", 0), ("out_T", 1), ("out", 0)):
                yield kind, k, n
                n += 1

        def uses(b, t):
            return 2 * b + t // 2 + 1

        @block.sync
        def _(sp):
            for tile, dram in ((ident, const["ident"]), (wT["q"], wqT_d), (wT["k"], wkT_d), (wT["v"], wvT_d), (woT, woT_d),
                               (gamma, gamma_d), (bias, bias_d)):
                sp.dma_start(tile[tuple(slice(None) for _ in tile.shape)], dram).then_inc(const_in, 16)

            def load_xT(b, t):
                sp.dma_start(xT[:, t % 2, :, :], xnT_d[ds(b, 1)].rearrange("a p k t -> p (a k) t")[:, :, t * P:(t + 1) * P]).then_inc(xT_in[t % 2], 16)

            def tokens(dram, b, t):
                return dram[ds(b, 1)].rearrange("a t c -> t (a c)")[t * P:(t + 1) * P, :]

            def store(b, t, done):
                hold(sp, emptied, done + 1, held)
                sp.dma_start(tokens(y_d, b, t), x[:, t % 2, :]).then_inc(y_out[t % 2], 16)

            def unit(b, t, first, last):
                static = isinstance(b, int)
                if not (static and b == B - 1 and t >= 2):
                    hold(sp, emptied, sections_before(b, t), held)
                    load_xT(b + (t + 2) // NT, (t + 2) % NT)
                if not (static and b == 0 and t < 2):
                    past = (b, t - 2) if t >= 2 else (b - 1, t + 2)
                    store(*past, sections_before(*following(*past)) + 2)
                    hold(sp, y_out[t % 2], 16 * (uses(b, t) - 1), held)
                sp.dma_start(x[:, t % 2, :], tokens(x_d, b, t)).then_inc(x_in[t % 2], 16)

            load_xT(0, 0)
            load_xT(0, 1)
            units(nc.sync, unit)
            store(B - 1, NT - 2, sections_before(B - 1, NT - 1) + 2)
            store(B - 1, NT - 1, sections_before(B - 1, NT - 1) + 5)
            for p in range(2):
                sp.wait_ge(y_out[p], 16 * (NT * B // 2))

        @block.tensor
        def _(pe):
            pe.sem_inc(transposed, 2)
            pe.sem_inc(valued, 2)
            pe.wait_ge(const_in, 16 * 7)

            def section(kind, k, n, b, t):
                w = NT * b + t
                if not (isinstance(n, int) and n == 0):
                    pe.wait_ge(emptied, n)
                if kind in ("q", "k", "v"):
                    if kind == "q" and k == 0:
                        pe.wait_ge(xT_in[t % 2], 16 * uses(b, t))
                    for c in range(KC):
                        last = nc.tensor.matmul(ps_w[:, :], xT[:, t % 2, c, :], wT[kind][:, c, k * HW:(k + 1) * HW],
                                                start=(c == 0), stop=(c == KC - 1))
                elif kind in ("q_T", "k_T"):
                    which = 0 if kind == "q_T" else 1
                    pe.wait_ge(normed_ready, 2 * w + which + 3)
                    for c in range(4):
                        last = nc.tensor.transpose(ps_w[:, c * P:(c + 1) * P], normed[:, which, (4 * k + c) * P:(4 * k + c + 1) * P], ident[:, :])
                elif kind == "out_T":
                    pe.wait_ge(o_taken, 2 * w + 3)
                    for c in range(4):
                        last = nc.tensor.transpose(ps_w[:, c * P:(c + 1) * P], o[:, t % 2, (4 * k + c) * P:(4 * k + c + 1) * P], ident[:, :])
                else:
                    for c in range(CH):
                        last = nc.tensor.matmul(ps_w[:, 0:C], oT[:, c, :], woT[:, c, :], start=(c == 0), stop=(c == CH - 1))
                last.then_inc(filled, 1)

            def unit(b, t, first, last):
                u = NT * b + t
                lo = 1 if t == 0 else 0
                pe.wait_ge(emptied, sections_before(b, t))
                for kind, k, n in steps(b, t, first, last):
                    if kind in NEXT:
                        section(kind, k, n, *following(b, t))
                    elif kind in PAST:
                        section(kind, k, n, *preceding(b, t))
                    elif kind == "scores":
                        pe.wait_ge(biased, 16 * u + 4 * k + 4)
                        for hh in range(4):
                            h = 4 * k + hh
                            r = slice(BD * (h % 2), BD * (h % 2) + BD)
                            mm = nc.tensor.matmul(ps_s[k % 2][hh % 2][:, hh // 2, lo * P:], qT[r, t % 2, h // 2, :],
                                                  kT[r, h // 2, (t - 1 + lo) * P:(t + 1) * P], start=True, stop=True)
                        mm.then_inc(scored, 1)
                    elif kind == "probs_T":
                        pe.wait_ge(exped, 16 * u + 2 * k + 6)
                        pe.wait_ge(copied, 8 * u + k + 1)
                        for r in range(2):
                            for c in range(lo, 2):
                                mm = nc.tensor.transpose(ps_p[k % 2][:, r, c, :], prob[:, 2 * (k % 2) + r, c * P:(c + 1) * P], ident[:, :])
                        mm.then_inc(transposed, 1)
                    else:
                        pe.wait_ge(copied, 8 * u + k + 3)
                        if k % 4 == 0:
                            pe.wait_ge(o_taken, 2 * u + k // 4 + 1)
                        for r in range(2):
                            h = 2 * k + r
                            for c in range(lo, 2):
                                mm = nc.tensor.matmul(ps_o[:, h % 8 * BD:(h % 8 + 1) * BD], probT[:, k % 2, r, c, :],
                                                      v[:, t - 1 + c, h * BD:(h + 1) * BD], start=(c == lo), stop=(c == 1))
                        mm.then_inc(valued, 1)

            for kind, k, n in first_tile():
                section(kind, k, n, 0, 0)
            units(nc.tensor, unit)
            for kind, k, n in last_tile():
                section(kind, k, n, B - 1, NT - 1)

        @block.scalar
        def _(act):
            act.sem_inc(exped, 4)

            def section(kind, k, n, b, t):
                if kind == "out":
                    return
                act.wait_ge(filled, n + 1)
                if kind in ("q", "k"):
                    which = 0 if kind == "q" else 1
                    nc.scalar.activation(square[:, :], ps_w[:, :], ACT.Square, accum_out=ss[:, which, k:k + 1]).then_inc(squared, 1)
                    return
                by_chunk = ps_w[:, :].rearrange("p (c t) -> p c t", t=P)
                if kind == "v":
                    copy = nc.scalar.copy(v[:, t, k * HW:(k + 1) * HW], ps_w[:, :])
                elif kind == "q_T":
                    copy = nc.scalar.copy(qT[:, t % 2, 4 * k:4 * k + 4, :], by_chunk)
                elif kind == "k_T":
                    copy = nc.scalar.copy(kT[:, 4 * k:4 * k + 4, t * P:(t + 1) * P], by_chunk)
                else:
                    copy = nc.scalar.copy(oT[:, 4 * k:4 * k + 4, :], by_chunk)
                copy.then_inc(emptied, 1)

            def unit(b, t, first, last):
                u = NT * b + t
                lo = 1 if t == 0 else 0
                for kind, k, n in steps(b, t, first, last):
                    if kind in NEXT:
                        section(kind, k, n, *following(b, t))
                    elif kind in PAST:
                        section(kind, k, n, *preceding(b, t))
                    elif kind == "scores":
                        for hh in range(4):
                            h = 4 * k + hh
                            act.wait_ge(biased, 16 * u + h + 9)
                            if h % 2 == 0:
                                act.wait_ge(transposed, 8 * u + h // 2 + 1)
                            nc.scalar.activation(prob[:, hh, lo * P:], score[:, hh, lo * P:], ACT.Exp, bias=low[:, hh:hh + 1], scale=-1.0,
                                                 accum_out=rsum[:, t % 2, h:h + 1]).then_inc(exped, 1)

            for kind, k, n in first_tile():
                section(kind, k, n, 0, 0)
            units(nc.scalar, unit)
            for kind, k, n in last_tile():
                section(kind, k, n, B - 1, NT - 1)

        @block.gpsimd
        def _(pool):
            nc.gpsimd.memset(minus_half[:, :], -0.5).then_inc(half_set, 1)
            pool.sem_inc(normed_ready, 2)
            pool.wait_ge(half_set, 1)
            with nc.gpsimd.Fori(0, NT * B) as w:
                pool.wait_ge(ms_ready, w + 1)
                nc.gpsimd.tensor_tensor(rrms[:, :], ms[:, :], minus_half[:, :], ALU.pow).then_inc(pow_ready, 1)
                hold(pool, pow_ready, w + 1, held)
                for i in range(2):
                    nc.gpsimd.tensor_scalar(normed[:, i, :], raw[:, i, :], rrms[:, i:i + 1], 1.0, ALU.mult, ALU.mult).then_inc(normed_ready, 1)

        @block.vector
        def _(dve):
            dve.sem_inc(biased, 8)
            dve.sem_inc(copied, 2)
            dve.sem_inc(o_taken, 1)
            dve.wait_ge(const_in, 16 * 7)

            def section(kind, k, n, b, t, ch):
                w = NT * b + t
                if kind in ("q", "k"):
                    which = 0 if kind == "q" else 1
                    dve.wait_ge(squared, 4 * w + 2 * which + k + 1)
                    if kind == "q" and k == 0:
                        dve.wait_ge(normed_ready, 2 * w + 2)
                    half = slice(k * HW, (k + 1) * HW)
                    nc.vector.tensor_tensor(raw[:, which, half], ps_w[:, :], gamma[:, which, half], ALU.mult).then_inc(emptied, 1)
                    if kind == "k" and k == 1:
                        ch.link(nc.vector.tensor_tensor(ms[:, :], ss[:, :, 0], ss[:, :, 1], ALU.add))
                        nc.vector.tensor_scalar(ms[:, :], ms[:, :], 1.0 / BC, RMS_EPS, ALU.mult, ALU.add).then_inc(ms_ready, 1)
                elif kind == "out":
                    dve.wait_ge(x_in[t % 2], 16 * uses(b, t))
                    dve.wait_ge(filled, n + 1)
                    nc.vector.tensor_tensor(x[:, t % 2, :], x[:, t % 2, :], ps_w[:, 0:C], ALU.add).then_inc(emptied, 1)

            def unit(b, t, first, last):
                u = NT * b + t
                lo = 1 if t == 0 else 0
                ch = Chain(dve, chain, 3 * u + 1)
                for kind, k, n in steps(b, t, first, last):
                    if kind in NEXT:
                        section(kind, k, n, *following(b, t), ch)
                    elif kind in PAST:
                        section(kind, k, n, *preceding(b, t), ch)
                    elif kind == "scores":
                        dve.wait_ge(scored, 4 * u + k + 1)
                        for hh in range(4):
                            h = 4 * k + hh
                            hold(dve, exped, 16 * u + h + 1, held)
                            nc.vector.tensor_tensor_reduce(out=score[:, hh, lo * P:], in0=ps_s[k % 2][hh % 2][:, hh // 2, lo * P:],
                                                           in1=bias[:, h, lo * P:], scale=-B_SCALE, scalar=3.0e38, op0=ALU.add, op1=ALU.min,
                                                           accum_out=low[:, hh:hh + 1]).then_inc(biased, 1)
                    elif kind == "probs_T":
                        dve.wait_ge(transposed, 8 * u + k + 3)
                        dve.wait_ge(valued, 8 * u + k + 1)
                        nc.vector.tensor_copy(probT[:, k % 2, :, lo:, :], ps_p[k % 2][:, :, lo:, :]).then_inc(copied, 1)
                    elif k % 4 == 3:
                        half = k // 4
                        dve.wait_ge(valued, 8 * u + k + 3)
                        hs = slice(8 * half, 8 * half + 8)
                        ch.link(nc.vector.reciprocal(rinv[:, t % 2, hs], rsum[:, t % 2, hs]))
                        nc.vector.tensor_tensor(o[:, t % 2, half * HW:(half + 1) * HW].rearrange("p (h d) -> p h d", d=BD),
                                                ps_o[:, :].rearrange("p (h d) -> p h d", d=BD),
                                                rinv[:, t % 2, hs].unsqueeze(2).to_broadcast([P, 8, BD]), ALU.mult).then_inc(o_taken, 1)

            ch = Chain(dve, chain)
            for kind, k, n in first_tile():
                section(kind, k, n, 0, 0, ch)
            units(nc.vector, unit)
            for kind, k, n in last_tile():
                section(kind, k, n, B - 1, NT - 1, ch)


RELATIVE_ORDER = [
    ("scores", 0), ("q", 0), ("k", 0), ("scores", 1), ("q_band", 0),
    ("probs_T", 0), ("k_band", 0), ("probs_T", 1), ("q_band", 1), ("values", 0),
    ("scores", 2), ("k_band", 1), ("probs_T", 2), ("values", 1), ("q_band", 2), ("probs_T", 3), ("values", 2), ("k_band", 2),
    ("scores", 3), ("probs_T", 4), ("values", 3), ("q_band", 3), ("probs_T", 5), ("values", 4), ("k_band", 3),
    ("scores", 4), ("probs_T", 6), ("values", 5), ("v", 0), ("probs_T", 7), ("values", 6),
    ("scores", 5), ("probs_T", 8), ("values", 7), ("bins_T", 0), ("probs_T", 9), ("values", 8), ("bins_T", 1),
    ("scores", 6), ("probs_T", 10), ("values", 9), ("bins", 0), ("probs_T", 11), ("values", 10),
    ("scores", 7), ("probs_T", 12), ("values", 11), ("probs_T", 13), ("values", 12),
    ("probs_T", 14), ("values", 13), ("probs_T", 15), ("values", 14), ("values", 15),
]
A_NEXT = ("q", "k", "v", "q_band", "k_band")
A_PAST = ("bins_T", "bins")


def relative_stage(nc, tag, const, xnT_d, wT_d, rows_d, table_d, base_d, bins_d, bins_base_d, vbase_d, scratch, o_d):
    Q, K = 0, 1
    W4 = HG * WIN
    with ExitStack() as ctx:
        s = Store(nc, ctx, tag)
        ident = s.sb("ident", [P, P])
        lower = s.sb("lower", [P, P])
        upper = s.sb("upper", [P, P])
        wT = s.sb("wT", [P, 2, NG, KC, P])
        wv = s.sb("wv", [P, KC, C])
        rows = s.sb("rows", [P, 2, NG, C])
        table = s.sb("table", [P, 2, NG, HG, XB + 1])
        base = s.sb("base", [P, 2, NG, HG, XB + 1])
        diff = s.sb("diff", [P, 2, NG, HG, XB + 1])
        bins_w = s.sb("bins_w", [P, NG, 2, 2 * AD])
        bins_b = s.sb("bins_b", [P, NG, 2, 2 * AD])
        vbase = s.sb("vbase", [P, 2, C])
        scale = s.sb("scale", [P, 3])
        shift = s.sb("shift", [P, 3])
        xT = s.sb("xT", [P, KC, T])
        qk = s.sb("qk", [P, 2, 3, T])
        v = s.sb("v", [P, 2, 2, NT, HG * AD])
        band = s.sb("band", [P, 2, NT, HG, WIN])
        edge = s.sb("edge", [P, 2, 2, NT, HG])
        win = s.sb("win", [P, 2, 2, NT, HG, WIN])
        tri = s.sb("tri", [P, 2, HG, P])
        low = s.sb("low", [P, 2, 2])
        prob = s.sb("prob", [P, 2, HG, 32 + T + 32])
        probT = s.sb("probT", [P, 2, T])
        rsum = s.sb("rsum", [P, 2, NT, HG])
        rinv = s.sb("rinv", [P, NT, HG])
        junk = s.sb("junk", [P, 2, P])
        below = s.sb("below", [P, 2, NT, HG])
        bins = s.sb("bins", [P, 2, NT, HG, XB])
        binsT = s.sb("binsT", [P, NT * 2, P])
        o_raw = s.sb("o_raw", [P, NT, HG, AD])
        o = s.sb("o", [P, 2, NT, HG, AD])
        ps_s = [s.ps(f"ps_s{q}", [P, 2, T]) for q in range(2)]
        ps_p = [s.ps(f"ps_p{q}", [P, T]) for q in range(2)]
        ps_o = s.ps("ps_o", [P, NT, HG, AD])
        ps_w = s.ps("ps_w", [P, T])
        const_in = s.sem("const_in")
        chain = s.sem("chain")
        pool_chain = s.sem("pool_chain")
        held = s.sem("held")
        folded = s.sem("folded")
        set_up = s.sem("set_up")
        xT_in = s.sem("xT_in")
        filled = s.sem("filled")
        emptied = s.sem("emptied")
        band_out = [[s.sem(f"band_out{d}{t}") for t in range(NT)] for d in range(2)]
        win_in = [[s.sem(f"win_in{d}{t}") for t in range(NT)] for d in range(2)]
        win_ready = s.sem("win_ready")
        scored = s.sem("scored")
        maxed = s.sem("maxed")
        exped = s.sem("exped")
        transposed = s.sem("transposed")
        copied = [s.sem(f"copied{q}") for q in range(2)]
        valued = s.sem("valued")
        summed = s.sem("summed")
        prob_out = [s.sem(f"prob_out{q}") for q in range(2)]
        bins_in = [s.sem(f"bins_in{q}") for q in range(2)]
        bins_ready = s.sem("bins_ready")
        o_taken = s.sem("o_taken")
        o_ready = s.sem("o_ready")
        o_out = [s.sem(f"o_out{q}") for q in range(2)]
        loads = ((ident, const["ident"]), (lower, const["lower"]), (upper, const["upper"]), (wT, wT_d[0]), (wv, wT_d[1]), (rows, rows_d),
                 (table, table_d), (base, base_d), (bins_w, bins_d), (bins_b, bins_base_d), (vbase, vbase_d),
                 (scale, const["row_scale"]), (shift, const["row_shift"]))
        block = ctx.enter_context(s.programs())

        PROLOGUE = 11
        UNIT = PROLOGUE + 3

        def sections_before(b, g):
            return PROLOGUE if isinstance(b, int) and b == 0 and g == 0 else UNIT * (NG * b + g) + PROLOGUE - 3

        def steps(b, g, first, last):
            n = sections_before(b, g)
            for kind, k in RELATIVE_ORDER:
                if (kind in A_NEXT and last) or (kind in A_PAST and first):
                    continue
                yield kind, k, n
                if kind in A_NEXT or kind in A_PAST:
                    n = n + 1

        def units(engine, unit):
            for g in range(NG):
                unit(0, g, g == 0, False)
            with engine.Fori(1, B - 1) as b:
                for g in range(NG):
                    unit(b, g, False, False)
            for g in range(NG):
                unit(B - 1, g, False, g == NG - 1)

        def following(b, g):
            return (b, g + 1) if g < NG - 1 else (b + 1, 0)

        def preceding(b, g):
            return (b, g - 1) if g else (b - 1, NG - 1)

        def first_unit():
            n = 0
            for kind, k in RELATIVE_ORDER:
                if kind in A_NEXT:
                    yield kind, k, n
                    n += 1

        def last_unit():
            n = sections_before(B - 1, NG - 1) + UNIT - PROLOGUE
            for kind, k in RELATIVE_ORDER:
                if kind in A_PAST:
                    yield kind, k, n
                    n += 1

        def section_number(b, g, kind, k):
            place = [x for x in RELATIVE_ORDER if x[0] in A_NEXT].index((kind, k))
            return place if isinstance(b, int) and b == 0 and g == 0 else sections_before(*preceding(b, g)) + place

        def uses(b, g):
            return 2 * b + g // 2 + 1

        def window_columns(t):
            return max(0, t * P - 32), min(T, t * P + P + 32), 32 if t == 0 else 0

        @block.sync
        def _(sp):
            for tile, dram in loads:
                sp.dma_start(tile[tuple(slice(None) for _ in tile.shape)], dram).then_inc(const_in, 16)

            def next_unit(b, g):
                u = NG * b + g
                if g == 0:
                    if not (isinstance(b, int) and b == 0):
                        hold(sp, emptied, section_number(*preceding(b, g), "v", 0) + 1, held)
                    sp.dma_start(xT[:, :, :], by_channel(xnT_d, b)).then_inc(xT_in, 16)
                for step in range(NT + 1):
                    for d in range(2):
                        if step < NT:
                            hold(sp, emptied, section_number(b, g, ("q_band", "k_band")[d], step) + 1, held)
                            sp.dma_start(scratch["band"][d, g % 2, step], band[:, d, step, :, :].rearrange("p h x -> p (h x)")).then_inc(band_out[d][step], 16)
                        if step:
                            t = step - 1
                            hold(sp, band_out[d][t], 16 * u + 16, held)
                            rows_at = scratch["band"][d, g % 2, t]
                            skewed = bass.AP(rows_at.tensor, rows_at.offset, [[W4 - 1, P], [1, W4]])
                            sp.dma_start(win[:, g % 2, d, t, :, :].rearrange("p h x -> p (h x)"), skewed).then_inc(win_in[d][t], 16)

            def store(b, g):
                hold(sp, o_ready, NG * b + g + 1, held)
                out = o_d[ds(b, 1)].rearrange("a (t p) c -> p (a t) c", p=P)[:, :, g * HG * AD:(g + 1) * HG * AD]
                sp.dma_start(out, o[:, g % 2, :, :, :].rearrange("p t h d -> p t (h d)")).then_inc(o_out[g % 2], 16)

            def unit(b, g, first, last):
                if not last:
                    next_unit(*following(b, g))
                if not first:
                    store(*preceding(b, g))

            next_unit(0, 0)
            units(nc.sync, unit)
            store(B - 1, NG - 1)
            for q in range(2):
                sp.wait_ge(o_out[q], 16 * NG * B // 2)

        @block.tensor
        def _(pe):
            pe.sem_inc(transposed, 8)
            pe.sem_inc(valued, 2)
            pe.wait_ge(const_in, 16 * len(loads))
            for d in range(2):
                for end in range(2):
                    x = ((1, BUCKETS), (BUCKETS, 1))[d][end]
                    for g in range(NG):
                        for c in range(KC):
                            at = (((d * 2 + end) * NG + g) * KC + c) * HG
                            last = nc.tensor.matmul(ps_w[:, at:at + HG], rows[:, d, g, c * P:(c + 1) * P], table[:, d, g, :, x], start=True, stop=True)
            last.then_inc(folded, 1)
            pe.wait_ge(set_up, 1)

            def section(kind, k, n, b, g):
                if not (isinstance(n, int) and n == 0):
                    pe.wait_ge(emptied, n)
                if kind in ("q", "k"):
                    if kind == "q" and g == 0:
                        pe.wait_ge(xT_in, 16 * b + 16)
                    for c in range(KC):
                        last = nc.tensor.matmul(ps_w[:, :], wT[:, 0 if kind == "q" else 1, g, c, :], xT[:, c, :], start=(c == 0), stop=(c == KC - 1))
                elif kind == "v":
                    for t in range(NT):
                        for c in range(KC):
                            last = nc.tensor.matmul(ps_w[:, t * HG * AD:(t + 1) * HG * AD], xT[:, c, t * P:(t + 1) * P],
                                                    wv[:, c, g * HG * AD:(g + 1) * HG * AD], start=(c == 0), stop=(c == KC - 1))
                elif kind in ("q_band", "k_band"):
                    d = 0 if kind == "q_band" else 1
                    last = nc.tensor.matmul(ps_w[:, 0:HG * (XB + 1)], qk[:, g % 2, d, k * P:(k + 1) * P],
                                            diff[:, d, g, :, :].rearrange("p h x -> p (h x)"), start=True, stop=True)
                elif kind == "bins_T":
                    if k == 0:
                        pe.wait_ge(bins_ready, NG * b + g + 1)
                    for m in range(4):
                        t, r = 2 * k + m // 2, m % 2
                        last = nc.tensor.transpose(ps_w[:, m * P:(m + 1) * P], bins[:, g % 2, t, 2 * r:2 * r + 2, :].rearrange("p h x -> p (h x)"), ident[:, :])
                else:
                    for t in range(NT):
                        for r in range(2):
                            at = (t * 2 + r) * 2 * AD
                            last = nc.tensor.matmul(ps_w[:, at:at + 2 * AD], binsT[:, 2 * t + r, :], bins_w[:, g, r, :], start=True, stop=True)
                last.then_inc(filled, 1)

            def unit(b, g, first, last):
                u = NG * b + g
                p = g % 2
                pe.wait_ge(emptied, sections_before(b, g))
                for kind, k, n in steps(b, g, first, last):
                    if kind in A_NEXT:
                        section(kind, k, n, *following(b, g))
                    elif kind in A_PAST:
                        section(kind, k, n, *preceding(b, g))
                    elif kind == "scores":
                        t = k // 2
                        pe.wait_ge(win_ready, 8 * u + 2 * min(t + 1, NT - 1) + 2)
                        pe.wait_ge(exped, 16 * u + 2 * k + 2)
                        heads = [2 * (k % 2), 2 * (k % 2) + 1]
                        for h in heads:
                            r = slice(32 * h, 32 * h + 32)
                            bank = ps_s[k % 2][:, h % 2, :]
                            if t:
                                nc.tensor.matmul(bank[:, 0:t * P], qk[r, p, 0, t * P:(t + 1) * P], qk[r, p, 1, 0:t * P], start=True, stop=False)
                            nc.tensor.matmul(bank[:, t * P:], qk[r, p, 0, t * P:(t + 1) * P], qk[r, p, 2, t * P:], start=(t == 0), stop=False)
                        for h in heads:
                            bank = ps_s[k % 2][:, h % 2, :]
                            if t:
                                nc.tensor.matmul(bank[0:32, t * P - 32:t * P], win[96:P, p, K, t - 1, h, 160:192], ident[96:P, 96:P], start=False, stop=False)
                            if t < NT - 1:
                                nc.tensor.matmul(bank[96:P, (t + 1) * P:(t + 1) * P + 32], win[0:32, p, K, t + 1, h, 0:32], ident[0:32, 0:32], start=False, stop=False)
                            mm = nc.tensor.matmul(bank[:, t * P:(t + 1) * P], win[:, p, K, t, h, 32:160], ident[:, :], start=False, stop=True)
                        mm.then_inc(scored, 1)
                    elif kind == "probs_T":
                        t, h = k // HG, k % HG
                        pe.wait_ge(exped, 16 * u + k + 5)
                        pe.wait_ge(copied[k % 2], 8 * u + k // 2 + 1)
                        for c in range(NT):
                            mm = nc.tensor.transpose(ps_p[k % 2][:, c * P:(c + 1) * P], prob[:, t % 2, h, 32 + c * P:32 + (c + 1) * P], ident[:, :])
                        mm.then_inc(transposed, 1)
                    else:
                        t, h = k // HG, k % HG
                        pe.wait_ge(copied[k % 2], 8 * u + k // 2 + 2)
                        if k == 0:
                            pe.wait_ge(o_taken, u + 1)
                        for c in range(NT):
                            mm = nc.tensor.matmul(ps_o[:, t, h, :], probT[:, k % 2, c * P:(c + 1) * P], v[:, p, 0 if c < t else 1, c, h * AD:(h + 1) * AD],
                                                  start=(c == 0), stop=(c == NT - 1))
                        mm.then_inc(valued, 1)

            for kind, k, n in first_unit():
                section(kind, k, n, 0, 0)
            units(nc.tensor, unit)
            for kind, k, n in last_unit():
                section(kind, k, n, B - 1, NG - 1)

        @block.scalar
        def _(act):
            act.sem_inc(exped, 4)
            act.sem_inc(copied[1], 1)
            act.wait_ge(const_in, 16 * len(loads))

            def section(kind, k, n, b, g):
                p = g % 2
                if kind in ("v", "bins"):
                    return
                act.wait_ge(filled, n + 1)
                if kind in ("q", "k"):
                    which = (0,) if kind == "q" else (1, 2)
                    for i in which:
                        last = nc.scalar.activation(qk[:, p, i, :], ps_w[:, :], ACT.Identity, bias=shift[:, i:i + 1], scale=scale[:, i:i + 1])
                elif kind in ("q_band", "k_band"):
                    d = 0 if kind == "q_band" else 1
                    if not (isinstance(b, int) and b == 0 and g == 0):
                        act.wait_ge(band_out[d][k], 16 * (NG * b + g))
                    got = ps_w[:, 0:HG * (XB + 1)].rearrange("p (h x) -> p h x", h=HG)
                    nc.scalar.copy(band[:, d, k, :, 0:XB], got[:, :, 0:XB])
                    last = nc.scalar.copy(edge[:, p, d, k, :].unsqueeze(2), got[:, :, XB:])
                else:
                    last = nc.scalar.copy(binsT[:, 4 * k:4 * k + 4, :].rearrange("p m i -> p (m i)"), ps_w[:, :])
                last.then_inc(emptied, 1)

            def bins_home(b, g, t):
                act.wait_ge(prob_out[t % 2], 16 * (2 * (NG * b + g) + t // 2 + 1))
                src = scratch["prob"][t % 2]
                skewed = bass.AP(src.tensor, src.offset, [[W4 + 1, P], [WIN, HG], [1, XB]])
                act.dma_start(bins[:, g % 2, t, :, :], skewed).then_inc(bins_in[t % 2], 16)

            def unit(b, g, first, last):
                u = NG * b + g
                p = g % 2
                for kind, k, n in steps(b, g, first, last):
                    if kind in A_NEXT:
                        section(kind, k, n, *following(b, g))
                    elif kind in A_PAST:
                        section(kind, k, n, *preceding(b, g))
                    elif kind == "scores":
                        t = k // 2
                        act.wait_ge(maxed, 8 * u + k + 1)
                        if k % 2 == 0:
                            act.wait_ge(transposed, 16 * u + 4 * t + 4)
                            act.wait_ge(summed, 16 * u + 4 * t + 4)
                            if not (first and t < 2):
                                act.wait_ge(prob_out[t % 2], 16 * (2 * u + t // 2))
                        for r in range(2):
                            h = 2 * (k % 2) + r
                            nc.scalar.activation(prob[:, t % 2, h, 32:32 + T], ps_s[k % 2][:, r, :], ACT.Exp, bias=low[:, k % 2, r:r + 1],
                                                 accum_out=rsum[:, p, t, h:h + 1]).then_inc(exped, 1)
                        if k % 2:
                            act.wait_ge(exped, 16 * u + 4 * t + 8)
                            if not (first and t < 2):
                                act.wait_ge(bins_in[t % 2], 16 * (2 * u + t // 2))
                            act.dma_start(scratch["prob"][t % 2].rearrange("p (h x) -> p h x", h=HG),
                                          prob[:, t % 2, :, t * P:t * P + WIN]).then_inc(prob_out[t % 2], 16)
                            if t:
                                bins_home(b, g, t - 1)
                            elif not first:
                                bins_home(*preceding(b, g), NT - 1)
                    elif kind == "probs_T" and k % 2:
                        act.wait_ge(transposed, 16 * u + k + 9)
                        act.wait_ge(valued, 16 * u + k + 1)
                        nc.scalar.copy(probT[:, 1, :], ps_p[1][:, :]).then_inc(copied[1], 1)

            act.wait_ge(set_up, 1)
            for kind, k, n in first_unit():
                section(kind, k, n, 0, 0)
            units(nc.scalar, unit)
            bins_home(B - 1, NG - 1, NT - 1)
            for kind, k, n in last_unit():
                section(kind, k, n, B - 1, NG - 1)

        @block.gpsimd
        def _(pool):
            def next_unit(b, g):
                u = NG * b + g
                ch = Chain(pool, pool_chain, 8 * u)
                for t in range(NT):
                    if not (isinstance(u, int) and u + t == 0):
                        pool.wait_ge(win_ready, 8 * u + 2 * t)
                    pool.wait_ge(emptied, section_number(b, g, "k_band", t) + 1)
                    for d in range(2):
                        ch.mark(nc.gpsimd.tensor_tensor(tri[:, d, :, :], (lower, upper)[d][:, :].unsqueeze(1).to_broadcast([P, HG, P]),
                                                        edge[:, g % 2, d, t, :].unsqueeze(2).to_broadcast([P, HG, P]), ALU.mult))
                    ch.settle()
                    for d in range(2):
                        pool.wait_ge(win_in[d][t], 16 * u + 16)
                        square = win[:, g % 2, d, t, :, 32:160]
                        nc.gpsimd.tensor_tensor(square, square, tri[:, d, :, :], ALU.add).then_inc(win_ready, 1)

            def unit(b, g, first, last):
                if not last:
                    next_unit(*following(b, g))

            pool.wait_ge(const_in, 16 * len(loads))
            next_unit(0, 0)
            units(nc.gpsimd, unit)

        @block.vector
        def _(dve):
            SETUP = 3
            dve.sem_inc(copied[0], 1)
            dve.sem_inc(summed, 8)
            dve.sem_inc(o_taken, 1)
            ch = Chain(dve, chain)
            ch.mark(nc.vector.memset(band[:, :, :, :, XB:].rearrange("p d t h x -> p (d t h) x"), 0.0))
            nc.vector.memset(prob[:, :, :, 0:32].rearrange("p t h x -> p (t h) x"), 0.0)
            ch.mark(nc.vector.memset(prob[:, :, :, 32 + T:].rearrange("p t h x -> p (t h) x"), 0.0))
            dve.wait_ge(const_in, 16 * len(loads))
            flat = lambda x: x[:, :, :, :, :].rearrange("p d g h x -> p (d g h x)")
            ch.mark(nc.vector.tensor_tensor(flat(diff), flat(table), flat(base), ALU.subtract))
            ch.settle()
            nc.vector.tensor_scalar(diff[:, K, :, :, :], diff[:, K, :, :, :], A_SCALE, None, ALU.mult)
            nc.vector.tensor_tensor(bins_w[:, :, :, :], bins_w[:, :, :, :], bins_b[:, :, :, :], ALU.subtract)
            dve.wait_ge(folded, 1)
            for d in range(2):
                for end in range(2):
                    at = (d * 2 + end) * NG * KC * HG
                    last = nc.vector.tensor_copy(wT[:, d, :, :, :].rearrange("p g c (h r) -> p (g c) h r", r=32)[:, :, :, AD + 2 * d + end],
                                                 ps_w[:, at:at + NG * KC * HG].rearrange("p (m h) -> p m h", h=HG))
            last.then_inc(set_up, 1)

            def section(kind, k, n, b, g, ch):
                p = g % 2
                if kind == "v":
                    dve.wait_ge(filled, n + 1)
                    for i in range(2):
                        last = nc.vector.tensor_tensor(v[:, p, i, :, :], ps_w[:, 0:C].rearrange("p (t x) -> p t x", t=NT),
                                                       vbase[:, i, g * HG * AD:(g + 1) * HG * AD].unsqueeze(1).to_broadcast([P, NT, HG * AD]), ALU.add)
                    last.then_inc(emptied, 1)
                elif kind == "bins":
                    ch.link(nc.vector.reciprocal(rinv[:, :, :], rsum[:, p, :, :]))
                    dve.wait_ge(filled, n + 1)
                    dve.wait_ge(o_taken, NG * b + g + 2)
                    flat = lambda x: x.rearrange("p t h d -> p (t h d)")
                    ch.link(nc.vector.tensor_tensor(flat(o_raw[:, :, :, :]), flat(o_raw[:, :, :, :]), ps_w[:, 0:C], ALU.add))
                    dve.sem_inc(emptied, 1)
                    if not (isinstance(b, int) and b == 0 and g < 2):
                        dve.wait_ge(o_out[p], 16 * (uses(b, g) - 1))
                    nc.vector.tensor_tensor(o[:, p, :, :, :].rearrange("p t h d -> p (t h) d"), o_raw[:, :, :, :].rearrange("p t h d -> p (t h) d"),
                                            rinv[:, :, :].rearrange("p t h -> p (t h)").unsqueeze(2).to_broadcast([P, NT * HG, AD]), ALU.mult).then_inc(o_ready, 1)
                elif kind == "bins_T" and k == 0:
                    for t in range(NT - 2, NT):
                        dve.wait_ge(bins_in[t % 2], 16 * (2 * (NG * b + g) + 2))
                    dve.wait_ge(summed, 16 * (NG * b + g) + 24)
                    nc.vector.tensor_copy(bins[:, p, :, :, 0], below[:, p, :, :]).then_inc(bins_ready, 1)

            def unit(b, g, first, last):
                u = NG * b + g
                p = g % 2
                links = 10
                ch = Chain(dve, chain, SETUP if isinstance(b, int) and u == 0 else links * u + SETUP - 2)
                for kind, k, n in steps(b, g, first, last):
                    if kind in A_NEXT:
                        section(kind, k, n, *following(b, g), ch)
                    elif kind in A_PAST:
                        section(kind, k, n, *preceding(b, g), ch)
                    elif kind == "scores":
                        t = k // 2
                        c0, c1, x0 = window_columns(t)
                        h0 = 2 * (k % 2)
                        dve.wait_ge(win_ready, 8 * u + 2 * t + 1)
                        dve.wait_ge(scored, 8 * u + k + 1)
                        both = ps_s[k % 2]
                        ch.link(nc.vector.tensor_tensor(both[:, :, c0:c1], both[:, :, c0:c1], win[:, p, Q, t, h0:h0 + 2, x0:x0 + c1 - c0], ALU.add))
                        nc.vector.reduce_max(low[:, k % 2, :], both[:, :, :], AX.X, negate=True).then_inc(maxed, 1)
                    elif kind == "probs_T":
                        t, h = k // HG, k % HG
                        if k % 2 == 0:
                            dve.wait_ge(transposed, 16 * u + k + 9)
                            dve.wait_ge(valued, 16 * u + k + 1)
                            nc.vector.tensor_copy(probT[:, 0, :], ps_p[0][:, :]).then_inc(copied[0], 1)
                        dve.wait_ge(summed, 16 * u + k + 7)
                        hold(dve, exped, 16 * u + k + 5, held)
                        nc.vector.tensor_tensor_reduce(out=junk[:, k % 2, :], in0=prob[:, t % 2, h, 32 + t * P:32 + (t + 1) * P], in1=lower[:, :],
                                                       scale=1.0, scalar=0.0, op0=ALU.mult, op1=ALU.add, accum_out=below[:, p, t, h:h + 1]).then_inc(summed, 1)
                    elif kind == "values" and k == 15:
                        dve.wait_ge(valued, 16 * u + 18)
                        flat = lambda x: x[:, :, :, :].rearrange("p t h d -> p (t h d)")
                        nc.vector.tensor_copy(flat(o_raw), flat(ps_o)).then_inc(o_taken, 1)

            for kind, k, n in first_unit():
                section(kind, k, n, 0, 0, ch)
            units(nc.vector, unit)
            ch = Chain(dve, chain, 10 * NG * B + SETUP - 2)
            for kind, k, n in last_unit():
                section(kind, k, n, B - 1, NG - 1, ch)


def hybrid_block(nc, ins, out):
    def scratch(name, shape):
        return nc.dram_tensor(name, shape, F32, kind="Internal").ap()

    with ExitStack() as ctx:
        scores = ctx.enter_context(nc.sbuf_tensor("scores", [P, NT, B, E], F32))
        slot_token = ctx.enter_context(nc.sbuf_tensor("slot_token", [P, E, CT], I32))
        slot_weight = ctx.enter_context(nc.sbuf_tensor("slot_weight", [P, E, CT], F32))
        xnT = scratch("xnT", (B, P, KC, T))
        xn = scratch("xn", (B, T, C))
        x1 = scratch("x1", (B, T, C))
        x2 = scratch("x2", (B, T, C))
        x3 = scratch("x3", (B, T, C))
        heads = scratch("heads", (B, T, C))
        trips = {"band": scratch("band", (2, 2, NT, P, HG * WIN)), "prob": scratch("prob", (2, P, HG * WIN))}
        ident = ins["ident"]

        def mixture(tag, x, y):
            route_stage(nc, f"{tag}r", ins, scores, slot_token, slot_weight)
            shared_stage(nc, f"{tag}s", xnT, x, ins["SgT"], ins["SuT"], ins["SdT"], y)
            expert_stage(nc, f"{tag}e", ident, xn, slot_token, slot_weight, ins["WgT"], ins["WuT"], ins["WdT"], y)

        norm_stage(nc, "n0", ident, ins["x"], xnT)
        relative_stage(nc, "a", ins, xnT, (ins["a_wT"], ins["a_wv"]), ins["a_rows"], ins["a_table"], ins["a_base"],
                       ins["a_bins"], ins["a_bins_base"], ins["a_vbase"], trips, heads)
        norm_stage(nc, "n1", ident, ins["x"], xnT, attn=(heads, ins["a_projT"], ins["a_bias"]), x1_d=x1, xn_d=xn, gate=ins["gateT"], scores=scores)
        mixture("f", x1, x2)
        norm_stage(nc, "n2", ident, x2, xnT)
        window_stage(nc, "b", ins, x2, xnT, ins["b_wqT"], ins["b_wkT"], ins["b_wvT"], ins["b_woT"], ins["b_gamma"], ins["b_bias"], x3)
        norm_stage(nc, "n3", ident, x3, xnT, xn_d=xn, gate=ins["gateT"], scores=scores)
        mixture("g", x3, out)



def constants():
    p = np.arange(P)
    f = np.float32
    row_scale, row_shift = np.zeros((P, 3), f), np.zeros((P, 3), f)
    for h in range(HG):
        o = 32 * h
        row_scale[o:o + AD + 2, 0] = A_SCALE
        row_shift[o + AD + 2:o + AD + 4, 0] = 1
        row_scale[o:o + AD, 1:] = 1
        row_shift[o + AD, 1] = row_shift[o + AD + 1, 2] = 1
        row_scale[o + AD + 2, 1] = row_scale[o + AD + 3, 2] = A_SCALE
    m = np.arange(NT * B)
    slopes = np.array([2.0 ** (-8.0 / BH * (h + 1)) for h in range(BH)], f)
    dist = np.arange(2 * P)[None] - P - p[:, None]
    masked = (dist > 0) | (dist < -WINDOW)
    b_bias = np.where(masked[:, None], f(-1e9 / B_SCALE), slopes[None, :, None] * dist[:, None].astype(f) / f(B_SCALE))
    same = p[:, None] % E == p[None] % E
    return {
        "ident": np.eye(P, dtype=f),
        "lower": (p[None] < p[:, None]).astype(f),
        "upper": (p[None] > p[:, None]).astype(f),
        "row_scale": row_scale,
        "row_shift": row_shift,
        "same": same.astype(f),
        "before": (same & (p[:, None] // E < p[None] // E)).astype(f),
        "iota": np.tile(p.astype(f), (P, 1)),
        "token": ((m % B) * T + (m // B) * P + p[:, None]).astype(f),
        "b_bias": b_bias.astype(f),
    }


def by_chunk(w):
    return np.ascontiguousarray(w.T.reshape(w.shape[1] // P, P, w.shape[0]).transpose(1, 0, 2))


def relative_layout(w_qkv, q_table, k_table, v_table):
    wT = np.zeros((P, 2, NG, KC, P), w_qkv.dtype)
    rows = np.zeros((P, 2, NG, C), w_qkv.dtype)
    table = np.zeros((P, 2, NG, HG, XB + 1), k_table.dtype)
    base = np.zeros_like(table)
    bins = np.zeros((P, NG, 2, 2 * AD), v_table.dtype)
    bins_base = np.zeros_like(bins)
    last = BUCKETS - 1
    for d, tab in enumerate((k_table, q_table)):
        first_end, low_end, up_end = HALF + 1 + d, (0, last)[d], (last, 0)[d]
        for h in range(AH):
            g, r = h // HG, slice(32 * (h % HG), 32 * (h % HG) + AD)
            w = w_qkv[d * C + h * AD:d * C + (h + 1) * AD]
            rows[r, d, g] = w
            wT[:, d, g, :, r] = w.T.reshape(KC, P, AD).transpose(1, 0, 2)
            table[r, d, g, h % HG, 1:XB] = tab[h]
            base[r, d, g, h % HG, 1:first_end] = tab[h][:, 0:1]
            base[r, d, g, h % HG, first_end:XB] = tab[h][:, last:]
            table[r, d, g, h % HG, XB] = tab[h][:, low_end]
            base[r, d, g, h % HG, XB] = tab[h][:, up_end]
    for h in range(AH):
        g, r, x, c = h // HG, h % HG // 2, XB * (h % 2), slice(AD * (h % 2), AD * (h % 2) + AD)
        bins[x, g, r, c] = v_table[h, 0]
        bins[x + 1:x + XB, g, r, c] = v_table[h]
        bins_base[x + 1:x + 1 + HALF, g, r, c] = v_table[h, 0]
        bins_base[x + 1 + HALF:x + XB, g, r, c] = v_table[h, last]
        bins_base[x, g, r, c] = v_table[h, last]
    ends = np.stack([v_table[:, 0].reshape(C), v_table[:, last].reshape(C)])
    return {
        "a_wT": wT, "a_wv": by_chunk(w_qkv[2 * C:]), "a_rows": rows, "a_table": table, "a_base": base,
        "a_bins": bins, "a_bins_base": bins_base, "a_vbase": np.tile(ends, (P, 1, 1)),
    }


def kernel(L0_attn_a_x, L0_attn_a_w_qkv, L0_attn_a_w_proj, L0_attn_a_b_proj, L0_attn_a_rpe_q_table, L0_attn_a_rpe_k_table,
           L0_attn_a_rpe_v_table, L0_attn_b_wq, L0_attn_b_wk, L0_attn_b_wv, L0_attn_b_wo, L0_attn_b_q_gamma, L0_attn_b_k_gamma,
           L0_ffn_gate_w, L0_ffn_Wg, L0_ffn_Wu, L0_ffn_Wd, L0_ffn_Sg, L0_ffn_Su, L0_ffn_Sd):
    import concourse.bacc as bacc
    from concourse.bass_utils import run_bass_kernel_spmd

    a = np.asarray
    arrays = {
        "x": a(L0_attn_a_x),
        "a_projT": by_chunk(a(L0_attn_a_w_proj)),
        "a_bias": np.tile(a(L0_attn_a_b_proj), (P, 1)),
        "b_wqT": by_chunk(a(L0_attn_b_wq)),
        "b_wkT": by_chunk(a(L0_attn_b_wk)),
        "b_wvT": by_chunk(a(L0_attn_b_wv)),
        "b_woT": by_chunk(a(L0_attn_b_wo)),
        "b_gamma": np.tile(np.stack([a(L0_attn_b_q_gamma), a(L0_attn_b_k_gamma)]), (P, 1, 1)),
        "gateT": by_chunk(a(L0_ffn_gate_w)),
        "WgT": np.stack([by_chunk(w) for w in a(L0_ffn_Wg)]),
        "WuT": np.stack([by_chunk(w) for w in a(L0_ffn_Wu)]),
        "WdT": np.stack([by_chunk(w) for w in a(L0_ffn_Wd)]),
        "SgT": by_chunk(a(L0_ffn_Sg)),
        "SuT": by_chunk(a(L0_ffn_Su)),
        "SdT": by_chunk(a(L0_ffn_Sd)),
        **relative_layout(a(L0_attn_a_w_qkv), a(L0_attn_a_rpe_q_table), a(L0_attn_a_rpe_k_table), a(L0_attn_a_rpe_v_table)),
        **constants(),
    }
    nc = bacc.Bacc("TRN2", target_bir_lowering=False, num_devices=1)
    ins = {name: nc.dram_tensor(f"in_{name}", x.shape, mybir.dt.from_np(x.dtype), kind="ExternalInput").ap() for name, x in arrays.items()}
    out = nc.dram_tensor("out", (B, T, C), F32, kind="ExternalOutput").ap()
    hybrid_block(nc, ins, out)
    result = run_bass_kernel_spmd(nc, [{f"in_{name}": np.ascontiguousarray(x) for name, x in arrays.items()}], core_ids=[0])
    return result.results[0]["out"]
```

```python
from contextlib import ExitStack, contextmanager

import numpy as np

import concourse.bass as bass
from concourse import mybir

F32 = mybir.dt.float32
F32R = mybir.dt.float32r
I32 = mybir.dt.int32
ACT = mybir.ActivationFunctionType
ALU = mybir.AluOpType
AX = mybir.AxisListType
ds = bass.ds

P = 128
B, T, C = 8, 512, 256
NT = T // P
KC = C // P
LN_EPS = 1e-5

AH, AD = 16, 16
HG = 4
NG = AH // HG
BUCKETS = 63
HALF = BUCKETS // 2
XB = BUCKETS + 1
WIN = 192
A_SCALE = AD ** -0.5
A_ROWS = AD + 4
STACKED = ((0, 0, 1), (0, 1, 0))
HIGH_BITS = -(1 << 12)

BH, BD = 16, 64
BC = BH * BD
WINDOW = 128
RMS_EPS = 1e-6
B_SCALE = BD ** -0.5

E = 16
CAP = B * T * 2 // E
CT = CAP // P
I_E = 4 * C
I_S = 2 * C


class Chain:

    def __init__(self, engine, sem, start=0):
        self.engine, self.sem, self.start, self.n = engine, sem, start, 0

    def link(self, instruction):
        instruction.then_inc(self.sem, 1)
        self.n += 1
        self.engine.wait_ge(self.sem, self.start + self.n)

    def mark(self, instruction):
        instruction.then_inc(self.sem, 1)
        self.n += 1

    def settle(self):
        self.engine.wait_ge(self.sem, self.start + self.n)


def hold(engine, sem, value, held):
    engine.wait_ge(sem, value)
    engine.sem_inc(held, 1)


class Store:

    def __init__(self, nc, ctx, tag):
        self.nc, self.ctx, self.tag = nc, ctx, tag
        self.sems = []

    def sb(self, name, shape, dt=F32):
        return self.ctx.enter_context(self.nc.sbuf_tensor(f"{self.tag}_{name}", shape, dt))

    def ps(self, name, shape):
        return self.ctx.enter_context(self.nc.psum_tensor(f"{self.tag}_{name}", shape, F32))

    def sem(self, name):
        self.sems.append(self.ctx.enter_context(self.nc.semaphore(f"{self.tag}_{name}")))
        return self.sems[-1]

    @contextmanager
    def programs(self):
        with self.nc.Block() as block:
            yield block
        with self.nc.Block() as ending:
            @ending.gpsimd
            def _(pool):
                for sem in self.sems:
                    pool.sem_clear(sem)


def by_token(dram, n):
    return dram[ds(n, 1)].rearrange("a (t p) c -> p (a t) c", p=P)


def by_channel(dram, n):
    return dram[ds(n, 1)].rearrange("a p k t -> p (a k) t")


def norm_stage(nc, tag, ident_d, x_d, xnT_d, attn=None, x1_d=None, xn_d=None, gate=None, scores=None):
    with ExitStack() as ctx:
        s = Store(nc, ctx, tag)
        ident = s.sb("ident", [P, P])
        x = s.sb("x", [P, 2, NT, C])
        xn = s.sb("xn", [P, 2, NT, C])
        xnT = s.sb("xnT", [P, 2, KC, T])
        stats = s.sb("stats", [P, NT, 6])
        mv = s.sb("mv", [P, NT, 2])
        var = s.sb("var", [P, NT, 1])
        minus_half = s.sb("minus_half", [P, NT, 1])
        rstd = s.sb("rstd", [P, NT, 1])
        ps_xT = [s.ps(f"ps_xT{k}", [P, T]) for k in range(KC)]
        const_in = s.sem("const_in")
        x_in = [s.sem(f"x_in{p}") for p in range(2)]
        chain = s.sem("chain")
        held = s.sem("held")
        half_set = s.sem("half_set")
        mv_ready = s.sem("mv_ready")
        rstd_ready = s.sem("rstd_ready")
        xn_ready = s.sem("xn_ready")
        xT_ready = s.sem("xT_ready")
        xnT_ready = s.sem("xnT_ready")
        stored = [s.sem(f"stored{p}") for p in range(2)]
        n_const, n_store, n_load = 1, 1, 1
        if xn_d is not None:
            n_store += 1
        if attn:
            o_d, wT_d, bias_d = attn
            n_const += 2
            n_store += 1
            n_load += 1
            o = s.sb("o", [P, 2, NT, C])
            oT = s.sb("oT", [P, KC, T])
            wT = s.sb("wT", [P, KC, C])
            bias = s.sb("bias", [P, C])
            ps_oT = [s.ps(f"ps_oT{k}", [P, T]) for k in range(KC)]
            ps_y = [s.ps(f"ps_y{k}", [P, T]) for k in range(2)]
            oT_ready = s.sem("oT_ready")
            oT_copied = s.sem("oT_copied")
            y_ready = s.sem("y_ready")
        if gate is not None:
            n_const += 1
            gwT = s.sb("gwT", [P, KC, E])
            sm = s.sb("sm", [P, NT, E])
            mx = s.sb("mx", [P, NT, 1])
            total = s.sb("total", [P, NT, 1])
            ps_l = s.ps("ps_l", [P, NT, E])
            logits_ready = s.sem("logits_ready")
            shifted = s.sem("shifted")
            exped = s.sem("exped")
        block = ctx.enter_context(s.programs())

        @block.sync
        def _(sp):
            sp.dma_start(ident[:, :], ident_d).then_inc(const_in, 16)
            if attn:
                sp.dma_start(wT[:, :, :], wT_d).then_inc(const_in, 16)
                sp.dma_start(bias[:, :], bias_d).then_inc(const_in, 16)
            if gate is not None:
                sp.dma_start(gwT[:, :, :], gate).then_inc(const_in, 16)

            def load(n, p):
                sp.dma_start(x[:, p, :, :], by_token(x_d, n)).then_inc(x_in[p], 16)
                if attn:
                    sp.dma_start(o[:, p, :, :], by_token(o_d, n)).then_inc(x_in[p], 16)

            def store(i, p, more):
                n = 2 * i + p
                sp.wait_ge(xnT_ready, KC * n + 2 * KC)
                sp.dma_start(by_channel(xnT_d, n), xnT[:, p, :, :]).then_inc(stored[p], 16)
                if xn_d is not None:
                    sp.dma_start(by_token(xn_d, n), xn[:, p, :, :]).then_inc(stored[p], 16)
                if attn:
                    sp.dma_start(by_token(x1_d, n), x[:, p, :, :]).then_inc(stored[p], 16)
                if more:
                    sp.wait_ge(stored[p], 16 * n_store * i + 32 * n_store)
                    load(n + 2, p)

            for p in range(2):
                sp.sem_inc(stored[p], 16 * n_store)
            load(0, 0)
            load(1, 1)
            with nc.sync.Fori(0, B // 2 - 1) as i:
                store(i, 0, True)
                store(i, 1, True)
            for p in range(2):
                store(B // 2 - 1, p, False)
            for p in range(2):
                sp.wait_ge(stored[p], 16 * n_store * (B // 2 + 1))

        @block.tensor
        def _(pe):
            pe.wait_ge(const_in, 16 * n_const)
            with nc.tensor.Fori(0, B // 2) as i:
                for p in range(2):
                    n = 2 * i + p
                    if attn:
                        pe.wait_ge(x_in[p], 16 * n_load * i + 16 * n_load)
                        for k in range(KC):
                            for t in range(NT):
                                last = nc.tensor.transpose(ps_oT[k][:, t * P:(t + 1) * P],
                                                           o[:, p, t, k * P:(k + 1) * P], ident[:, :])
                            last.then_inc(oT_ready, 1)
                        pe.wait_ge(oT_copied, KC * n + KC)
                        for t in range(NT):
                            for k in range(KC):
                                last = nc.tensor.matmul(ps_y[t // 2][:, (t % 2) * C:(t % 2 + 1) * C],
                                                        oT[:, k, t * P:(t + 1) * P], wT[:, k, :],
                                                        start=(k == 0), stop=(k == KC - 1))
                            if t % 2:
                                last.then_inc(y_ready, 1)
                    pe.wait_ge(xn_ready, n + 1)
                    pe.wait_ge(xnT_ready, KC * n + KC)
                    for k in range(KC):
                        for t in range(NT):
                            last = nc.tensor.transpose(ps_xT[k][:, t * P:(t + 1) * P],
                                                       xn[:, p, t, k * P:(k + 1) * P], ident[:, :])
                        last.then_inc(xT_ready, 1)
                    if gate is not None:
                        pe.wait_ge(xnT_ready, KC * n + 2 * KC)
                        for t in range(NT):
                            for k in range(KC):
                                last = nc.tensor.matmul(ps_l[:, t, :], xnT[:, p, k, t * P:(t + 1) * P], gwT[:, k, :],
                                                        start=(k == 0), stop=(k == KC - 1))
                        last.then_inc(logits_ready, 1)

        @block.scalar
        def _(act):
            act.sem_inc(xnT_ready, KC)
            with nc.scalar.Fori(0, B // 2) as i:
                for p in range(2):
                    n = 2 * i + p
                    if attn:
                        for k in range(KC):
                            act.wait_ge(oT_ready, KC * n + k + 1)
                            nc.scalar.copy(oT[:, k, :], ps_oT[k][:, :]).then_inc(oT_copied, 1)
                    act.wait_ge(stored[p], 16 * n_store * i + 16 * n_store)
                    for k in range(KC):
                        act.wait_ge(xT_ready, KC * n + k + 1)
                        nc.scalar.copy(xnT[:, p, k, :], ps_xT[k][:, :]).then_inc(xnT_ready, 1)
                    if gate is not None:
                        act.wait_ge(shifted, n + 1)
                        nc.scalar.activation(sm[:, :, :], sm[:, :, :], ACT.Exp).then_inc(exped, 1)

        @block.gpsimd
        def _(pool):
            nc.gpsimd.memset(minus_half[:, :, :], -0.5).then_inc(half_set, 1)
            pool.wait_ge(half_set, 1)
            with nc.gpsimd.Fori(0, B) as n:
                pool.wait_ge(mv_ready, n + 1)
                nc.gpsimd.tensor_tensor(rstd[:, :, :], var[:, :, :], minus_half[:, :, :], ALU.pow).then_inc(rstd_ready, 1)

        @block.vector
        def _(dve):
            LINKS = 2 * NT + (1 if attn else 0) + (2 if attn else 0) + (3 if gate is not None else 0)
            if attn:
                dve.wait_ge(const_in, 16 * n_const)
            with nc.vector.Fori(0, B // 2) as i:
                for p in range(2):
                    n = 2 * i + p
                    ch = Chain(dve, chain, LINKS * n)
                    dve.wait_ge(x_in[p], 16 * n_load * i + 16 * n_load)
                    if attn:
                        ch.link(nc.vector.tensor_tensor(x[:, p, :, :], x[:, p, :, :],
                                                        bias[:, :].unsqueeze(1).to_broadcast([P, NT, C]), ALU.add))
                        for h in range(2):
                            dve.wait_ge(y_ready, 2 * n + h + 1)
                            xh = x[:, p, 2 * h:2 * h + 2, :]
                            ch.mark(nc.vector.tensor_tensor(xh, ps_y[h][:, :].rearrange("p (t c) -> p t c", c=C), xh, ALU.add))
                        ch.settle()
                    for t in range(NT):
                        ch.mark(nc.vector.bn_stats(stats[:, t, :], x[:, p, t, :]))
                    ch.settle()
                    dve.sem_inc(held, 1)
                    for t in range(NT):
                        ch.mark(nc.vector.bn_aggr(mv[:, t, :], stats[:, t, :]))
                    ch.settle()
                    nc.vector.tensor_scalar(var[:, :, :], mv[:, :, 1:2], LN_EPS, None, ALU.add).then_inc(mv_ready, 1)
                    dve.wait_ge(rstd_ready, n + 1)
                    dve.wait_ge(stored[p], 16 * n_store * i + 16 * n_store)
                    for t in range(NT):
                        last = nc.vector.tensor_scalar(xn[:, p, t, :], x[:, p, t, :], mv[:, t, 0:1], rstd[:, t, :],
                                                       ALU.subtract, ALU.mult)
                    last.then_inc(xn_ready, 1)
                    if gate is not None:
                        dve.wait_ge(logits_ready, n + 1)
                        ch.link(nc.vector.reduce_max(mx[:, :, :], ps_l[:, :, :], AX.X))
                        nc.vector.tensor_tensor(sm[:, :, :], ps_l[:, :, :], mx[:, :, :].to_broadcast([P, NT, E]),
                                                ALU.subtract).then_inc(shifted, 1)
                        dve.wait_ge(exped, n + 1)
                        ch.link(nc.vector.reduce_sum(total[:, :, :], sm[:, :, :], AX.X))
                        ch.link(nc.vector.reciprocal(total[:, :, :], total[:, :, :]))
                        nc.vector.tensor_tensor(scores[:, :, ds(n, 1), :].rearrange("p t a e -> p (t a) e"), sm[:, :, :],
                                                total[:, :, :].to_broadcast([P, NT, E]), ALU.mult)
                    assert ch.n == LINKS


def route_stage(nc, tag, const, scores, slot_token, slot_weight):
    FLOOR = 2.0 ** -126
    EXPONENT = [2.0 ** (2 ** k) for k in range(6, -1, -1)]
    MANTISSA = [2.0 ** -k for k in range(1, 24)]
    ROUNDS = 1 + len(EXPONENT) + len(MANTISSA)
    with ExitStack() as ctx:
        s = Store(nc, ctx, tag)
        ident = s.sb("ident", [P, P])
        same = s.sb("same", [P, P])
        before = s.sb("before", [P, P])
        iota = s.sb("iota", [P, P])
        token = s.sb("token", [P, NT * B])
        st = s.sb("st", [P, T])
        work = s.sb("work", [P, T])
        equal = s.sb("equal", [P, T])
        sel = s.sb("sel", [P, T])
        ones = s.sb("ones", [P, T])
        pos = s.sb("pos", [P, T])
        posi = s.sb("posi", [P, 2, T], I32)
        parts = s.sb("parts", [P, 2, T])
        partsT = s.sb("partsT", [P, 2, NT, P])
        thr = s.sb("thr", [P, 1])
        expo = s.sb("expo", [P, 1])
        cand = s.sb("cand", [P, 1])
        count = s.sb("count", [P, 1])
        got = s.sb("got", [P, 1])
        need = s.sb("need", [P, 1])
        offset = s.sb("offset", [P, 1])
        hit = s.sb("hit", [P, NT * P, CT])
        score_high = s.sb("score_high", [P, NT * P])
        score_rest = s.sb("score_rest", [P, NT * P])
        value = s.sb("value", [P, NT * P, 3, CT], F32R)
        onehot = s.sb("onehot", [P, 2, NT * B, P], F32R)
        found = s.sb("found", [P, E, 3, CT])
        ps_t = [s.ps(f"ps_t{k}", [P, T]) for k in range(2)]
        ps_c = s.ps("ps_c", [P, 1])
        ps_f = [s.ps(f"ps_f{k}", [P, 3 * CT]) for k in range(2)]
        const_in = s.sem("const_in")
        t_ready = s.sem("t_ready")
        chain = s.sem("chain")
        counted = s.sem("counted")
        summed = s.sem("summed")
        parts_ready = s.sem("parts_ready")
        parts_T = s.sem("parts_T")
        hot_ready = s.sem("hot_ready")
        found_ready = s.sem("found_ready")
        taken = s.sem("taken")
        block = ctx.enter_context(s.programs())

        @block.sync
        def _(sp):
            for tile, dram in ((ident, "ident"), (same, "same"), (before, "before"), (iota, "iota"), (token, "token")):
                sp.dma_start(tile[:, :], const[dram]).then_inc(const_in, 16)

        @block.tensor
        def _(pe):
            pe.wait_ge(const_in, 16 * 5)
            for t in range(NT):
                last = nc.tensor.transpose(ps_t[0][:, t * P:(t + 1) * P], scores[:, t, :, :].rearrange("p b e -> p (b e)"), ident[:, :])
            last.then_inc(t_ready, 1)
            for r in range(ROUNDS + 3):
                pe.wait_ge(counted, r + 1)
                table = same if r <= ROUNDS else before
                nc.tensor.matmul(ps_c[:, :], table[:, :], count[:, :], start=True, stop=True).then_inc(summed, 1)
            pe.wait_ge(parts_ready, 1)
            for k in range(2):
                for t in range(NT):
                    last = nc.tensor.transpose(ps_t[k][:, t * P:(t + 1) * P], parts[:, k, t * P:(t + 1) * P], ident[:, :])
            last.then_inc(parts_T, 1)
            with nc.tensor.Fori(0, E // 2) as i:
                for q in range(2):
                    e = 2 * i + q
                    pe.wait_ge(hot_ready, e + 1)
                    pe.wait_ge(taken, e + 1)
                    for m in range(NT * B):
                        last = nc.tensor.matmul(ps_f[q][:, :], onehot[:, q, m, :],
                                                value[:, ds(m * E + e, 1), :, :].rearrange("p a v c -> p (a v c)"),
                                                start=(m == 0), stop=(m == NT * B - 1))
                    last.then_inc(found_ready, 1)

        @block.vector
        def _(dve):
            ch = Chain(dve, chain)
            rounds = [0]

            def total(count_of, op, scalar):
                nc.vector.tensor_scalar(work[:, :], count_of, scalar, None, op, op1=ALU.add, accum_out=count[:, :]).then_inc(counted, 1)
                rounds[0] += 1
                dve.wait_ge(summed, rounds[0])

            dve.sem_inc(taken, 2)
            nc.vector.memset(ones[:, :], 1.0)
            ch.mark(nc.vector.memset(cand[:, :], FLOOR))
            dve.wait_ge(const_in, 16 * 5)
            dve.wait_ge(t_ready, 1)
            ch.mark(nc.vector.tensor_copy(st[:, :], ps_t[0][:, :]))
            ch.settle()
            total(st[:, :], ALU.is_ge, cand[:, :])
            ch.link(nc.vector.tensor_scalar(thr[:, :], ps_c[:, :], CAP - 0.5, cand[:, :], ALU.is_ge, ALU.mult))

            def keep():
                ch.link(nc.vector.tensor_scalar(got[:, :], ps_c[:, :], CAP - 0.5, cand[:, :], ALU.is_ge, ALU.mult))
                ch.link(nc.vector.tensor_tensor(thr[:, :], thr[:, :], got[:, :], ALU.max))

            for f in EXPONENT:
                ch.link(nc.vector.tensor_scalar(cand[:, :], thr[:, :], f, None, ALU.mult))
                total(st[:, :], ALU.is_ge, cand[:, :])
                keep()
            ch.link(nc.vector.tensor_copy(expo[:, :], thr[:, :]))
            for f in MANTISSA:
                ch.link(nc.vector.scalar_tensor_tensor(cand[:, :], expo[:, :], f, thr[:, :], ALU.mult, ALU.add))
                total(st[:, :], ALU.is_ge, cand[:, :])
                keep()
            total(st[:, :], ALU.is_gt, thr[:, :])
            ch.link(nc.vector.tensor_scalar(need[:, :], ps_c[:, :], -1.0, float(CAP), ALU.mult, ALU.add))
            total(st[:, :], ALU.is_equal, thr[:, :])
            ch.link(nc.vector.tensor_copy(offset[:, :], ps_c[:, :]))
            ch.link(nc.vector.tensor_scalar(equal[:, :], st[:, :], thr[:, :], None, ALU.is_equal))
            ch.link(nc.vector.tensor_tensor_scan(pos[:, :], ones[:, :], equal[:, :], offset[:, :], ALU.mult, ALU.add))
            ch.link(nc.vector.scalar_tensor_tensor(equal[:, :], pos[:, :], need[:, :], equal[:, :], ALU.is_le, ALU.mult))
            ch.link(nc.vector.scalar_tensor_tensor(sel[:, :], st[:, :], thr[:, :], equal[:, :], ALU.is_gt, ALU.add))
            total(sel[:, :], ALU.mult, 1.0)
            ch.link(nc.vector.tensor_copy(offset[:, :], ps_c[:, :]))
            ch.link(nc.vector.tensor_tensor_scan(pos[:, :], ones[:, :], sel[:, :], offset[:, :], ALU.mult, ALU.add))
            ch.link(nc.vector.tensor_tensor(pos[:, :], pos[:, :], sel[:, :], ALU.mult))
            ch.link(nc.vector.tensor_scalar(pos[:, :], pos[:, :], -1.0, None, ALU.add))
            ch.link(nc.vector.tensor_copy(posi[:, 0, :], pos[:, :]))
            ch.link(nc.vector.tensor_single_scalar(posi[:, 1, :], posi[:, 0, :], P - 1, ALU.bitwise_and))
            ch.link(nc.vector.tensor_single_scalar(posi[:, 0, :], posi[:, 0, :], 7, ALU.arith_shift_right))
            nc.vector.tensor_copy(parts[:, :, :], posi[:, :, :]).then_inc(parts_ready, 1)
            dve.wait_ge(parts_T, 1)
            for k in range(2):
                ch.mark(nc.vector.tensor_copy(partsT[:, k, :, :].rearrange("p t r -> p (t r)"), ps_t[k][:, :]))
            ch.settle()
            slot_tile = partsT[:, 0, :, :].rearrange("p t r -> p (t r)")
            ch.link(nc.vector.tensor_tensor(hit[:, :, :], slot_tile.unsqueeze(2).to_broadcast([P, NT * P, CT]),
                                            iota[:, 0:CT].unsqueeze(1).to_broadcast([P, NT * P, CT]), ALU.is_equal))
            sc = scores[:, :, :, :].rearrange("p t b e -> p (t b e)")
            ch.link(nc.vector.tensor_single_scalar(score_high[:, :].bitcast(I32), sc.bitcast(I32), HIGH_BITS, ALU.bitwise_and))
            ch.link(nc.vector.tensor_tensor(score_rest[:, :], sc, score_high[:, :], ALU.subtract))
            tok = token[:, :].unsqueeze(2).to_broadcast([P, NT * B, E]).unsqueeze(3).to_broadcast([P, NT * B, E, CT])
            ch.mark(nc.vector.tensor_tensor(value[:, :, 0, :].rearrange("p (m e) c -> p m e c", e=E), hit[:, :, :].rearrange("p (m e) c -> p m e c", e=E), tok, ALU.mult))
            for i, part in enumerate((score_high, score_rest)):
                ch.mark(nc.vector.tensor_tensor(value[:, :, 1 + i, :], hit[:, :, :], part[:, :].unsqueeze(2).to_broadcast([P, NT * P, CT]), ALU.mult))
            ch.settle()

            def one_hot(e, q):
                dve.wait_ge(taken, e + 1)
                low = partsT[:, 1, :, :].rearrange("p t (b e) -> p (t b) e", e=E)[:, :, ds(e, 1)]
                nc.vector.tensor_tensor(onehot[:, q, :, :], low.to_broadcast([P, NT * B, P]),
                                        iota[:, :].unsqueeze(1).to_broadcast([P, NT * B, P]), ALU.is_equal).then_inc(hot_ready, 1)

            def take(e, q):
                dve.wait_ge(found_ready, e + 1)
                nc.vector.tensor_copy(found[:, ds(e, 1), :, :].rearrange("p a v c -> p (a v c)"), ps_f[q][:, :]).then_inc(taken, 1)

            one_hot(0, 0)
            one_hot(1, 1)
            with nc.vector.Fori(0, E // 2 - 1) as i:
                for q in range(2):
                    take(2 * i + q, q)
                    one_hot(2 * i + q + 2, q)
            take(E - 2, 0)
            take(E - 1, 1)
            dve.wait_ge(taken, E + 2)
            nc.vector.tensor_copy(slot_token[:, :, :], found[:, :, 0, :])
            nc.vector.tensor_tensor(slot_weight[:, :, :], found[:, :, 1, :], found[:, :, 2, :], ALU.add)


def split_piece(nc, ch, masked, x, high, rest):
    ch.link(nc.vector.tensor_single_scalar(masked.bitcast(I32), x.bitcast(I32), HIGH_BITS, ALU.bitwise_and))
    ch.mark(nc.vector.tensor_copy(high, masked))
    ch.mark(nc.vector.tensor_tensor(rest, x, masked, ALU.subtract))
    ch.settle()


def hidden_pe(nc, pe, n, hidden, x, g, u, ps_g, ps_u, gu_ready, h_ready):
    for j in range(hidden):
        q = j % 2
        pe.wait_ge(h_ready, hidden * n + j + 1)
        for ps, w in ((ps_g[q], g), (ps_u[q], u)):
            terms = [(k, a, b) for k in range(KC) for a, b in ((1, 0), (0, 0), (0, 1))]
            for k, a, b in terms:
                last = nc.tensor.matmul(ps[:, :], w[a][:, k, j * P:(j + 1) * P], x[b][:, k, :],
                                        start=((k, a, b) == terms[0]), stop=((k, a, b) == terms[-1]))
        last.then_inc(gu_ready, 1)


def hidden_act(nc, act, n, hidden, ps_g, gelu, gu_ready, h_ready, gelu_ready):
    for j in range(hidden):
        act.wait_ge(gu_ready, hidden * n + j + 1)
        act.wait_ge(h_ready, hidden * n + j + 1)
        nc.scalar.activation(gelu[:, j % 2, :], ps_g[j % 2][:, :], ACT.Gelu).then_inc(gelu_ready, 1)


def hidden_dve(nc, dve, n, hidden, ps_u, gelu, hT, gelu_ready, h_ready, between=lambda j: None):
    for j in range(hidden):
        dve.wait_ge(gelu_ready, hidden * n + j + 1)
        nc.vector.tensor_tensor(hT[:, j, :], gelu[:, j % 2, :], ps_u[j % 2][:, :], ALU.mult).then_inc(h_ready, 1)
        between(j)


def down_pe(nc, pe, n, hidden, hT, dT, ps_d, h_ready, d_ready, d_taken):
    pe.wait_ge(h_ready, hidden * n + hidden + 2)
    for t in range(NT):
        pe.wait_ge(d_taken, NT * n + t + 1)
        for j in range(hidden):
            last = nc.tensor.matmul(ps_d[t % 2][:, :], hT[:, j, t * P:(t + 1) * P], dT[:, j, :], start=(j == 0), stop=(j == hidden - 1))
        last.then_inc(d_ready, 1)


def shared_stage(nc, tag, xnT_d, x_d, gT_d, uT_d, dT_d, y_d):
    HB = I_S // P
    with ExitStack() as ctx:
        s = Store(nc, ctx, tag)
        gT = s.sb("gT", [P, KC, I_S])
        uT = s.sb("uT", [P, KC, I_S])
        dT = s.sb("dT", [P, HB, C])
        masked = s.sb("masked", [P, T])
        g = [s.sb(f"g_{part}", [P, KC, I_S], F32R) for part in ("high", "rest")]
        u = [s.sb(f"u_{part}", [P, KC, I_S], F32R) for part in ("high", "rest")]
        xT = s.sb("xT", [P, 2, KC, T])
        xs = [s.sb(f"x_{part}", [P, 2, KC, T], F32R) for part in ("high", "rest")]
        x = s.sb("x", [P, 2, NT, C])
        gelu = s.sb("gelu", [P, 2, T])
        hT = s.sb("hT", [P, 2, HB, T])
        ps_g = [s.ps(f"ps_g{q}", [P, T]) for q in range(2)]
        ps_u = [s.ps(f"ps_u{q}", [P, T]) for q in range(2)]
        ps_d = [s.ps(f"ps_d{q}", [P, C]) for q in range(2)]
        w_in = s.sem("w_in")
        xT_in = [s.sem(f"xT_in{p}") for p in range(2)]
        x_in = [s.sem(f"x_in{p}") for p in range(2)]
        chain = s.sem("chain")
        held = s.sem("held")
        w_split = s.sem("w_split")
        x_split = s.sem("x_split")
        gu_ready = s.sem("gu_ready")
        gelu_ready = s.sem("gelu_ready")
        h_ready = s.sem("h_ready")
        d_ready = s.sem("d_ready")
        d_taken = s.sem("d_taken")
        y_out = [s.sem(f"y_out{p}") for p in range(2)]
        block = ctx.enter_context(s.programs())

        @block.sync
        def _(sp):
            def load(n, p):
                sp.dma_start(xT[:, p, :, :], by_channel(xnT_d, n)).then_inc(xT_in[p], 16)
                sp.dma_start(x[:, p, :, :], by_token(x_d, n)).then_inc(x_in[p], 16)

            sp.dma_start(gT[:, :, :], gT_d).then_inc(w_in, 16)
            sp.dma_start(uT[:, :, :], uT_d).then_inc(w_in, 16)
            load(0, 0)
            load(1, 1)
            sp.dma_start(dT[:, :, :], dT_d).then_inc(w_in, 16)

            def store(i, p, more):
                n = 2 * i + p
                sp.wait_ge(d_taken, NT * n + NT + 2)
                sp.dma_start(by_token(y_d, n), x[:, p, :, :]).then_inc(y_out[p], 16)
                if more:
                    sp.wait_ge(y_out[p], 16 * i + 16)
                    load(n + 2, p)

            with nc.sync.Fori(0, B // 2 - 1) as i:
                store(i, 0, True)
                store(i, 1, True)
            store(B // 2 - 1, 0, False)
            store(B // 2 - 1, 1, False)
            for p in range(2):
                sp.wait_ge(y_out[p], 16 * (B // 2))

        @block.tensor
        def _(pe):
            pe.wait_ge(w_in, 16 * 3)
            pe.wait_ge(w_split, 1)
            with nc.tensor.Fori(0, B // 2) as i:
                for p in range(2):
                    pe.wait_ge(x_split, 2 * i + p + 1)
                    hidden_pe(nc, pe, 2 * i + p, HB, [x_[:, p, :, :] for x_ in xs], g, u, ps_g, ps_u, gu_ready, h_ready)
                    down_pe(nc, pe, 2 * i + p, HB, hT[:, p, :, :], dT, ps_d, h_ready, d_ready, d_taken)

        @block.scalar
        def _(act):
            with nc.scalar.Fori(0, B) as n:
                hidden_act(nc, act, n, HB, ps_g, gelu, gu_ready, h_ready, gelu_ready)

        @block.vector
        def _(dve):
            dve.sem_inc(h_ready, 2)
            dve.sem_inc(d_taken, 2)
            LINKS = 3 * KC

            def split_x(ch, i, p):
                hold(dve, xT_in[p], 16 * i + 16, held)
                for k in range(KC):
                    split_piece(nc, ch, masked[:, :], xT[:, p, k, :], *[part[:, p, k, :] for part in xs])
                dve.sem_inc(x_split, 1)

            ch = Chain(dve, chain)
            dve.wait_ge(w_in, 16 * 3)
            for w, parts in ((gT, g), (uT, u)):
                for k in range(KC):
                    split_piece(nc, ch, masked[:, :], w[:, k, :], *[part[:, k, :] for part in parts])
            dve.sem_inc(w_split, 1)
            SETUP = ch.n
            split_x(ch, 0, 0)

            def step(i, p, more):
                n = 2 * i + p
                ch = Chain(dve, chain, LINKS * n + SETUP + LINKS)
                hidden_dve(nc, dve, n, HB, ps_u, gelu, hT[:, p, :, :], gelu_ready, h_ready)
                if more:
                    split_x(ch, i + p, 1 - p)
                dve.wait_ge(x_in[p], 16 * i + 16)
                for t in range(NT):
                    dve.wait_ge(d_ready, NT * n + t + 1)
                    nc.vector.tensor_tensor(x[:, p, t, :], x[:, p, t, :], ps_d[t % 2][:, :], ALU.add).then_inc(d_taken, 1)

            with nc.vector.Fori(0, B // 2 - 1) as i:
                step(i, 0, True)
                step(i, 1, True)
            step(B // 2 - 1, 0, True)
            step(B // 2 - 1, 1, False)


def expert_stage(nc, tag, ident_d, xn_d, slot_token, slot_weight, gT_d, uT_d, dT_d, y_d):
    HB = I_E // P
    DONE = 16 * CT
    rows_xn = xn_d.rearrange("b t c -> (b t) c")
    rows_y = y_d.rearrange("b t c -> (b t) c")
    with ExitStack() as ctx:
        s = Store(nc, ctx, tag)
        ident = s.sb("ident", [P, P])
        gT = s.sb("gT", [P, 2, KC, I_E])
        uT = s.sb("uT", [P, 2, KC, I_E])
        dT = s.sb("dT", [P, 2, HB, C])
        masked = s.sb("masked", [P, T])
        g = [s.sb(f"g_{part}", [P, 2, KC, I_E], F32R) for part in ("high", "rest")]
        u = [s.sb(f"u_{part}", [P, 2, KC, I_E], F32R) for part in ("high", "rest")]
        index = s.sb("index", [P, 2, CT], I32)
        xg = s.sb("xg", [P, 2, CT, C])
        xT = s.sb("xT", [P, 2, KC, T])
        xs = [s.sb(f"x_{part}", [P, 2, KC, T], F32R) for part in ("high", "rest")]
        gelu = s.sb("gelu", [P, 2, T])
        hT = s.sb("hT", [P, HB, T])
        eo = s.sb("eo", [P, 2, CT, C])
        ps_x = [s.ps(f"ps_x{k}", [P, T]) for k in range(KC)]
        ps_g = [s.ps(f"ps_g{q}", [P, T]) for q in range(2)]
        ps_u = [s.ps(f"ps_u{q}", [P, T]) for q in range(2)]
        ps_d = [s.ps(f"ps_d{q}", [P, C]) for q in range(2)]
        ident_in = s.sem("ident_in")
        up_in = [s.sem(f"up_in{q}") for q in range(2)]
        down_in = [s.sem(f"down_in{q}") for q in range(2)]
        held = s.sem("held")
        chain = s.sem("chain")
        w_split = s.sem("w_split")
        x_split = s.sem("x_split")
        index_ready = s.sem("index_ready")
        gathered = [s.sem(f"gathered{q}") for q in range(2)]
        x_T = s.sem("x_T")
        xT_ready = s.sem("xT_ready")
        gu_ready = s.sem("gu_ready")
        gelu_ready = s.sem("gelu_ready")
        h_ready = s.sem("h_ready")
        d_ready = s.sem("d_ready")
        d_taken = s.sem("d_taken")
        added = [s.sem(f"added{q}") for q in range(2)]
        block = ctx.enter_context(s.programs())

        @block.sync
        def _(sp):
            sp.dma_start(ident[:, :], ident_d).then_inc(ident_in, 16)

            def load_up(e, q):
                sp.dma_start(gT[:, q, :, :], gT_d[ds(e, 1)].rearrange("a p k i -> p (a k) i")).then_inc(up_in[q], 16)
                sp.dma_start(uT[:, q, :, :], uT_d[ds(e, 1)].rearrange("a p k i -> p (a k) i")).then_inc(up_in[q], 16)

            def load_down(e, q):
                sp.dma_start(dT[:, q, :, :], dT_d[ds(e, 1)].rearrange("a p k i -> p (a k) i")).then_inc(down_in[q], 16)

            def step(i, q, up=True):
                e = 2 * i + q
                if up:
                    sp.wait_ge(w_split, e + 2)
                    load_up(e + 3, 1 - q)
                sp.wait_ge(d_ready, CT * e + CT)
                load_down(e + 2, q)

            load_up(0, 0)
            load_up(1, 1)
            load_down(0, 0)
            load_down(1, 1)
            sp.wait_ge(w_split, 1)
            load_up(2, 0)
            with nc.sync.Fori(0, E // 2 - 2) as i:
                step(i, 0)
                step(i, 1)
            step(E // 2 - 2, 0)
            step(E // 2 - 2, 1, up=False)

        @block.gpsimd
        def _(pool):
            def gather(e, q):
                nc.gpsimd.tensor_copy(index[:, q, :], slot_token[:, ds(e, 1), :].rearrange("p a c -> p (a c)")).then_inc(index_ready, 1)
                hold(pool, index_ready, e + 1, held)
                for t in range(CT):
                    nc.gpsimd.indirect_dma_start(xg[:, q, t, :], None, rows_xn, bass.IndirectOffsetOnAxis(index[:, q, t:t + 1], 0),
                                                 bounds_check=B * T - 1).then_inc(gathered[q], 16)

            def step(i, q, more, first=False):
                e = 2 * i + q
                if not first or q:
                    hold(pool, added[1 - q], DONE * (i + q), held)
                if more:
                    hold(pool, x_T, KC * e + KC, held)
                    gather(e + 1, 1 - q)
                for t in range(CT):
                    hold(pool, d_taken, CT * e + t + 3, held)
                    nc.gpsimd.indirect_dma_start(rows_y, bass.IndirectOffsetOnAxis(index[:, q, t:t + 1], 0), eo[:, q, t, :], None,
                                                 bounds_check=B * T - 1, compute_op=ALU.add).then_inc(added[q], 16)

            gather(0, 0)
            step(0, 0, True, first=True)
            step(0, 1, True, first=True)
            with nc.gpsimd.Fori(1, E // 2 - 1) as i:
                step(i, 0, True)
                step(i, 1, True)
            step(E // 2 - 1, 0, True)
            step(E // 2 - 1, 1, False)
            for q in range(2):
                pool.wait_ge(added[q], DONE * (E // 2))

        @block.tensor
        def _(pe):
            def transpose_rows(i, q, e):
                pe.wait_ge(gathered[q], DONE * i + DONE)
                for k in range(KC):
                    for t in range(CT):
                        last = nc.tensor.transpose(ps_x[k][:, t * P:(t + 1) * P], xg[:, q, t, k * P:(k + 1) * P], ident[:, :])
                    last.then_inc(x_T, 1)

            def step(i, q, more):
                e = 2 * i + q
                pe.wait_ge(w_split, e + 1)
                pe.wait_ge(x_split, e + 1)
                hidden_pe(nc, pe, e, HB, *[[part[:, q, :, :] for part in parts] for parts in (xs, g, u)], ps_g, ps_u, gu_ready, h_ready)
                if more:
                    transpose_rows(i + q, 1 - q, e + 1)
                pe.wait_ge(down_in[q], 16 * i + 16)
                down_pe(nc, pe, e, HB, hT, dT[:, q, :, :], ps_d, h_ready, d_ready, d_taken)

            pe.sem_inc(x_T, KC)
            pe.wait_ge(ident_in, 16)
            transpose_rows(0, 0, 0)
            with nc.tensor.Fori(0, E // 2 - 1) as i:
                step(i, 0, True)
                step(i, 1, True)
            step(E // 2 - 1, 0, True)
            step(E // 2 - 1, 1, False)

        @block.scalar
        def _(act):
            def copy_rows(e, q):
                for k in range(KC):
                    act.wait_ge(x_T, KC * e + k + 1 + KC)
                    nc.scalar.copy(xT[:, q, k, :], ps_x[k][:, :]).then_inc(xT_ready, 1)

            def step(i, q, more):
                hidden_act(nc, act, 2 * i + q, HB, ps_g, gelu, gu_ready, h_ready, gelu_ready)
                if more:
                    copy_rows(2 * i + q + 1, 1 - q)

            copy_rows(0, 0)
            with nc.scalar.Fori(0, E // 2 - 1) as i:
                step(i, 0, True)
                step(i, 1, True)
            step(E // 2 - 1, 0, True)
            step(E // 2 - 1, 1, False)

        @block.vector
        def _(dve):
            dve.sem_inc(h_ready, 2)
            dve.sem_inc(d_taken, 2)

            PIECES = [(w, parts, k, slice(i, i + T)) for w, parts in ((gT, g), (uT, u)) for k in range(KC) for i in range(0, I_E, T)]
            LINKS = 3 * (len(PIECES) + KC)

            def split_w(ch, i, q, j):
                if j >= len(PIECES):
                    return
                if j == 0:
                    hold(dve, up_in[q], 32 * i + 32, held)
                w, parts, k, columns = PIECES[j]
                split_piece(nc, ch, masked[:, :], w[:, q, k, columns], *[part[:, q, k, columns] for part in parts])
                if j == len(PIECES) - 1:
                    dve.sem_inc(w_split, 1)

            def split_x(ch, e, q):
                hold(dve, xT_ready, KC * e + KC, held)
                for k in range(KC):
                    split_piece(nc, ch, masked[:, :], xT[:, q, k, :], *[part[:, q, k, :] for part in xs])
                dve.sem_inc(x_split, 1)

            def step(i, q, first=False, more=True):
                e = 2 * i + q
                ch = Chain(dve, chain, LINKS * e + LINKS)
                hidden_dve(nc, dve, e, HB, ps_u, gelu, hT, gelu_ready, h_ready, (lambda j: split_w(ch, i + q, 1 - q, j)) if more else (lambda j: None))
                if more:
                    split_x(ch, e + 1, 1 - q)
                if not first:
                    dve.wait_ge(added[q], DONE * i)
                for t in range(CT):
                    dve.wait_ge(d_ready, CT * e + t + 1)
                    nc.vector.tensor_tensor(eo[:, q, t, :], ps_d[t % 2][:, :],
                                            slot_weight[:, ds(e, 1), t:t + 1].rearrange("p a c -> p (a c)").to_broadcast([P, C]),
                                            ALU.mult).then_inc(d_taken, 1)

            ch = Chain(dve, chain)
            for j in range(len(PIECES)):
                split_w(ch, 0, 0, j)
            split_x(ch, 0, 0)
            step(0, 0, first=True)
            step(0, 1, first=True)
            with nc.vector.Fori(1, E // 2 - 1) as i:
                step(i, 0)
                step(i, 1)
            step(E // 2 - 1, 0)
            step(E // 2 - 1, 1, more=False)


def scores_later(order, last_before):
    scores = [x for x in order if x[0] == "scores"]
    places = scores[1:] + [last_before]
    out = []
    for x in order:
        if x in places:
            out.append(scores[places.index(x)])
        if x[0] != "scores":
            out.append(x)
    return out


WINDOW_ORDER = [
    ("scores", 0), ("out_T", 0), ("out_T", 1), ("scores", 1), ("out", 0),
    ("probs_T", 0), ("q", 0), ("probs_T", 1), ("values", 0), ("q", 1),
    ("scores", 2), ("probs_T", 2), ("values", 1), ("k", 0), ("probs_T", 3), ("values", 2), ("k", 1),
    ("scores", 3), ("probs_T", 4), ("values", 3), ("v", 0), ("probs_T", 5), ("values", 4), ("v", 1),
    ("q_T", 0), ("probs_T", 6), ("values", 5), ("q_T", 1), ("k_T", 0), ("probs_T", 7), ("values", 6), ("k_T", 1), ("values", 7),
]
WINDOW_SCALAR_ORDER = scores_later(WINDOW_ORDER, ("q_T", 0))
NEXT = ("q", "k", "v", "q_T", "k_T")
PAST = ("out_T", "out")


def window_stage(nc, tag, const, x_d, xnT_d, wqT_d, wkT_d, wvT_d, woT_d, gamma_d, bias_d, y_d):
    CH = BC // P
    HALVES = 2
    HW = BC // HALVES
    with ExitStack() as ctx:
        s = Store(nc, ctx, tag)
        ident = s.sb("ident", [P, P])
        wT = {"q": s.sb("wqT", [P, KC, BC]), "k": s.sb("wkT", [P, KC, BC]), "v": s.sb("wvT", [P, KC, BC])}
        woT = s.sb("woT", [P, CH, C])
        gamma = s.sb("gamma", [P, 2, BC])
        bias = s.sb("bias", [P, BH, 2 * P])
        minus_half = s.sb("minus_half", [P, 2])
        xT = s.sb("xT", [P, 2, KC, P])
        x = s.sb("x", [P, 2, C])
        raw = s.sb("raw", [P, 2, BC])
        square = s.sb("square", [P, HW])
        ss = s.sb("ss", [P, 2, HALVES])
        ms = s.sb("ms", [P, 2])
        rrms = s.sb("rrms", [P, 2])
        normed = s.sb("normed", [P, 2, BC])
        qT = s.sb("qT", [P, 2, CH, P])
        kT = s.sb("kT", [P, CH, T])
        v = s.sb("v", [P, NT, BC])
        score = s.sb("score", [P, 4, 2 * P])
        low = s.sb("low", [P, 4])
        prob = s.sb("prob", [P, 4, 2 * P])
        probT = s.sb("probT", [P, 2, 2, 2, P])
        rsum = s.sb("rsum", [P, 2, BH])
        rinv = s.sb("rinv", [P, 2, BH])
        o = s.sb("o", [P, 2, BC])
        oT = s.sb("oT", [P, CH, P])
        ps_s = [[s.ps(f"ps_s{q}{r}", [P, 2, 2 * P]) for r in range(2)] for q in range(2)]
        ps_p = [s.ps(f"ps_p{q}", [P, 2, 2, P]) for q in range(2)]
        ps_o = s.ps("ps_o", [P, HW])
        ps_w = s.ps("ps_w", [P, HW])
        const_in = s.sem("const_in")
        xT_in = [s.sem(f"xT_in{p}") for p in range(2)]
        x_in = [s.sem(f"x_in{p}") for p in range(2)]
        y_out = [s.sem(f"y_out{p}") for p in range(2)]
        chain = s.sem("chain")
        held = s.sem("held")
        half_set = s.sem("half_set")
        filled = s.sem("filled")
        emptied = s.sem("emptied")
        squared = s.sem("squared")
        ms_ready = s.sem("ms_ready")
        pow_ready = s.sem("pow_ready")
        normed_ready = s.sem("normed_ready")
        scored = s.sem("scored")
        biased = s.sem("biased")
        exped = s.sem("exped")
        transposed = s.sem("transposed")
        copied = s.sem("copied")
        valued = s.sem("valued")
        o_taken = s.sem("o_taken")
        block = ctx.enter_context(s.programs())

        PROLOGUE = 10
        UNIT = 13

        def sections_before(b, t):
            return PROLOGUE if isinstance(b, int) and b == 0 and t == 0 else UNIT * (NT * b + t) + PROLOGUE - 3

        def steps(b, t, first, last, order=WINDOW_ORDER):
            n = sections_before(b, t)
            for kind, k in order:
                if (kind in NEXT and last) or (kind in PAST and first):
                    continue
                yield kind, k, n
                if kind in NEXT or kind in PAST:
                    n = n + 1

        def units(engine, unit):
            for t in range(NT):
                unit(0, t, t == 0, False)
            with engine.Fori(1, B - 1) as b:
                for t in range(NT):
                    unit(b, t, False, False)
            for t in range(NT):
                unit(B - 1, t, False, t == NT - 1)

        def following(b, t):
            return (b, t + 1) if t < NT - 1 else (b + 1, 0)

        def preceding(b, t):
            return (b, t - 1) if t else (b - 1, NT - 1)

        def first_tile():
            n = 0
            for kind, k in WINDOW_ORDER:
                if kind in NEXT:
                    yield kind, k, n
                    n += 1

        def last_tile():
            n = sections_before(B - 1, NT - 1) + UNIT - PROLOGUE
            for kind, k in (("out_T", 0), ("out_T", 1), ("out", 0)):
                yield kind, k, n
                n += 1

        def uses(b, t):
            return 2 * b + t // 2 + 1

        @block.sync
        def _(sp):
            for tile, dram in ((ident, const["ident"]), (wT["q"], wqT_d), (wT["k"], wkT_d), (wT["v"], wvT_d), (woT, woT_d),
                               (gamma, gamma_d), (bias, bias_d)):
                sp.dma_start(tile[tuple(slice(None) for _ in tile.shape)], dram).then_inc(const_in, 16)

            def load_xT(b, t):
                sp.dma_start(xT[:, t % 2, :, :], xnT_d[ds(b, 1)].rearrange("a p k t -> p (a k) t")[:, :, t * P:(t + 1) * P]).then_inc(xT_in[t % 2], 16)

            def tokens(dram, b, t):
                return dram[ds(b, 1)].rearrange("a t c -> t (a c)")[t * P:(t + 1) * P, :]

            def store(b, t, done):
                hold(sp, emptied, done + 1, held)
                sp.dma_start(tokens(y_d, b, t), x[:, t % 2, :]).then_inc(y_out[t % 2], 16)

            def unit(b, t, first, last):
                static = isinstance(b, int)
                if not (static and b == B - 1 and t >= 2):
                    hold(sp, emptied, sections_before(b, t), held)
                    load_xT(b + (t + 2) // NT, (t + 2) % NT)
                if not (static and b == 0 and t < 2):
                    past = (b, t - 2) if t >= 2 else (b - 1, t + 2)
                    store(*past, sections_before(*following(*past)) + 2)
                    hold(sp, y_out[t % 2], 16 * (uses(b, t) - 1), held)
                sp.dma_start(x[:, t % 2, :], tokens(x_d, b, t)).then_inc(x_in[t % 2], 16)

            load_xT(0, 0)
            load_xT(0, 1)
            units(nc.sync, unit)
            store(B - 1, NT - 2, sections_before(B - 1, NT - 1) + 2)
            store(B - 1, NT - 1, sections_before(B - 1, NT - 1) + 5)
            for p in range(2):
                sp.wait_ge(y_out[p], 16 * (NT * B // 2))

        @block.tensor
        def _(pe):
            pe.sem_inc(transposed, 2)
            pe.sem_inc(valued, 2)
            pe.wait_ge(const_in, 16 * 7)

            def section(kind, k, n, b, t):
                w = NT * b + t
                if not (isinstance(n, int) and n == 0):
                    pe.wait_ge(emptied, n)
                if kind in ("q", "k", "v"):
                    if kind == "q" and k == 0:
                        pe.wait_ge(xT_in[t % 2], 16 * uses(b, t))
                    for c in range(KC):
                        last = nc.tensor.matmul(ps_w[:, :], xT[:, t % 2, c, :], wT[kind][:, c, k * HW:(k + 1) * HW],
                                                start=(c == 0), stop=(c == KC - 1))
                elif kind in ("q_T", "k_T"):
                    which = 0 if kind == "q_T" else 1
                    pe.wait_ge(normed_ready, 2 * w + which + 3)
                    for c in range(4):
                        last = nc.tensor.transpose(ps_w[:, c * P:(c + 1) * P], normed[:, which, (4 * k + c) * P:(4 * k + c + 1) * P], ident[:, :])
                elif kind == "out_T":
                    pe.wait_ge(o_taken, 2 * w + 3)
                    for c in range(4):
                        last = nc.tensor.transpose(ps_w[:, c * P:(c + 1) * P], o[:, t % 2, (4 * k + c) * P:(4 * k + c + 1) * P], ident[:, :])
                else:
                    for c in range(CH):
                        last = nc.tensor.matmul(ps_w[:, 0:C], oT[:, c, :], woT[:, c, :], start=(c == 0), stop=(c == CH - 1))
                last.then_inc(filled, 1)

            def unit(b, t, first, last):
                u = NT * b + t
                lo = 1 if t == 0 else 0
                pe.wait_ge(emptied, sections_before(b, t))
                for kind, k, n in steps(b, t, first, last):
                    if kind in NEXT:
                        section(kind, k, n, *following(b, t))
                    elif kind in PAST:
                        section(kind, k, n, *preceding(b, t))
                    elif kind == "scores":
                        pe.wait_ge(biased, 16 * u + 4 * k + 4)
                        for hh in range(4):
                            h = 4 * k + hh
                            r = slice(BD * (h % 2), BD * (h % 2) + BD)
                            mm = nc.tensor.matmul(ps_s[k % 2][hh % 2][:, hh // 2, lo * P:], qT[r, t % 2, h // 2, :],
                                                  kT[r, h // 2, (t - 1 + lo) * P:(t + 1) * P], start=True, stop=True)
                        mm.then_inc(scored, 1)
                    elif kind == "probs_T":
                        pe.wait_ge(exped, 16 * u + 2 * k + 6)
                        pe.wait_ge(copied, 8 * u + k + 1)
                        for r in range(2):
                            for c in range(lo, 2):
                                mm = nc.tensor.transpose(ps_p[k % 2][:, r, c, :], prob[:, 2 * (k % 2) + r, c * P:(c + 1) * P], ident[:, :])
                        mm.then_inc(transposed, 1)
                    else:
                        pe.wait_ge(copied, 8 * u + k + 3)
                        if k % 4 == 0:
                            pe.wait_ge(o_taken, 2 * u + k // 4 + 1)
                        for r in range(2):
                            h = 2 * k + r
                            for c in range(lo, 2):
                                mm = nc.tensor.matmul(ps_o[:, h % 8 * BD:(h % 8 + 1) * BD], probT[:, k % 2, r, c, :],
                                                      v[:, t - 1 + c, h * BD:(h + 1) * BD], start=(c == lo), stop=(c == 1))
                        mm.then_inc(valued, 1)

            for kind, k, n in first_tile():
                section(kind, k, n, 0, 0)
            units(nc.tensor, unit)
            for kind, k, n in last_tile():
                section(kind, k, n, B - 1, NT - 1)

        @block.scalar
        def _(act):
            act.sem_inc(exped, 4)

            def section(kind, k, n, b, t):
                if kind == "out":
                    return
                act.wait_ge(filled, n + 1)
                if kind in ("q", "k"):
                    which = 0 if kind == "q" else 1
                    nc.scalar.activation(square[:, :], ps_w[:, :], ACT.Square, accum_out=ss[:, which, k:k + 1]).then_inc(squared, 1)
                    return
                by_chunk = ps_w[:, :].rearrange("p (c t) -> p c t", t=P)
                if kind == "v":
                    copy = nc.scalar.copy(v[:, t, k * HW:(k + 1) * HW], ps_w[:, :])
                elif kind == "q_T":
                    copy = nc.scalar.copy(qT[:, t % 2, 4 * k:4 * k + 4, :], by_chunk)
                elif kind == "k_T":
                    copy = nc.scalar.copy(kT[:, 4 * k:4 * k + 4, t * P:(t + 1) * P], by_chunk)
                else:
                    copy = nc.scalar.copy(oT[:, 4 * k:4 * k + 4, :], by_chunk)
                copy.then_inc(emptied, 1)

            def unit(b, t, first, last):
                u = NT * b + t
                lo = 1 if t == 0 else 0
                for kind, k, n in steps(b, t, first, last, WINDOW_SCALAR_ORDER):
                    if kind in NEXT:
                        section(kind, k, n, *following(b, t))
                    elif kind in PAST:
                        section(kind, k, n, *preceding(b, t))
                    elif kind == "scores":
                        for hh in range(4):
                            h = 4 * k + hh
                            act.wait_ge(biased, 16 * u + h + 9)
                            if h % 2 == 0:
                                act.wait_ge(transposed, 8 * u + h // 2 + 1)
                            nc.scalar.activation(prob[:, hh, lo * P:], score[:, hh, lo * P:], ACT.Exp, bias=low[:, hh:hh + 1], scale=-1.0,
                                                 accum_out=rsum[:, t % 2, h:h + 1]).then_inc(exped, 1)

            for kind, k, n in first_tile():
                section(kind, k, n, 0, 0)
            units(nc.scalar, unit)
            for kind, k, n in last_tile():
                section(kind, k, n, B - 1, NT - 1)

        @block.gpsimd
        def _(pool):
            nc.gpsimd.memset(minus_half[:, :], -0.5).then_inc(half_set, 1)
            pool.sem_inc(normed_ready, 2)
            pool.wait_ge(half_set, 1)
            with nc.gpsimd.Fori(0, NT * B) as w:
                pool.wait_ge(ms_ready, w + 1)
                nc.gpsimd.tensor_tensor(rrms[:, :], ms[:, :], minus_half[:, :], ALU.pow).then_inc(pow_ready, 1)
                hold(pool, pow_ready, w + 1, held)
                for i in range(2):
                    nc.gpsimd.tensor_scalar(normed[:, i, :], raw[:, i, :], rrms[:, i:i + 1], 1.0, ALU.mult, ALU.mult).then_inc(normed_ready, 1)

        @block.vector
        def _(dve):
            dve.sem_inc(biased, 8)
            dve.sem_inc(copied, 2)
            dve.sem_inc(o_taken, 1)
            dve.wait_ge(const_in, 16 * 7)

            def section(kind, k, n, b, t, ch):
                w = NT * b + t
                if kind in ("q", "k"):
                    which = 0 if kind == "q" else 1
                    dve.wait_ge(squared, 4 * w + 2 * which + k + 1)
                    if kind == "q" and k == 0:
                        dve.wait_ge(normed_ready, 2 * w + 2)
                    half = slice(k * HW, (k + 1) * HW)
                    nc.vector.tensor_tensor(raw[:, which, half], ps_w[:, :], gamma[:, which, half], ALU.mult).then_inc(emptied, 1)
                    if kind == "k" and k == 1:
                        ch.link(nc.vector.tensor_tensor(ms[:, :], ss[:, :, 0], ss[:, :, 1], ALU.add))
                        nc.vector.tensor_scalar(ms[:, :], ms[:, :], 1.0 / BC, RMS_EPS, ALU.mult, ALU.add).then_inc(ms_ready, 1)
                elif kind == "out":
                    dve.wait_ge(x_in[t % 2], 16 * uses(b, t))
                    dve.wait_ge(filled, n + 1)
                    nc.vector.tensor_tensor(x[:, t % 2, :], x[:, t % 2, :], ps_w[:, 0:C], ALU.add).then_inc(emptied, 1)

            def unit(b, t, first, last):
                u = NT * b + t
                lo = 1 if t == 0 else 0
                ch = Chain(dve, chain, 3 * u + 1)
                for kind, k, n in steps(b, t, first, last):
                    if kind in NEXT:
                        section(kind, k, n, *following(b, t), ch)
                    elif kind in PAST:
                        section(kind, k, n, *preceding(b, t), ch)
                    elif kind == "scores":
                        dve.wait_ge(scored, 4 * u + k + 1)
                        for hh in range(4):
                            h = 4 * k + hh
                            hold(dve, exped, 16 * u + h + 1, held)
                            nc.vector.tensor_tensor_reduce(out=score[:, hh, lo * P:], in0=ps_s[k % 2][hh % 2][:, hh // 2, lo * P:],
                                                           in1=bias[:, h, lo * P:], scale=-B_SCALE, scalar=3.0e38, op0=ALU.add, op1=ALU.min,
                                                           accum_out=low[:, hh:hh + 1]).then_inc(biased, 1)
                    elif kind == "probs_T":
                        dve.wait_ge(transposed, 8 * u + k + 3)
                        dve.wait_ge(valued, 8 * u + k + 1)
                        nc.vector.tensor_copy(probT[:, k % 2, :, lo:, :], ps_p[k % 2][:, :, lo:, :]).then_inc(copied, 1)
                    elif k % 4 == 3:
                        half = k // 4
                        dve.wait_ge(valued, 8 * u + k + 3)
                        hs = slice(8 * half, 8 * half + 8)
                        ch.link(nc.vector.reciprocal(rinv[:, t % 2, hs], rsum[:, t % 2, hs]))
                        nc.vector.tensor_tensor(o[:, t % 2, half * HW:(half + 1) * HW].rearrange("p (h d) -> p h d", d=BD),
                                                ps_o[:, :].rearrange("p (h d) -> p h d", d=BD),
                                                rinv[:, t % 2, hs].unsqueeze(2).to_broadcast([P, 8, BD]), ALU.mult).then_inc(o_taken, 1)

            ch = Chain(dve, chain)
            for kind, k, n in first_tile():
                section(kind, k, n, 0, 0, ch)
            units(nc.vector, unit)
            for kind, k, n in last_tile():
                section(kind, k, n, B - 1, NT - 1, ch)


RELATIVE_ORDER = [
    ("scores", 0), ("q", 0), ("scores", 1), ("k", 0),
    ("scores", 2), ("probs_T", 0), ("v", 0), ("probs_T", 1), ("q_band", 0),
    ("scores", 3), ("probs_T", 2), ("k_band", 0), ("probs_T", 3), ("q_band", 1),
    ("scores", 4), ("probs_T", 4), ("values", 0), ("k_band", 1), ("probs_T", 5), ("q_band", 2),
    ("scores", 5), ("probs_T", 6), ("k_band", 2), ("probs_T", 7), ("q_band", 3),
    ("scores", 6), ("probs_T", 8), ("values", 1), ("k_band", 3), ("probs_T", 9), ("bins_T", 0),
    ("scores", 7), ("probs_T", 10), ("bins_T", 1), ("probs_T", 11), ("bins", 0),
    ("probs_T", 12), ("values", 2), ("q_stack", 0), ("probs_T", 13), ("out", 0), ("q_stack", 1),
    ("probs_T", 14), ("k_stack", 0), ("probs_T", 15), ("k_stack", 1), ("values", 3),
]


RELATIVE_SCALAR_ORDER = scores_later(RELATIVE_ORDER, ("probs_T", 12))
A_NEXT = ("q", "k", "v", "q_band", "k_band", "q_stack", "k_stack")
A_PAST = ("bins_T", "bins", "out")


def relative_stage(nc, tag, const, xnT_d, wT_d, rows_d, table_d, base_d, bins_d, bins_base_d, vbase_d, scratch, o_d):
    Q, K = 0, 1
    W4 = HG * WIN
    with ExitStack() as ctx:
        s = Store(nc, ctx, tag)
        ident = s.sb("ident", [P, P])
        lower = s.sb("lower", [P, P])
        upper = s.sb("upper", [P, P])
        wT = s.sb("wT", [P, 2, NG, KC, P])
        wv = s.sb("wv", [P, KC, C])
        diff = s.sb("diff", [P, 2, NG, HG, XB + 1])
        bins_w = s.sb("bins_w", [P, NG, 2, 64])
        vbase = s.sb("vbase", [P, 2, C])
        scale = s.sb("scale", [P, 4])
        shift = s.sb("shift", [P, 4])
        spread = s.sb("spread", [P, 2, 2, 2, P], F32R)
        xT = s.sb("xT", [P, KC, T])
        qk = s.sb("qk", [P, 2, T])
        masked = s.sb("masked", [P, T])
        high = s.sb("high", [P, 2, T], F32R)
        rest = s.sb("rest", [P, 2, T], F32R)
        q_stack = s.sb("q_stack", [P, 2, 2, T], F32R)
        k_stack = s.sb("k_stack", [P, 2, 2, 2, T], F32R)
        v = s.sb("v", [P, 2, 2, NT, HG, 32])
        band = s.sb("band", [P, 2, NT, HG, WIN])
        edge = s.sb("edge", [P, 2, 2, NT, HG])
        win = s.sb("win", [P, 2, 2, NT, HG, WIN])
        spare = win[:, :, :, :, :, :].rearrange("p a b c d e -> p (a b c d e)")
        spares = []
        for shape in ((2, NG, C), (2, NG, HG, XB + 1), (2, NG, HG, XB + 1), (NG, 2, 64), (2, 2, 2, P)):
            n = int(np.prod(shape))
            names = "abcdef"[:len(shape)]
            at = sum(spares[i][1] for i in range(len(spares)))
            spares.append((spare[:, at:at + n].rearrange(f"p ({' '.join(names)}) -> p {' '.join(names)}", **dict(zip(names, shape))), n))
        rows = spares[0][0]
        table = spares[1][0]
        base = spares[2][0]
        bins_b = spares[3][0]
        spread_in = spares[4][0]
        tri = s.sb("tri", [P, 2, HG, P])
        low = s.sb("low", [P, 2, 2])
        prob = s.sb("prob", [P, 2, HG, 32 + T + 32])
        probT = s.sb("probT", [P, 2, HG, T])
        rsum = s.sb("rsum", [P, 2, NT, HG])
        rinv = s.sb("rinv", [P, NT, HG])
        junk = s.sb("junk", [P, 2, P])
        below = s.sb("below", [P, 2, NT, HG])
        bins = s.sb("bins", [P, 2, NT, HG, XB])
        binsT = s.sb("binsT", [P, 2, NT, P])
        oT = s.sb("oT", [P, T])
        o = s.sb("o", [P, 2, NT, HG, AD])
        ps_s = [s.ps(f"ps_s{q}", [P, 2, T]) for q in range(2)]
        ps_p = [s.ps(f"ps_p{q}", [P, T]) for q in range(2)]
        ps_o = s.ps("ps_o", [P, T])
        ps_w = s.ps("ps_w", [P, T])
        const_in = s.sem("const_in")
        chain = s.sem("chain")
        pool_chain = s.sem("pool_chain")
        held = s.sem("held")
        folded = s.sem("folded")
        set_up = s.sem("set_up")
        xT_in = s.sem("xT_in")
        filled = s.sem("filled")
        emptied = s.sem("emptied")
        split = s.sem("split")
        band_out = [[s.sem(f"band_out{d}{t}") for t in range(NT)] for d in range(2)]
        win_in = [[s.sem(f"win_in{d}{t}") for t in range(NT)] for d in range(2)]
        win_ready = s.sem("win_ready")
        scored = s.sem("scored")
        maxed = s.sem("maxed")
        exped = s.sem("exped")
        transposed = s.sem("transposed")
        copied = [s.sem(f"copied{q}") for q in range(2)]
        valued = s.sem("valued")
        summed = s.sem("summed")
        prob_out = [s.sem(f"prob_out{q}") for q in range(2)]
        bins_in = [s.sem(f"bins_in{q}") for q in range(2)]
        bins_ready = s.sem("bins_ready")
        o_taken = s.sem("o_taken")
        o_ready = s.sem("o_ready")
        o_out = [s.sem(f"o_out{q}") for q in range(2)]
        loads = ((ident, const["ident"]), (lower, const["lower"]), (upper, const["upper"]), (wT, wT_d[0]), (wv, wT_d[1]), (rows, rows_d),
                 (table, table_d), (base, base_d), (bins_w, bins_d), (bins_b, bins_base_d), (vbase, vbase_d),
                 (scale, const["row_scale"]), (shift, const["row_shift"]), (spread_in, const["spread"]))
        block = ctx.enter_context(s.programs())

        PROLOGUE = sum(kind in A_NEXT for kind, _ in RELATIVE_ORDER)
        PAST = sum(kind in A_PAST for kind, _ in RELATIVE_ORDER)
        UNIT = PROLOGUE + PAST

        def sections_before(b, g):
            return PROLOGUE if isinstance(b, int) and b == 0 and g == 0 else UNIT * (NG * b + g) + PROLOGUE - PAST

        def steps(b, g, first, last, order=RELATIVE_ORDER):
            n = sections_before(b, g)
            for kind, k in order:
                if (kind in A_NEXT and last) or (kind in A_PAST and first):
                    continue
                yield kind, k, n
                if kind in A_NEXT or kind in A_PAST:
                    n = n + 1

        def units(engine, unit):
            for g in range(NG):
                unit(0, g, g == 0, False)
            with engine.Fori(1, B - 1) as b:
                for g in range(NG):
                    unit(b, g, False, False)
            for g in range(NG):
                unit(B - 1, g, False, g == NG - 1)

        def following(b, g):
            return (b, g + 1) if g < NG - 1 else (b + 1, 0)

        def preceding(b, g):
            return (b, g - 1) if g else (b - 1, NG - 1)

        def first_unit():
            n = 0
            for kind, k in RELATIVE_ORDER:
                if kind in A_NEXT:
                    yield kind, k, n
                    n += 1

        def last_unit():
            n = sections_before(B - 1, NG - 1) + UNIT - PROLOGUE
            for kind, k in RELATIVE_ORDER:
                if kind in A_PAST:
                    yield kind, k, n
                    n += 1

        def section_number(b, g, kind, k):
            early = isinstance(b, int) and b == 0 and g < 2
            place = [x for x in RELATIVE_ORDER if x[0] in A_NEXT or (x[0] in A_PAST and not early)].index((kind, k))
            return place if early and g == 0 else sections_before(*preceding(b, g)) + place

        def uses(b, g):
            return 2 * b + g // 2 + 1

        def window_columns(t):
            return max(0, t * P - 32), min(T, t * P + P + 32), 32 if t == 0 else 0

        @block.sync
        def _(sp):
            for tile, dram in loads:
                sp.dma_start(tile[tuple(slice(None) for _ in tile.shape)], dram).then_inc(const_in, 16)

            def next_unit(b, g):
                u = NG * b + g
                if g == 0:
                    if not (isinstance(b, int) and b == 0):
                        hold(sp, emptied, section_number(*preceding(b, g), "v", 0) + 1, held)
                    sp.dma_start(xT[:, :, :], by_channel(xnT_d, b)).then_inc(xT_in, 16)
                for step in range(NT + 1):
                    for d in range(2):
                        if step < NT:
                            hold(sp, emptied, section_number(b, g, ("q_band", "k_band")[d], step) + 1, held)
                            sp.dma_start(scratch["band"][d, g % 2, step], band[:, d, step, :, :].rearrange("p h x -> p (h x)")).then_inc(band_out[d][step], 16)
                        if step:
                            t = step - 1
                            hold(sp, band_out[d][t], 16 * u + 16, held)
                            rows_at = scratch["band"][d, g % 2, t]
                            skewed = bass.AP(rows_at.tensor, rows_at.offset, [[W4 - 1, P], [1, W4]])
                            sp.dma_start(win[:, g % 2, d, t, :, :].rearrange("p h x -> p (h x)"), skewed).then_inc(win_in[d][t], 16)

            def store(b, g):
                hold(sp, o_ready, NG * b + g + 1, held)
                out = o_d[ds(b, 1)].rearrange("a (t p) c -> p (a t) c", p=P)[:, :, g * HG * AD:(g + 1) * HG * AD]
                sp.dma_start(out, o[:, g % 2, :, :, :].rearrange("p t h d -> p t (h d)")).then_inc(o_out[g % 2], 16)

            def unit(b, g, first, last):
                if not last:
                    next_unit(*following(b, g))
                if not first:
                    store(*preceding(b, g))

            next_unit(0, 0)
            units(nc.sync, unit)
            store(B - 1, NG - 1)
            for q in range(2):
                sp.wait_ge(o_out[q], 16 * NG * B // 2)

        @block.tensor
        def _(pe):
            pe.sem_inc(transposed, 8)
            pe.sem_inc(valued, 2)
            pe.wait_ge(const_in, 16 * len(loads))
            for d in range(2):
                for end in range(2):
                    x = ((1, BUCKETS), (BUCKETS, 1))[d][end]
                    for g in range(NG):
                        for c in range(KC):
                            at = (((d * 2 + end) * NG + g) * KC + c) * HG
                            last = nc.tensor.matmul(ps_w[:, at:at + HG], rows[:, d, g, c * P:(c + 1) * P], table[:, d, g, :, x], start=True, stop=True)
            last.then_inc(folded, 1)
            pe.wait_ge(set_up, 1)

            def section(kind, k, n, b, g):
                if not (isinstance(n, int) and n == 0):
                    pe.wait_ge(emptied, n)
                if kind in ("q", "k"):
                    if kind == "q" and g == 0:
                        pe.wait_ge(xT_in, 16 * b + 16)
                    for c in range(KC):
                        last = nc.tensor.matmul(ps_w[:, :], wT[:, 0 if kind == "q" else 1, g, c, :], xT[:, c, :], start=(c == 0), stop=(c == KC - 1))
                elif kind == "v":
                    for t in range(NT):
                        for c in range(KC):
                            last = nc.tensor.matmul(ps_w[:, t * HG * AD:(t + 1) * HG * AD], xT[:, c, t * P:(t + 1) * P],
                                                    wv[:, c, g * HG * AD:(g + 1) * HG * AD], start=(c == 0), stop=(c == KC - 1))
                elif kind in ("q_band", "k_band"):
                    d = 0 if kind == "q_band" else 1
                    last = nc.tensor.matmul(ps_w[:, 0:HG * (XB + 1)], qk[:, d, k * P:(k + 1) * P],
                                            diff[:, d, g, :, :].rearrange("p h x -> p (h x)"), start=True, stop=True)
                elif kind in ("q_stack", "k_stack"):
                    d = 0 if kind == "q_stack" else 1
                    pe.wait_ge(split, 2 * (NG * b + g) + 1 + d)
                    nc.tensor.matmul(ps_w[:, :], spread[:, d, k, 0, :], high[:, d, :], start=True, stop=False)
                    last = nc.tensor.matmul(ps_w[:, :], spread[:, d, k, 1, :], rest[:, d, :], start=False, stop=True)
                elif kind == "bins_T":
                    if k == 0:
                        pe.wait_ge(bins_ready, NG * b + g + 1)
                    for m in range(4):
                        t, r = 2 * k + m % 2, m // 2
                        last = nc.tensor.transpose(ps_w[:, m * P:(m + 1) * P], bins[:, g % 2, t, 2 * r:2 * r + 2, :].rearrange("p h x -> p (h x)"), ident[:, :])
                elif kind == "bins":
                    for r in range(2):
                        last = nc.tensor.matmul(ps_w[64 * r:64 * r + 64, :], bins_w[:, g, r, :], binsT[:, r, :, :].rearrange("p t i -> p (t i)"), start=True, stop=True)
                else:
                    for t in range(NT):
                        last = nc.tensor.transpose(ps_w[:, t * P:(t + 1) * P], oT[:, t * P:(t + 1) * P], ident[:, :])
                last.then_inc(filled, 1)

            def unit(b, g, first, last):
                u = NG * b + g
                p = g % 2
                pe.wait_ge(emptied, sections_before(b, g))
                for kind, k, n in steps(b, g, first, last):
                    if kind in A_NEXT:
                        section(kind, k, n, *following(b, g))
                    elif kind in A_PAST:
                        section(kind, k, n, *preceding(b, g))
                    elif kind == "scores":
                        t = k // 2
                        pe.wait_ge(win_ready, 8 * u + 2 * min(t + 1, NT - 1) + 2)
                        pe.wait_ge(exped, 16 * u + 2 * k + 2)
                        heads = [2 * (k % 2), 2 * (k % 2) + 1]
                        for h in heads:
                            r = slice(64 * (h % 2), 64 * (h % 2) + 64)
                            q_tile = q_stack[r, p, k % 2, t * P:(t + 1) * P]
                            bank = ps_s[k % 2][:, h % 2, :]
                            if t:
                                nc.tensor.matmul(bank[:, 0:t * P], q_tile, k_stack[r, p, 0, k % 2, 0:t * P], start=True, stop=False)
                            nc.tensor.matmul(bank[:, t * P:], q_tile, k_stack[r, p, 1, k % 2, t * P:], start=(t == 0), stop=False)
                        for h in heads:
                            bank = ps_s[k % 2][:, h % 2, :]
                            if t:
                                nc.tensor.matmul(bank[0:32, t * P - 32:t * P], win[96:P, p, K, t - 1, h, 160:192], ident[96:P, 96:P], start=False, stop=False)
                            if t < NT - 1:
                                nc.tensor.matmul(bank[96:P, (t + 1) * P:(t + 1) * P + 32], win[0:32, p, K, t + 1, h, 0:32], ident[0:32, 0:32], start=False, stop=False)
                            mm = nc.tensor.matmul(bank[:, t * P:(t + 1) * P], win[:, p, K, t, h, 32:160], ident[:, :], start=False, stop=True)
                        mm.then_inc(scored, 1)
                    elif kind == "probs_T":
                        t, h = k // HG, k % HG
                        pe.wait_ge(exped, 16 * u + k + 5)
                        pe.wait_ge(copied[k % 2], 8 * u + k // 2 + 1)
                        for c in range(NT):
                            mm = nc.tensor.transpose(ps_p[k % 2][:, c * P:(c + 1) * P], prob[:, t % 2, h, 32 + c * P:32 + (c + 1) * P], ident[:, :])
                        mm.then_inc(transposed, 1)
                    else:
                        t = k
                        for q in range(2):
                            pe.wait_ge(copied[q], 8 * u + 2 * t + 3)
                        if t == 0:
                            pe.wait_ge(o_taken, u + 1)
                        for c in range(NT):
                            for h in range(HG):
                                mm = nc.tensor.matmul(ps_o[32 * h:32 * h + 32, t * P:(t + 1) * P], v[:, p, 0 if c < t else 1, c, h, :],
                                                      probT[:, t % 2, h, c * P:(c + 1) * P], start=(c == 0), stop=(c == NT - 1))
                        mm.then_inc(valued, 1)

            for kind, k, n in first_unit():
                section(kind, k, n, 0, 0)
            units(nc.tensor, unit)
            for kind, k, n in last_unit():
                section(kind, k, n, B - 1, NG - 1)

        @block.scalar
        def _(act):
            act.sem_inc(exped, 4)
            act.sem_inc(copied[1], 1)
            act.wait_ge(const_in, 16 * len(loads))

            def section(kind, k, n, b, g):
                p = g % 2
                if kind in ("v", "bins", "out", "q_stack"):
                    return
                act.wait_ge(filled, n + 1)
                if kind in ("q", "k"):
                    i = 0 if kind == "q" else 1
                    last = nc.scalar.activation(qk[:, i, :], ps_w[:, :], ACT.Identity, bias=shift[:, i:i + 1], scale=scale[:, i:i + 1])
                elif kind == "k_stack":
                    for i in range(2):
                        last = nc.scalar.activation(k_stack[:, p, i, k, :], ps_w[:, :], ACT.Identity, bias=shift[:, 2 + i:3 + i], scale=scale[:, 2 + i:3 + i])
                elif kind in ("q_band", "k_band"):
                    d = 0 if kind == "q_band" else 1
                    if not (isinstance(b, int) and b == 0 and g == 0):
                        act.wait_ge(band_out[d][k], 16 * (NG * b + g))
                    got = ps_w[:, 0:HG * (XB + 1)].rearrange("p (h x) -> p h x", h=HG)
                    nc.scalar.copy(band[:, d, k, :, 0:XB], got[:, :, 0:XB])
                    last = nc.scalar.copy(edge[:, p, d, k, :].unsqueeze(2), got[:, :, XB:])
                else:
                    last = nc.scalar.copy(binsT[:, :, 2 * k:2 * k + 2, :].rearrange("p r t i -> p r (t i)"), ps_w[:, :].rearrange("p (r x) -> p r x", r=2))
                last.then_inc(emptied, 1)

            def bins_home(b, g, t):
                act.wait_ge(prob_out[t % 2], 16 * (2 * (NG * b + g) + t // 2 + 1))
                src = scratch["prob"][t % 2]
                skewed = bass.AP(src.tensor, src.offset, [[W4 + 1, P], [WIN, HG], [1, XB]])
                act.dma_start(bins[:, g % 2, t, :, :], skewed).then_inc(bins_in[t % 2], 16)

            def unit(b, g, first, last):
                u = NG * b + g
                p = g % 2
                for kind, k, n in steps(b, g, first, last, RELATIVE_SCALAR_ORDER):
                    if kind in A_NEXT:
                        section(kind, k, n, *following(b, g))
                    elif kind in A_PAST:
                        section(kind, k, n, *preceding(b, g))
                    elif kind == "scores":
                        t = k // 2
                        act.wait_ge(maxed, 8 * u + k + 1)
                        if k % 2 == 0:
                            act.wait_ge(transposed, 16 * u + 4 * t + 4)
                            act.wait_ge(summed, 16 * u + 4 * t + 4)
                            if not (first and t < 2):
                                act.wait_ge(prob_out[t % 2], 16 * (2 * u + t // 2))
                        for r in range(2):
                            h = 2 * (k % 2) + r
                            nc.scalar.activation(prob[:, t % 2, h, 32:32 + T], ps_s[k % 2][:, r, :], ACT.Exp, bias=low[:, k % 2, r:r + 1],
                                                 accum_out=rsum[:, p, t, h:h + 1]).then_inc(exped, 1)
                        if k % 2:
                            act.wait_ge(exped, 16 * u + 4 * t + 8)
                            if not (first and t < 2):
                                act.wait_ge(bins_in[t % 2], 16 * (2 * u + t // 2))
                            act.dma_start(scratch["prob"][t % 2].rearrange("p (h x) -> p h x", h=HG),
                                          prob[:, t % 2, :, t * P:t * P + WIN]).then_inc(prob_out[t % 2], 16)
                            if t:
                                bins_home(b, g, t - 1)
                            elif not first:
                                bins_home(*preceding(b, g), NT - 1)
                    elif kind == "probs_T" and k % 2:
                        act.wait_ge(transposed, 16 * u + k + 9)
                        act.wait_ge(valued, 4 * u + k // HG + 1)
                        nc.scalar.copy(probT[:, k // HG % 2, k % HG, :], ps_p[1][:, :]).then_inc(copied[1], 1)

            act.wait_ge(set_up, 1)
            for kind, k, n in first_unit():
                section(kind, k, n, 0, 0)
            units(nc.scalar, unit)
            bins_home(B - 1, NG - 1, NT - 1)
            for kind, k, n in last_unit():
                section(kind, k, n, B - 1, NG - 1)

        @block.gpsimd
        def _(pool):
            def next_unit(b, g):
                u = NG * b + g
                ch = Chain(pool, pool_chain, 8 * u)
                for t in range(NT):
                    if not (isinstance(u, int) and u + t == 0):
                        pool.wait_ge(win_ready, 8 * u + 2 * t)
                    pool.wait_ge(emptied, section_number(b, g, "k_band", t) + 1)
                    for d in range(2):
                        ch.mark(nc.gpsimd.tensor_tensor(tri[:, d, :, :], (lower, upper)[d][:, :].unsqueeze(1).to_broadcast([P, HG, P]),
                                                        edge[:, g % 2, d, t, :].unsqueeze(2).to_broadcast([P, HG, P]), ALU.mult))
                    ch.settle()
                    for d in range(2):
                        pool.wait_ge(win_in[d][t], 16 * u + 16)
                        square = win[:, g % 2, d, t, :, 32:160]
                        nc.gpsimd.tensor_tensor(square, square, tri[:, d, :, :], ALU.add).then_inc(win_ready, 1)

            def unit(b, g, first, last):
                if not last:
                    next_unit(*following(b, g))

            pool.wait_ge(const_in, 16 * len(loads))
            next_unit(0, 0)
            units(nc.gpsimd, unit)

        @block.vector
        def _(dve):
            SETUP = 3
            dve.sem_inc(copied[0], 1)
            dve.sem_inc(summed, 8)
            dve.sem_inc(o_taken, 1)
            ch = Chain(dve, chain)
            nc.vector.memset(v[:, :, :, :, :, AD:].rearrange("p a b t h d -> p (a b t h) d"), 0.0)
            ch.mark(nc.vector.memset(band[:, :, :, :, XB:].rearrange("p d t h x -> p (d t h) x"), 0.0))
            nc.vector.memset(prob[:, :, :, 0:32].rearrange("p t h x -> p (t h) x"), 0.0)
            ch.mark(nc.vector.memset(prob[:, :, :, 32 + T:].rearrange("p t h x -> p (t h) x"), 0.0))
            dve.wait_ge(const_in, 16 * len(loads))
            flat = lambda x: x[:, :, :, :, :].rearrange("p d g h x -> p (d g h x)")
            ch.mark(nc.vector.tensor_tensor(flat(diff), flat(table), flat(base), ALU.subtract))
            ch.settle()
            nc.vector.tensor_scalar(diff[:, K, :, :, :], diff[:, K, :, :, :], A_SCALE, None, ALU.mult)
            nc.vector.tensor_tensor(bins_w[:, :, :, :], bins_w[:, :, :, :], bins_b[:, :, :, :], ALU.subtract)
            nc.vector.tensor_copy(spread[:, :, :, :, :].rearrange("p d k i x -> p (d k i x)"), spread_in[:, :, :, :, :].rearrange("p d k i x -> p (d k i x)"))
            dve.wait_ge(folded, 1)
            for d in range(2):
                for end in range(2):
                    at = (d * 2 + end) * NG * KC * HG
                    last = nc.vector.tensor_copy(wT[:, d, :, :, :].rearrange("p g c (h r) -> p (g c) h r", r=32)[:, :, :, AD + 2 * d + end],
                                                 ps_w[:, at:at + NG * KC * HG].rearrange("p (m h) -> p m h", h=HG))
            last.then_inc(set_up, 1)

            def section(kind, k, n, b, g, ch):
                p = g % 2
                if kind == "v":
                    dve.wait_ge(filled, n + 1)
                    for i in range(2):
                        last = nc.vector.tensor_tensor(v[:, p, i, :, :, 0:AD], ps_w[:, 0:C].rearrange("p (t h d) -> p t h d", t=NT, h=HG),
                                                       vbase[:, i, g * HG * AD:(g + 1) * HG * AD].rearrange("p (h d) -> p h d", h=HG)
                                                       .unsqueeze(1).to_broadcast([P, NT, HG, AD]), ALU.add)
                    last.then_inc(emptied, 1)
                elif kind in ("q", "k"):
                    i = 0 if kind == "q" else 1
                    dve.wait_ge(emptied, n + 1)
                    if not (isinstance(b, int) and b == 0 and g + i == 0):
                        dve.wait_ge(split, 2 * (NG * b + g) + i)
                    ch.link(nc.vector.tensor_single_scalar(masked[:, :].bitcast(I32), qk[:, i, :].bitcast(I32), HIGH_BITS, ALU.bitwise_and))
                    nc.vector.tensor_copy(high[:, i, :], masked[:, :])
                    nc.vector.tensor_tensor(rest[:, i, :], qk[:, i, :], masked[:, :], ALU.subtract).then_inc(split, 1)
                elif kind == "q_stack":
                    dve.wait_ge(filled, n + 1)
                    nc.vector.tensor_copy(q_stack[:, p, k, :], ps_w[:, :]).then_inc(emptied, 1)
                elif kind == "bins":
                    ch.link(nc.vector.reciprocal(rinv[:, :, :], rsum[:, p, :, :]))
                    dve.wait_ge(filled, n + 1)
                    dve.wait_ge(o_taken, NG * b + g + 2)
                    nc.vector.tensor_tensor(oT[:, :], oT[:, :], ps_w[:, :], ALU.add).then_inc(emptied, 1)
                elif kind == "out":
                    dve.wait_ge(filled, n + 1)
                    if not (isinstance(b, int) and b == 0 and g < 2):
                        dve.wait_ge(o_out[p], 16 * (uses(b, g) - 1))
                    ch.link(nc.vector.tensor_tensor(o[:, p, :, :, :].rearrange("p t h d -> p (t h) d"), ps_w[:, :].rearrange("p (m r) -> p m r", r=32)[:, :, 0:AD],
                                                    rinv[:, :, :].rearrange("p t h -> p (t h)").unsqueeze(2).to_broadcast([P, NT * HG, AD]), ALU.mult))
                    dve.sem_inc(emptied, 1)
                    dve.sem_inc(o_ready, 1)
                elif kind == "bins_T" and k == 0:
                    for t in range(NT - 2, NT):
                        dve.wait_ge(bins_in[t % 2], 16 * (2 * (NG * b + g) + 2))
                    dve.wait_ge(summed, 16 * (NG * b + g) + 24)
                    nc.vector.tensor_copy(bins[:, p, :, :, 0], below[:, p, :, :]).then_inc(bins_ready, 1)

            def unit(b, g, first, last):
                u = NG * b + g
                p = g % 2
                ch = Chain(dve, chain, SETUP + 2 if isinstance(b, int) and u == 0 else 12 * u + SETUP)
                for kind, k, n in steps(b, g, first, last):
                    if kind in A_NEXT:
                        section(kind, k, n, *following(b, g), ch)
                    elif kind in A_PAST:
                        section(kind, k, n, *preceding(b, g), ch)
                    elif kind == "scores":
                        t = k // 2
                        c0, c1, x0 = window_columns(t)
                        h0 = 2 * (k % 2)
                        dve.wait_ge(win_ready, 8 * u + 2 * t + 1)
                        dve.wait_ge(scored, 8 * u + k + 1)
                        both = ps_s[k % 2]
                        ch.link(nc.vector.tensor_tensor(both[:, :, c0:c1], both[:, :, c0:c1], win[:, p, Q, t, h0:h0 + 2, x0:x0 + c1 - c0], ALU.add))
                        nc.vector.reduce_max(low[:, k % 2, :], both[:, :, :], AX.X, negate=True).then_inc(maxed, 1)
                    elif kind == "probs_T":
                        t, h = k // HG, k % HG
                        if k % 2 == 0:
                            dve.wait_ge(transposed, 16 * u + k + 9)
                            dve.wait_ge(valued, 4 * u + k // HG + 1)
                            nc.vector.tensor_copy(probT[:, k // HG % 2, k % HG, :], ps_p[0][:, :]).then_inc(copied[0], 1)
                        dve.wait_ge(summed, 16 * u + k + 7)
                        hold(dve, exped, 16 * u + k + 5, held)
                        nc.vector.tensor_tensor_reduce(out=junk[:, k % 2, :], in0=prob[:, t % 2, h, 32 + t * P:32 + (t + 1) * P], in1=lower[:, :],
                                                       scale=1.0, scalar=0.0, op0=ALU.mult, op1=ALU.add, accum_out=below[:, p, t, h:h + 1]).then_inc(summed, 1)
                    elif kind == "values" and k == NT - 1:
                        dve.wait_ge(valued, 4 * u + 6)
                        nc.vector.tensor_copy(oT[:, :], ps_o[:, :]).then_inc(o_taken, 1)

            for kind, k, n in first_unit():
                section(kind, k, n, 0, 0, ch)
            units(nc.vector, unit)
            ch = Chain(dve, chain, 12 * NG * B + SETUP - 2)
            for kind, k, n in last_unit():
                section(kind, k, n, B - 1, NG - 1, ch)


def hybrid_block(nc, ins, out):
    def scratch(name, shape):
        return nc.dram_tensor(name, shape, F32, kind="Internal").ap()

    with ExitStack() as ctx:
        scores = ctx.enter_context(nc.sbuf_tensor("scores", [P, NT, B, E], F32))
        slot_token = ctx.enter_context(nc.sbuf_tensor("slot_token", [P, E, CT], I32))
        slot_weight = ctx.enter_context(nc.sbuf_tensor("slot_weight", [P, E, CT], F32))
        xnT = scratch("xnT", (B, P, KC, T))
        xn = scratch("xn", (B, T, C))
        x1 = scratch("x1", (B, T, C))
        x2 = scratch("x2", (B, T, C))
        x3 = scratch("x3", (B, T, C))
        heads = scratch("heads", (B, T, C))
        trips = {"band": scratch("band", (2, 2, NT, P, HG * WIN)), "prob": scratch("prob", (2, P, HG * WIN))}
        ident = ins["ident"]

        def mixture(tag, x, y):
            route_stage(nc, f"{tag}r", ins, scores, slot_token, slot_weight)
            shared_stage(nc, f"{tag}s", xnT, x, ins["SgT"], ins["SuT"], ins["SdT"], y)
            expert_stage(nc, f"{tag}e", ident, xn, slot_token, slot_weight, ins["WgT"], ins["WuT"], ins["WdT"], y)

        norm_stage(nc, "n0", ident, ins["x"], xnT)
        relative_stage(nc, "a", ins, xnT, (ins["a_wT"], ins["a_wv"]), ins["a_rows"], ins["a_table"], ins["a_base"],
                       ins["a_bins"], ins["a_bins_base"], ins["a_vbase"], trips, heads)
        norm_stage(nc, "n1", ident, ins["x"], xnT, attn=(heads, ins["a_projT"], ins["a_bias"]), x1_d=x1, xn_d=xn, gate=ins["gateT"], scores=scores)
        mixture("f", x1, x2)
        norm_stage(nc, "n2", ident, x2, xnT)
        window_stage(nc, "b", ins, x2, xnT, ins["b_wqT"], ins["b_wkT"], ins["b_wvT"], ins["b_woT"], ins["b_gamma"], ins["b_bias"], x3)
        norm_stage(nc, "n3", ident, x3, xnT, xn_d=xn, gate=ins["gateT"], scores=scores)
        mixture("g", x3, out)



def constants():
    p = np.arange(P)
    f = np.float32
    row_scale, row_shift = np.zeros((P, 4), f), np.zeros((P, 4), f)
    for h in range(HG):
        o = 32 * h
        row_scale[o:o + AD + 2, 0] = A_SCALE
        row_shift[o + AD + 2:o + AD + 4, 0] = 1
        row_scale[o:o + AD, 1] = 1
        row_scale[o + AD + 2:o + AD + 4, 1] = A_SCALE
    spread = np.zeros((P, 2, 2, 2, P), f)
    for h in range(2):
        for j in range(3):
            o = 64 * h + A_ROWS * j
            for i in range(2):
                row_scale[o:o + AD, 2 + i] = 1
                row_scale[o + AD + 2 + i, 2 + i] = 1
                row_shift[o + AD + i, 2 + i] = STACKED[1][j] == 0
            for d in range(2):
                for pair in range(2):
                    for r in range(A_ROWS):
                        spread[32 * (2 * pair + h) + r, d, pair, STACKED[d][j], o + r] = 1
    m = np.arange(NT * B)
    slopes = np.array([2.0 ** (-8.0 / BH * (h + 1)) for h in range(BH)], f)
    dist = np.arange(2 * P)[None] - P - p[:, None]
    masked = (dist > 0) | (dist < -WINDOW)
    b_bias = np.where(masked[:, None], f(-1e9 / B_SCALE), slopes[None, :, None] * dist[:, None].astype(f) / f(B_SCALE))
    same = p[:, None] % E == p[None] % E
    return {
        "ident": np.eye(P, dtype=f),
        "lower": (p[None] < p[:, None]).astype(f),
        "upper": (p[None] > p[:, None]).astype(f),
        "row_scale": row_scale,
        "row_shift": row_shift,
        "spread": spread,
        "same": same.astype(f),
        "before": (same & (p[:, None] // E < p[None] // E)).astype(f),
        "iota": np.tile(p.astype(f), (P, 1)),
        "token": ((m % B) * T + (m // B) * P + p[:, None]).astype(f),
        "b_bias": b_bias.astype(f),
    }


def by_chunk(w):
    return np.ascontiguousarray(w.T.reshape(w.shape[1] // P, P, w.shape[0]).transpose(1, 0, 2))


def relative_layout(w_qkv, q_table, k_table, v_table):
    wT = np.zeros((P, 2, NG, KC, P), w_qkv.dtype)
    rows = np.zeros((P, 2, NG, C), w_qkv.dtype)
    table = np.zeros((P, 2, NG, HG, XB + 1), k_table.dtype)
    base = np.zeros_like(table)
    bins = np.zeros((P, NG, 2, 64), v_table.dtype)
    bins_base = np.zeros_like(bins)
    last = BUCKETS - 1
    for d, tab in enumerate((k_table, q_table)):
        first_end, low_end, up_end = HALF + 1 + d, (0, last)[d], (last, 0)[d]
        for h in range(AH):
            g, r = h // HG, slice(32 * (h % HG), 32 * (h % HG) + AD)
            w = w_qkv[d * C + h * AD:d * C + (h + 1) * AD]
            rows[r, d, g] = w
            wT[:, d, g, :, r] = w.T.reshape(KC, P, AD).transpose(1, 0, 2)
            table[r, d, g, h % HG, 1:XB] = tab[h]
            base[r, d, g, h % HG, 1:first_end] = tab[h][:, 0:1]
            base[r, d, g, h % HG, first_end:XB] = tab[h][:, last:]
            table[r, d, g, h % HG, XB] = tab[h][:, low_end]
            base[r, d, g, h % HG, XB] = tab[h][:, up_end]
    for h in range(AH):
        g, r, x, c = h // HG, h % HG // 2, XB * (h % 2), slice(32 * (h % 2), 32 * (h % 2) + AD)
        bins[x, g, r, c] = v_table[h, 0]
        bins[x + 1:x + XB, g, r, c] = v_table[h]
        bins_base[x + 1:x + 1 + HALF, g, r, c] = v_table[h, 0]
        bins_base[x + 1 + HALF:x + XB, g, r, c] = v_table[h, last]
        bins_base[x, g, r, c] = v_table[h, last]
    ends = np.stack([v_table[:, 0].reshape(C), v_table[:, last].reshape(C)])
    return {
        "a_wT": wT, "a_wv": by_chunk(w_qkv[2 * C:]), "a_rows": rows, "a_table": table, "a_base": base,
        "a_bins": bins, "a_bins_base": bins_base, "a_vbase": np.tile(ends, (P, 1, 1)),
    }


def kernel(L0_attn_a_x, L0_attn_a_w_qkv, L0_attn_a_w_proj, L0_attn_a_b_proj, L0_attn_a_rpe_q_table, L0_attn_a_rpe_k_table,
           L0_attn_a_rpe_v_table, L0_attn_b_wq, L0_attn_b_wk, L0_attn_b_wv, L0_attn_b_wo, L0_attn_b_q_gamma, L0_attn_b_k_gamma,
           L0_ffn_gate_w, L0_ffn_Wg, L0_ffn_Wu, L0_ffn_Wd, L0_ffn_Sg, L0_ffn_Su, L0_ffn_Sd):
    import concourse.bacc as bacc
    from concourse.bass_utils import run_bass_kernel_spmd

    a = np.asarray
    arrays = {
        "x": a(L0_attn_a_x),
        "a_projT": by_chunk(a(L0_attn_a_w_proj)),
        "a_bias": np.tile(a(L0_attn_a_b_proj), (P, 1)),
        "b_wqT": by_chunk(a(L0_attn_b_wq)),
        "b_wkT": by_chunk(a(L0_attn_b_wk)),
        "b_wvT": by_chunk(a(L0_attn_b_wv)),
        "b_woT": by_chunk(a(L0_attn_b_wo)),
        "b_gamma": np.tile(np.stack([a(L0_attn_b_q_gamma), a(L0_attn_b_k_gamma)]), (P, 1, 1)),
        "gateT": by_chunk(a(L0_ffn_gate_w)),
        "WgT": np.stack([by_chunk(w) for w in a(L0_ffn_Wg)]),
        "WuT": np.stack([by_chunk(w) for w in a(L0_ffn_Wu)]),
        "WdT": np.stack([by_chunk(w) for w in a(L0_ffn_Wd)]),
        "SgT": by_chunk(a(L0_ffn_Sg)),
        "SuT": by_chunk(a(L0_ffn_Su)),
        "SdT": by_chunk(a(L0_ffn_Sd)),
        **relative_layout(a(L0_attn_a_w_qkv), a(L0_attn_a_rpe_q_table), a(L0_attn_a_rpe_k_table), a(L0_attn_a_rpe_v_table)),
        **constants(),
    }
    nc = bacc.Bacc("TRN2", target_bir_lowering=False, num_devices=1)
    ins = {name: nc.dram_tensor(f"in_{name}", x.shape, mybir.dt.from_np(x.dtype), kind="ExternalInput").ap() for name, x in arrays.items()}
    out = nc.dram_tensor("out", (B, T, C), F32, kind="ExternalOutput").ap()
    hybrid_block(nc, ins, out)
    result = run_bass_kernel_spmd(nc, [{f"in_{name}": np.ascontiguousarray(x) for name, x in arrays.items()}], core_ids=[0])
    return result.results[0]["out"]
```

```python
from contextlib import ExitStack, contextmanager

import numpy as np

import concourse.bass as bass
from concourse import mybir

F32 = mybir.dt.float32
F32R = mybir.dt.float32r
I32 = mybir.dt.int32
ACT = mybir.ActivationFunctionType
ALU = mybir.AluOpType
AX = mybir.AxisListType
ds = bass.ds

P = 128
B, T, C = 8, 512, 256
NT = T // P
KC = C // P
LN_EPS = 1e-5

AH, AD = 16, 16
HG = 4
NG = AH // HG
BUCKETS = 63
HALF = BUCKETS // 2
XB = BUCKETS + 1
WIN = 192
A_SCALE = AD ** -0.5
A_ROWS = AD + 4
STACKED = ((0, 0, 1), (0, 1, 0))
HIGH_BITS = -(1 << 12)

BH, BD = 16, 64
BC = BH * BD
WINDOW = 128
RMS_EPS = 1e-6
B_SCALE = BD ** -0.5

E = 16
CAP = B * T * 2 // E
CT = CAP // P
I_E = 4 * C
I_S = 2 * C


class Chain:

    def __init__(self, engine, sem, start=0):
        self.engine, self.sem, self.start, self.n = engine, sem, start, 0

    def link(self, instruction):
        instruction.then_inc(self.sem, 1)
        self.n += 1
        self.engine.wait_ge(self.sem, self.start + self.n)

    def mark(self, instruction):
        instruction.then_inc(self.sem, 1)
        self.n += 1

    def settle(self):
        self.engine.wait_ge(self.sem, self.start + self.n)


def hold(engine, sem, value, held):
    engine.wait_ge(sem, value)
    engine.sem_inc(held, 1)


class Store:

    def __init__(self, nc, ctx, tag):
        self.nc, self.ctx, self.tag = nc, ctx, tag
        self.sems = []

    def sb(self, name, shape, dt=F32):
        return self.ctx.enter_context(self.nc.sbuf_tensor(f"{self.tag}_{name}", shape, dt))

    def ps(self, name, shape):
        return self.ctx.enter_context(self.nc.psum_tensor(f"{self.tag}_{name}", shape, F32))

    def sem(self, name):
        self.sems.append(self.ctx.enter_context(self.nc.semaphore(f"{self.tag}_{name}")))
        return self.sems[-1]

    @contextmanager
    def programs(self):
        with self.nc.Block() as block:
            yield block
        with self.nc.Block() as ending:
            @ending.gpsimd
            def _(pool):
                numbers = sorted(sem.num for sem in self.sems)
                starts = [n for n in numbers if n - 1 not in numbers]
                ends = [n for n in numbers if n + 1 not in numbers]
                for start, end in zip(starts, ends):
                    pool.sem_clear(range(start, end + 1))


def by_token(dram, n):
    return dram[ds(n, 1)].rearrange("a (t p) c -> p (a t) c", p=P)


def by_channel(dram, n):
    return dram[ds(n, 1)].rearrange("a p k t -> p (a k) t")


def norm_stage(nc, tag, ident_d, x_d, xnT_d, attn=None, x1_d=None, xn_d=None, gate=None, scores=None):
    with ExitStack() as ctx:
        s = Store(nc, ctx, tag)
        ident = s.sb("ident", [P, P])
        x = s.sb("x", [P, 2, NT, C])
        xn = s.sb("xn", [P, 2, NT, C])
        xnT = s.sb("xnT", [P, 2, KC, T])
        stats = s.sb("stats", [P, NT, 6])
        mv = s.sb("mv", [P, NT, 2])
        var = s.sb("var", [P, NT, 1])
        minus_half = s.sb("minus_half", [P, NT, 1])
        rstd = s.sb("rstd", [P, NT, 1])
        ps_xT = [s.ps(f"ps_xT{k}", [P, T]) for k in range(KC)]
        const_in = s.sem("const_in")
        x_in = [s.sem(f"x_in{p}") for p in range(2)]
        chain = s.sem("chain")
        held = s.sem("held")
        half_set = s.sem("half_set")
        mv_ready = s.sem("mv_ready")
        rstd_ready = s.sem("rstd_ready")
        xn_ready = s.sem("xn_ready")
        xT_ready = s.sem("xT_ready")
        xnT_ready = s.sem("xnT_ready")
        rows_out = [s.sem(f"rows_out{p}") for p in range(2)]
        xnT_out = [s.sem(f"xnT_out{p}") for p in range(2)]
        n_const, n_rows, n_load = 1, 0, 1
        if xn_d is not None:
            n_rows += 1
        if attn:
            o_d, wT_d, bias_d = attn
            n_const += 2
            n_rows += 1
            n_load += 1
            o = s.sb("o", [P, 2, NT, C])
            oT = s.sb("oT", [P, KC, T])
            wT = s.sb("wT", [P, KC, C])
            bias = s.sb("bias", [P, C])
            ps_oT = [s.ps(f"ps_oT{k}", [P, T]) for k in range(KC)]
            ps_y = [s.ps(f"ps_y{k}", [P, T]) for k in range(2)]
            oT_ready = s.sem("oT_ready")
            oT_copied = s.sem("oT_copied")
            y_ready = s.sem("y_ready")
            y_taken = s.sem("y_taken")
        if gate is not None:
            n_const += 1
            gwT = s.sb("gwT", [P, KC, E])
            sm = s.sb("sm", [P, NT, E])
            mx = s.sb("mx", [P, NT, 1])
            total = s.sb("total", [P, NT, 1])
            ps_l = s.ps("ps_l", [P, NT, E])
            logits_ready = s.sem("logits_ready")
            shifted = s.sem("shifted")
            exped = s.sem("exped")
        block = ctx.enter_context(s.programs())

        @block.sync
        def _(sp):
            sp.dma_start(ident[:, :], ident_d).then_inc(const_in, 16)
            if attn:
                sp.dma_start(wT[:, :, :], wT_d).then_inc(const_in, 16)
                sp.dma_start(bias[:, :], bias_d).then_inc(const_in, 16)
            if gate is not None:
                sp.dma_start(gwT[:, :, :], gate).then_inc(const_in, 16)

            def load(n, p):
                sp.dma_start(x[:, p, :, :], by_token(x_d, n)).then_inc(x_in[p], 16)
                if attn:
                    sp.dma_start(o[:, p, :, :], by_token(o_d, n)).then_inc(x_in[p], 16)

            def rows(i, p):
                sp.wait_ge(xn_ready, 2 * i + p + 1)
                if xn_d is not None:
                    sp.dma_start(by_token(xn_d, 2 * i + p), xn[:, p, :, :]).then_inc(rows_out[p], 16)
                if attn:
                    sp.dma_start(by_token(x1_d, 2 * i + p), x[:, p, :, :]).then_inc(rows_out[p], 16)

            def transposed(i, p):
                n = 2 * i + p
                sp.wait_ge(xnT_ready, KC * n + 2 * KC)
                sp.dma_start(by_channel(xnT_d, n), xnT[:, p, :, :]).then_inc(xnT_out[p], 16)

            def reload(i, p):
                if attn:
                    sp.wait_ge(rows_out[p], 16 * n_rows * i + 32 * n_rows)
                load(2 * i + p + 2, p)

            for p in range(2):
                sp.sem_inc(rows_out[p], 16 * max(n_rows, 1))
                sp.sem_inc(xnT_out[p], 16)
            load(0, 0)
            load(1, 1)
            rows(0, 0)
            reload(0, 0)
            with nc.sync.Fori(0, B // 2 - 2) as i:
                rows(i, 1)
                transposed(i, 0)
                reload(i, 1)
                rows(i + 1, 0)
                transposed(i, 1)
                reload(i + 1, 0)
            rows(B // 2 - 2, 1)
            transposed(B // 2 - 2, 0)
            reload(B // 2 - 2, 1)
            rows(B // 2 - 1, 0)
            transposed(B // 2 - 2, 1)
            rows(B // 2 - 1, 1)
            transposed(B // 2 - 1, 0)
            transposed(B // 2 - 1, 1)
            for p in range(2):
                sp.wait_ge(xnT_out[p], 16 * (B // 2 + 1))
                if n_rows:
                    sp.wait_ge(rows_out[p], 16 * n_rows * (B // 2 + 1))

        @block.tensor
        def _(pe):
            pe.wait_ge(const_in, 16 * n_const)

            def first(i, p):
                n = 2 * i + p
                if not attn:
                    return
                pe.wait_ge(x_in[p], 16 * n_load * i + 16 * n_load)
                for k in range(KC):
                    for t in range(NT):
                        last = nc.tensor.transpose(ps_oT[k][:, t * P:(t + 1) * P], o[:, p, t, k * P:(k + 1) * P], ident[:, :])
                    last.then_inc(oT_ready, 1)
                pe.wait_ge(oT_copied, KC * n + KC)
                pe.wait_ge(y_taken, n + 1)
                for t in range(NT):
                    for k in range(KC):
                        last = nc.tensor.matmul(ps_y[t // 2][:, (t % 2) * C:(t % 2 + 1) * C], oT[:, k, t * P:(t + 1) * P], wT[:, k, :],
                                                start=(k == 0), stop=(k == KC - 1))
                    if t % 2:
                        last.then_inc(y_ready, 1)

            def transpose(i, p):
                n = 2 * i + p
                pe.wait_ge(xn_ready, n + 1)
                pe.wait_ge(xnT_ready, KC * n + KC)
                for k in range(KC):
                    for t in range(NT):
                        last = nc.tensor.transpose(ps_xT[k][:, t * P:(t + 1) * P], xn[:, p, t, k * P:(k + 1) * P], ident[:, :])
                    last.then_inc(xT_ready, 1)

            def logits(i, p):
                n = 2 * i + p
                if gate is None:
                    return
                pe.wait_ge(xnT_ready, KC * n + 2 * KC)
                pe.wait_ge(shifted, n + 1)
                for t in range(NT):
                    for k in range(KC):
                        last = nc.tensor.matmul(ps_l[:, t, :], xnT[:, p, k, t * P:(t + 1) * P], gwT[:, k, :],
                                                start=(k == 0), stop=(k == KC - 1))
                last.then_inc(logits_ready, 1)

            first(0, 0)
            with nc.tensor.Fori(0, B // 2 - 1) as i:
                for p in range(2):
                    transpose(i, p)
                    first(i + p, 1 - p)
                    logits(i, p)
            transpose(B // 2 - 1, 0)
            first(B // 2 - 1, 1)
            logits(B // 2 - 1, 0)
            transpose(B // 2 - 1, 1)
            logits(B // 2 - 1, 1)

        @block.scalar
        def _(act):
            act.sem_inc(xnT_ready, KC)

            def first(i, p):
                n = 2 * i + p
                if attn:
                    for k in range(KC):
                        act.wait_ge(oT_ready, KC * n + k + 1)
                        nc.scalar.copy(oT[:, k, :], ps_oT[k][:, :]).then_inc(oT_copied, 1)

            def copy(i, p):
                n = 2 * i + p
                act.wait_ge(xnT_out[p], 16 * i + 16)
                for k in range(KC):
                    act.wait_ge(xT_ready, KC * n + k + 1)
                    nc.scalar.copy(xnT[:, p, k, :], ps_xT[k][:, :]).then_inc(xnT_ready, 1)

            def exp(i, p):
                if gate is not None:
                    act.wait_ge(shifted, 2 * i + p + 2)
                    nc.scalar.activation(sm[:, :, :], sm[:, :, :], ACT.Exp).then_inc(exped, 1)

            first(0, 0)
            with nc.scalar.Fori(0, B // 2 - 1) as i:
                for p in range(2):
                    copy(i, p)
                    first(i + p, 1 - p)
                    exp(i, p)
            copy(B // 2 - 1, 0)
            first(B // 2 - 1, 1)
            exp(B // 2 - 1, 0)
            copy(B // 2 - 1, 1)
            exp(B // 2 - 1, 1)

        @block.gpsimd
        def _(pool):
            nc.gpsimd.memset(minus_half[:, :, :], -0.5).then_inc(half_set, 1)
            pool.wait_ge(half_set, 1)
            with nc.gpsimd.Fori(0, B) as n:
                pool.wait_ge(mv_ready, n + 1)
                nc.gpsimd.tensor_tensor(rstd[:, :, :], var[:, :, :], minus_half[:, :, :], ALU.pow).then_inc(rstd_ready, 1)

        @block.vector
        def _(dve):
            FIRST = 2 * NT + (3 if attn else 0)
            SECOND = 3 if gate is not None else 0
            if attn:
                dve.sem_inc(y_taken, 1)
                dve.wait_ge(const_in, 16 * n_const)
            if gate is not None:
                dve.sem_inc(shifted, 1)

            def first(i, p, ch, start=False):
                n = 2 * i + p
                dve.wait_ge(x_in[p], 16 * n_load * i + 16 * n_load)
                if attn:
                    ch.link(nc.vector.tensor_tensor(x[:, p, :, :], x[:, p, :, :], bias[:, :].unsqueeze(1).to_broadcast([P, NT, C]), ALU.add))
                    for h in range(2):
                        dve.wait_ge(y_ready, 2 * n + h + 1)
                        xh = x[:, p, 2 * h:2 * h + 2, :]
                        ch.mark(nc.vector.tensor_tensor(xh, ps_y[h][:, :].rearrange("p (t c) -> p t c", c=C), xh, ALU.add))
                    ch.settle()
                    dve.sem_inc(y_taken, 1)
                for t in range(NT):
                    ch.mark(nc.vector.bn_stats(stats[:, t, :], x[:, p, t, :]))
                ch.settle()
                dve.sem_inc(held, 1)
                for t in range(NT):
                    ch.mark(nc.vector.bn_aggr(mv[:, t, :], stats[:, t, :]))
                ch.settle()
                nc.vector.tensor_scalar(var[:, :, :], mv[:, :, 1:2], LN_EPS, None, ALU.add).then_inc(mv_ready, 1)
                dve.wait_ge(rstd_ready, n + 1)
                if n_rows:
                    dve.wait_ge(rows_out[p], 16 * n_rows * i + 16 * n_rows)
                if not start:
                    dve.wait_ge(xnT_ready, KC * n)
                for t in range(NT):
                    last = nc.vector.tensor_scalar(xn[:, p, t, :], x[:, p, t, :], mv[:, t, 0:1], rstd[:, t, :], ALU.subtract, ALU.mult)
                last.then_inc(xn_ready, 1)

            def second(i, p, ch):
                n = 2 * i + p
                if gate is None:
                    return
                dve.wait_ge(logits_ready, n + 1)
                ch.link(nc.vector.reduce_max(mx[:, :, :], ps_l[:, :, :], AX.X))
                nc.vector.tensor_tensor(sm[:, :, :], ps_l[:, :, :], mx[:, :, :].to_broadcast([P, NT, E]), ALU.subtract).then_inc(shifted, 1)
                dve.wait_ge(exped, n + 1)
                ch.link(nc.vector.reduce_sum(total[:, :, :], sm[:, :, :], AX.X))
                ch.link(nc.vector.reciprocal(total[:, :, :], total[:, :, :]))
                nc.vector.tensor_tensor(scores[:, :, ds(n, 1), :].rearrange("p t a e -> p (t a) e"), sm[:, :, :],
                                        total[:, :, :].to_broadcast([P, NT, E]), ALU.mult)

            def step(i, p):
                ch = Chain(dve, chain, FIRST + (FIRST + SECOND) * (2 * i + p))
                first(i + p, 1 - p, ch)
                second(i, p, ch)
                assert ch.n == FIRST + SECOND

            first(0, 0, Chain(dve, chain), start=True)
            with nc.vector.Fori(0, B // 2 - 1) as i:
                step(i, 0)
                step(i, 1)
            step(B // 2 - 1, 0)
            second(B // 2 - 1, 1, Chain(dve, chain, FIRST + (FIRST + SECOND) * (B - 1)))


def route_stage(nc, tag, const, scores, st, thr, slot_token, slot_weight):
    with ExitStack() as ctx:
        s = Store(nc, ctx, tag)
        ident = s.sb("ident", [P, P])
        same = s.sb("same", [P, P])
        before = s.sb("before", [P, P])
        iota = s.sb("iota", [P, P])
        token = s.sb("token", [P, NT * B])
        work = s.sb("work", [P, T])
        equal = s.sb("equal", [P, T])
        sel = s.sb("sel", [P, T])
        ones = s.sb("ones", [P, T])
        pos = s.sb("pos", [P, T])
        posi = s.sb("posi", [P, 2, T], I32)
        parts = s.sb("parts", [P, 2, T])
        partsT = s.sb("partsT", [P, 2, NT, P])
        count = s.sb("count", [P, 1])
        need = s.sb("need", [P, 1])
        offset = s.sb("offset", [P, 1])
        hit = s.sb("hit", [P, NT * P, CT])
        part = s.sb("part", [P, 3, NT * B, E])
        value = s.sb("value", [P, 2, NT * B, 3, CT], F32R)
        onehot = s.sb("onehot", [P, 2, NT * B, P], F32R)
        found = s.sb("found", [3 * CT, E, P])
        ps_t = [s.ps(f"ps_t{k}", [P, T]) for k in range(2)]
        ps_c = s.ps("ps_c", [P, 1])
        ps_f = [s.ps(f"ps_f{k}", [3 * CT, P]) for k in range(2)]
        ps_s = s.ps("ps_s", [P, E, 3, CT])
        const_in = s.sem("const_in")
        chain = s.sem("chain")
        counted = s.sem("counted")
        summed = s.sem("summed")
        parts_ready = s.sem("parts_ready")
        parts_T = s.sem("parts_T")
        hot_ready = s.sem("hot_ready")
        found_ready = s.sem("found_ready")
        value_ready = s.sem("value_ready")
        taken = s.sem("taken")
        block = ctx.enter_context(s.programs())

        @block.sync
        def _(sp):
            for tile, dram in ((ident, "ident"), (same, "same"), (before, "before"), (iota, "iota"), (token, "token")):
                sp.dma_start(tile[:, :], const[dram]).then_inc(const_in, 16)

        @block.tensor
        def _(pe):
            pe.wait_ge(const_in, 16 * 5)
            for r in range(3):
                pe.wait_ge(counted, r + 1)
                table = same if r == 0 else before
                nc.tensor.matmul(ps_c[:, :], table[:, :], count[:, :], start=True, stop=True).then_inc(summed, 1)
            pe.wait_ge(parts_ready, 1)
            for k in range(2):
                for t in range(NT):
                    last = nc.tensor.transpose(ps_t[k][:, t * P:(t + 1) * P], parts[:, k, t * P:(t + 1) * P], ident[:, :])
            last.then_inc(parts_T, 1)
            with nc.tensor.Fori(0, E // 2) as i:
                for q in range(2):
                    pe.wait_ge(hot_ready, 2 * i + q + 1)
                    pe.wait_ge(taken, 2 * i + q + 1)
                    for m in range(NT * B):
                        last = nc.tensor.matmul(ps_f[q][:, :], value[:, q, m, :, :].rearrange("p v c -> p (v c)"), onehot[:, q, m, :],
                                                start=(m == 0), stop=(m == NT * B - 1))
                    last.then_inc(found_ready, 1)
            pe.wait_ge(taken, E + 2)
            for e in range(E):
                last = nc.tensor.transpose(ps_s[:, e, :, :].rearrange("p v c -> p (v c)"), found[:, e, :], ident[0:3 * CT, 0:3 * CT])
            last.then_inc(found_ready, 1)

        @block.vector
        def _(dve):
            ch = Chain(dve, chain)
            rounds = [0]

            def total(count_of, op, scalar):
                nc.vector.tensor_scalar(work[:, :], count_of, scalar, None, op, op1=ALU.add, accum_out=count[:, :]).then_inc(counted, 1)
                rounds[0] += 1
                dve.wait_ge(summed, rounds[0])

            nc.vector.memset(ones[:, :], 1.0)
            dve.wait_ge(const_in, 16 * 5)
            total(st[:, :], ALU.is_gt, thr[:, :])
            ch.link(nc.vector.tensor_scalar(need[:, :], ps_c[:, :], -1.0, float(CAP), ALU.mult, ALU.add))
            total(st[:, :], ALU.is_equal, thr[:, :])
            ch.link(nc.vector.tensor_copy(offset[:, :], ps_c[:, :]))
            ch.link(nc.vector.tensor_scalar(equal[:, :], st[:, :], thr[:, :], None, ALU.is_equal))
            ch.link(nc.vector.tensor_tensor_scan(pos[:, :], ones[:, :], equal[:, :], offset[:, :], ALU.mult, ALU.add))
            ch.link(nc.vector.scalar_tensor_tensor(equal[:, :], pos[:, :], need[:, :], equal[:, :], ALU.is_le, ALU.mult))
            ch.link(nc.vector.scalar_tensor_tensor(sel[:, :], st[:, :], thr[:, :], equal[:, :], ALU.is_gt, ALU.add))
            total(sel[:, :], ALU.mult, 1.0)
            ch.link(nc.vector.tensor_copy(offset[:, :], ps_c[:, :]))
            ch.link(nc.vector.tensor_tensor_scan(pos[:, :], ones[:, :], sel[:, :], offset[:, :], ALU.mult, ALU.add))
            ch.link(nc.vector.tensor_tensor(pos[:, :], pos[:, :], sel[:, :], ALU.mult))
            ch.link(nc.vector.tensor_scalar(pos[:, :], pos[:, :], -1.0, None, ALU.add))
            ch.link(nc.vector.tensor_copy(posi[:, 0, :], pos[:, :]))
            ch.link(nc.vector.tensor_single_scalar(posi[:, 1, :], posi[:, 0, :], P - 1, ALU.bitwise_and))
            ch.link(nc.vector.tensor_single_scalar(posi[:, 0, :], posi[:, 0, :], 7, ALU.arith_shift_right))
            nc.vector.tensor_copy(parts[:, :, :], posi[:, :, :]).then_inc(parts_ready, 1)
            dve.wait_ge(parts_T, 1)
            for k in range(2):
                ch.mark(nc.vector.tensor_copy(partsT[:, k, :, :].rearrange("p t r -> p (t r)"), ps_t[k][:, :]))
            ch.settle()
            slot_tile = partsT[:, 0, :, :].rearrange("p t r -> p (t r)")
            ch.link(nc.vector.tensor_tensor(hit[:, :, :], slot_tile.unsqueeze(2).to_broadcast([P, NT * P, CT]),
                                            iota[:, 0:CT].unsqueeze(1).to_broadcast([P, NT * P, CT]), ALU.is_equal))
            sc = scores[:, :, :, :].rearrange("p t b e -> p (t b e)")
            flat = lambda k: part[:, k, :, :].rearrange("p m e -> p (m e)")
            ch.mark(nc.vector.tensor_copy(part[:, 0, :, :], token[:, :].unsqueeze(2).to_broadcast([P, NT * B, E])))
            ch.link(nc.vector.tensor_single_scalar(flat(1).bitcast(I32), sc.bitcast(I32), HIGH_BITS, ALU.bitwise_and))
            ch.link(nc.vector.tensor_tensor(flat(2), sc, flat(1), ALU.subtract))

            def one_hot(e, q):
                low = partsT[:, 1, :, :].rearrange("p t (b e) -> p (t b) e", e=E)[:, :, ds(e, 1)]
                mine = hit[:, :, :].rearrange("p (m e) c -> p m e c", e=E)[:, :, ds(e, 1), :].rearrange("p m a c -> p m (a c)")
                for k in range(3):
                    nc.vector.tensor_tensor(value[:, q, :, k, :], mine, part[:, k, :, ds(e, 1)].to_broadcast([P, NT * B, CT]), ALU.mult).then_inc(value_ready, 1)
                dve.wait_ge(value_ready, 3 * e + 3)
                nc.vector.tensor_tensor(onehot[:, q, :, :], low.to_broadcast([P, NT * B, P]),
                                        iota[:, :].unsqueeze(1).to_broadcast([P, NT * B, P]), ALU.is_equal).then_inc(hot_ready, 1)

            def take(e, q):
                dve.wait_ge(found_ready, e + 1)
                nc.vector.tensor_copy(found[:, ds(e, 1), :].rearrange("p a s -> p (a s)"), ps_f[q][:, :]).then_inc(taken, 1)

            dve.sem_inc(taken, 2)
            one_hot(0, 0)
            one_hot(1, 1)
            with nc.vector.Fori(0, E // 2 - 1) as i:
                for q in range(2):
                    take(2 * i + q, q)
                    one_hot(2 * i + q + 2, q)
            take(E - 2, 0)
            take(E - 1, 1)
            dve.wait_ge(found_ready, E + 1)
            nc.vector.tensor_copy(slot_token[:, :, :], ps_s[:, :, 0, :])
            ch.link(nc.vector.tensor_copy(slot_weight[:, :, :], ps_s[:, :, 1, :]))
            nc.vector.tensor_tensor(slot_weight[:, :, :], slot_weight[:, :, :], ps_s[:, :, 2, :], ALU.add)


BITS = [1 << k for k in range(30, -1, -1)] + [0]


def threshold_dve(nc, dve, ch, n, t, summed, counted):
    st, thr, bits, cand, got, work, count, ps_c = t
    dve.wait_ge(summed, (len(BITS) if n is None else n) + 1)
    ch.link(nc.vector.tensor_scalar(got[:, :], ps_c[:, :], CAP - 0.5, cand[:, :], ALU.is_ge, ALU.mult))
    ch.link(nc.vector.tensor_tensor(thr[:, :], thr[:, :], got[:, :], ALU.max))
    if n is not None:
        ch.link(nc.vector.tensor_tensor(cand[:, :].bitcast(I32), thr[:, :].bitcast(I32), bits[:, ds(n, 1)], ALU.bitwise_or))
        nc.vector.tensor_scalar(work[:, :], st[:, :], cand[:, :], None, ALU.is_ge, op1=ALU.add, accum_out=count[:, :]).then_inc(counted, 1)


def threshold_pe(nc, pe, n, same, count, ps_c, counted, summed):
    pe.wait_ge(counted, n + 1)
    nc.tensor.matmul(ps_c[:, :], same[:, :], count[:, :], start=True, stop=True).then_inc(summed, 1)


def split_piece(nc, ch, masked, x, high, rest):
    ch.link(nc.vector.tensor_single_scalar(masked.bitcast(I32), x.bitcast(I32), HIGH_BITS, ALU.bitwise_and))
    ch.mark(nc.vector.tensor_copy(high, masked))
    ch.mark(nc.vector.tensor_tensor(rest, x, masked, ALU.subtract))
    ch.settle()


def hidden_pe(nc, pe, n, hidden, x, g, u, ps_g, ps_u, gu_ready, h_ready, between=lambda j: None):
    for j in range(hidden):
        q = j % 2
        pe.wait_ge(h_ready, hidden * n + j + 1)
        for ps, w in ((ps_g[q], g), (ps_u[q], u)):
            terms = [(k, a, b) for k in range(KC) for a, b in ((1, 0), (0, 0), (0, 1))]
            for k, a, b in terms:
                last = nc.tensor.matmul(ps[:, :], w[a][:, k, j * P:(j + 1) * P], x[b][:, k, :],
                                        start=((k, a, b) == terms[0]), stop=((k, a, b) == terms[-1]))
        last.then_inc(gu_ready, 1)
        between(j)


def hidden_act(nc, act, n, hidden, ps_g, gelu, gu_ready, h_ready, gelu_ready):
    for j in range(hidden):
        act.wait_ge(gu_ready, hidden * n + j + 1)
        act.wait_ge(h_ready, hidden * n + j + 1)
        nc.scalar.activation(gelu[:, j % 2, :], ps_g[j % 2][:, :], ACT.Gelu).then_inc(gelu_ready, 1)


def hidden_dve(nc, dve, n, hidden, ps_u, gelu, hT, gelu_ready, h_ready, between=lambda j: None):
    for j in range(hidden):
        dve.wait_ge(gelu_ready, hidden * n + j + 1)
        nc.vector.tensor_tensor(hT[:, j, :], gelu[:, j % 2, :], ps_u[j % 2][:, :], ALU.mult).then_inc(h_ready, 1)
        between(j)


def down_pe(nc, pe, n, hidden, hT, dT, ps_d, h_ready, d_ready, d_taken):
    pe.wait_ge(h_ready, hidden * n + hidden + 2)
    for t in range(NT):
        pe.wait_ge(d_taken, NT * n + t + 1)
        for j in range(hidden):
            last = nc.tensor.matmul(ps_d[t % 2][:, :], hT[:, j, t * P:(t + 1) * P], dT[:, j, :], start=(j == 0), stop=(j == hidden - 1))
        last.then_inc(d_ready, 1)


def shared_stage(nc, tag, const, scores, st, thr, xnT_d, x_d, gT_d, uT_d, dT_d, y_d):
    HB = I_S // P
    assert HB * B == len(BITS)
    with ExitStack() as ctx:
        s = Store(nc, ctx, tag)
        gT = s.sb("gT", [P, KC, I_S])
        uT = s.sb("uT", [P, KC, I_S])
        dT = s.sb("dT", [P, HB, C])
        masked = s.sb("masked", [P, T])
        g = [s.sb(f"g_{part}", [P, KC, I_S], F32R) for part in ("high", "rest")]
        u = [s.sb(f"u_{part}", [P, KC, I_S], F32R) for part in ("high", "rest")]
        xT = s.sb("xT", [P, 2, KC, T])
        xs = [s.sb(f"x_{part}", [P, 2, KC, T], F32R) for part in ("high", "rest")]
        x = s.sb("x", [P, 2, NT, C])
        ident = s.sb("ident", [P, P])
        same = s.sb("same", [P, P])
        bits = s.sb("bits", [P, len(BITS)], I32)
        cand = s.sb("cand", [P, 1])
        got = s.sb("got", [P, 1])
        work = s.sb("work", [P, T])
        count = s.sb("count", [P, 1])
        gelu = s.sb("gelu", [P, 2, T])
        hT = s.sb("hT", [P, 2, HB, T])
        ps_g = [s.ps(f"ps_g{q}", [P, T]) for q in range(2)]
        ps_u = [s.ps(f"ps_u{q}", [P, T]) for q in range(2)]
        ps_d = [s.ps(f"ps_d{q}", [P, C]) for q in range(2)]
        ps_t = s.ps("ps_t", [P, T])
        ps_c = s.ps("ps_c", [P, 1])
        search = (st, thr, bits, cand, got, work, count, ps_c)
        table_in = s.sem("table_in")
        st_ready = s.sem("st_ready")
        counted = s.sem("counted")
        summed = s.sem("summed")
        w_in = s.sem("w_in")
        xT_in = [s.sem(f"xT_in{p}") for p in range(2)]
        x_in = [s.sem(f"x_in{p}") for p in range(2)]
        chain = s.sem("chain")
        held = s.sem("held")
        w_split = s.sem("w_split")
        x_split = s.sem("x_split")
        gu_ready = s.sem("gu_ready")
        gelu_ready = s.sem("gelu_ready")
        h_ready = s.sem("h_ready")
        d_ready = s.sem("d_ready")
        d_taken = s.sem("d_taken")
        y_out = [s.sem(f"y_out{p}") for p in range(2)]
        block = ctx.enter_context(s.programs())

        @block.sync
        def _(sp):
            def load(n, p):
                sp.dma_start(xT[:, p, :, :], by_channel(xnT_d, n)).then_inc(xT_in[p], 16)
                sp.dma_start(x[:, p, :, :], by_token(x_d, n)).then_inc(x_in[p], 16)

            for tile, name in ((ident, "ident"), (same, "same"), (bits, "bits")):
                sp.dma_start(tile[:, :], const[name]).then_inc(table_in, 16)
            sp.dma_start(gT[:, :, :], gT_d).then_inc(w_in, 16)
            sp.dma_start(uT[:, :, :], uT_d).then_inc(w_in, 16)
            load(0, 0)
            load(1, 1)
            sp.dma_start(dT[:, :, :], dT_d).then_inc(w_in, 16)

            def store(i, p, more):
                n = 2 * i + p
                sp.wait_ge(d_taken, NT * n + NT + 2)
                sp.dma_start(by_token(y_d, n), x[:, p, :, :]).then_inc(y_out[p], 16)
                if more:
                    sp.wait_ge(y_out[p], 16 * i + 16)
                    load(n + 2, p)

            with nc.sync.Fori(0, B // 2 - 1) as i:
                store(i, 0, True)
                store(i, 1, True)
            store(B // 2 - 1, 0, False)
            store(B // 2 - 1, 1, False)
            for p in range(2):
                sp.wait_ge(y_out[p], 16 * (B // 2))

        @block.tensor
        def _(pe):
            pe.wait_ge(table_in, 16 * 3)
            for t in range(NT):
                last = nc.tensor.transpose(ps_t[:, t * P:(t + 1) * P], scores[:, t, :, :].rearrange("p b e -> p (b e)"), ident[:, :])
            last.then_inc(st_ready, 1)
            pe.wait_ge(w_in, 16 * 3)
            pe.wait_ge(w_split, 1)
            with nc.tensor.Fori(0, B // 2) as i:
                for p in range(2):
                    pe.wait_ge(x_split, 2 * i + p + 1)
                    hidden_pe(nc, pe, 2 * i + p, HB, [x_[:, p, :, :] for x_ in xs], g, u, ps_g, ps_u, gu_ready, h_ready,
                              lambda j: threshold_pe(nc, pe, HB * (2 * i + p) + j, same, count, ps_c, counted, summed))
                    down_pe(nc, pe, 2 * i + p, HB, hT[:, p, :, :], dT, ps_d, h_ready, d_ready, d_taken)

            threshold_pe(nc, pe, len(BITS), same, count, ps_c, counted, summed)

        @block.scalar
        def _(act):
            with nc.scalar.Fori(0, B) as n:
                hidden_act(nc, act, n, HB, ps_g, gelu, gu_ready, h_ready, gelu_ready)

        @block.vector
        def _(dve):
            dve.sem_inc(h_ready, 2)
            dve.sem_inc(d_taken, 2)
            LINKS = 3 * KC + 3 * HB

            def split_x(ch, i, p):
                hold(dve, xT_in[p], 16 * i + 16, held)
                for k in range(KC):
                    split_piece(nc, ch, masked[:, :], xT[:, p, k, :], *[part[:, p, k, :] for part in xs])
                dve.sem_inc(x_split, 1)

            ch = Chain(dve, chain)
            ch.mark(nc.vector.memset(thr[:, :], 0.0))
            ch.mark(nc.vector.memset(cand[:, :], 0.0))
            dve.wait_ge(table_in, 16 * 3)
            dve.wait_ge(st_ready, 1)
            ch.link(nc.vector.tensor_copy(st[:, :], ps_t[:, :]))
            nc.vector.tensor_scalar(work[:, :], st[:, :], cand[:, :], None, ALU.is_ge, op1=ALU.add, accum_out=count[:, :]).then_inc(counted, 1)
            dve.wait_ge(w_in, 16 * 3)
            for w, parts in ((gT, g), (uT, u)):
                for k in range(KC):
                    split_piece(nc, ch, masked[:, :], w[:, k, :], *[part[:, k, :] for part in parts])
            dve.sem_inc(w_split, 1)
            SETUP = ch.n
            split_x(ch, 0, 0)

            def step(i, p, more):
                n = 2 * i + p
                ch = Chain(dve, chain, LINKS * n + SETUP + 3 * KC)
                hidden_dve(nc, dve, n, HB, ps_u, gelu, hT[:, p, :, :], gelu_ready, h_ready,
                           lambda j: threshold_dve(nc, dve, ch, HB * n + j, search, summed, counted))
                if more:
                    split_x(ch, i + p, 1 - p)
                dve.wait_ge(x_in[p], 16 * i + 16)
                for t in range(NT):
                    dve.wait_ge(d_ready, NT * n + t + 1)
                    nc.vector.tensor_tensor(x[:, p, t, :], x[:, p, t, :], ps_d[t % 2][:, :], ALU.add).then_inc(d_taken, 1)

            with nc.vector.Fori(0, B // 2 - 1) as i:
                step(i, 0, True)
                step(i, 1, True)
            step(B // 2 - 1, 0, True)
            step(B // 2 - 1, 1, False)
            threshold_dve(nc, dve, Chain(dve, chain, LINKS * B + SETUP), None, search, summed, counted)


def expert_stage(nc, tag, ident_d, xn_d, slot_token, slot_weight, gT_d, uT_d, dT_d, y_d):
    HB = I_E // P
    DONE = 16 * CT
    rows_xn = xn_d.rearrange("b t c -> (b t) c")
    rows_y = y_d.rearrange("b t c -> (b t) c")
    with ExitStack() as ctx:
        s = Store(nc, ctx, tag)
        ident = s.sb("ident", [P, P])
        gT = s.sb("gT", [P, 2, KC, I_E])
        uT = s.sb("uT", [P, 2, KC, I_E])
        dT = s.sb("dT", [P, 2, HB, C])
        masked = s.sb("masked", [P, T])
        g = [s.sb(f"g_{part}", [P, 2, KC, I_E], F32R) for part in ("high", "rest")]
        u = [s.sb(f"u_{part}", [P, 2, KC, I_E], F32R) for part in ("high", "rest")]
        index = s.sb("index", [P, 2, CT], I32)
        xg = s.sb("xg", [P, 2, CT, C])
        xT = s.sb("xT", [P, 2, KC, T])
        xs = [s.sb(f"x_{part}", [P, 2, KC, T], F32R) for part in ("high", "rest")]
        gelu = s.sb("gelu", [P, 2, T])
        hT = s.sb("hT", [P, HB, T])
        eo = s.sb("eo", [P, 2, CT, C])
        ps_x = [s.ps(f"ps_x{k}", [P, T]) for k in range(KC)]
        ps_g = [s.ps(f"ps_g{q}", [P, T]) for q in range(2)]
        ps_u = [s.ps(f"ps_u{q}", [P, T]) for q in range(2)]
        ps_d = [s.ps(f"ps_d{q}", [P, C]) for q in range(2)]
        ident_in = s.sem("ident_in")
        up_in = [s.sem(f"up_in{q}") for q in range(2)]
        down_in = [s.sem(f"down_in{q}") for q in range(2)]
        held = s.sem("held")
        chain = s.sem("chain")
        w_split = s.sem("w_split")
        x_split = s.sem("x_split")
        index_ready = s.sem("index_ready")
        gathered = [s.sem(f"gathered{q}") for q in range(2)]
        x_T = s.sem("x_T")
        xT_ready = s.sem("xT_ready")
        gu_ready = s.sem("gu_ready")
        gelu_ready = s.sem("gelu_ready")
        h_ready = s.sem("h_ready")
        d_ready = s.sem("d_ready")
        d_taken = s.sem("d_taken")
        added = [s.sem(f"added{q}") for q in range(2)]
        block = ctx.enter_context(s.programs())

        @block.sync
        def _(sp):
            sp.dma_start(ident[:, :], ident_d).then_inc(ident_in, 16)

            def load_up(e, q):
                sp.dma_start(gT[:, q, :, :], gT_d[ds(e, 1)].rearrange("a p k i -> p (a k) i")).then_inc(up_in[q], 16)
                sp.dma_start(uT[:, q, :, :], uT_d[ds(e, 1)].rearrange("a p k i -> p (a k) i")).then_inc(up_in[q], 16)

            def load_down(e, q):
                sp.dma_start(dT[:, q, :, :], dT_d[ds(e, 1)].rearrange("a p k i -> p (a k) i")).then_inc(down_in[q], 16)

            def step(i, q, up=True):
                e = 2 * i + q
                if up:
                    sp.wait_ge(w_split, e + 2)
                    load_up(e + 3, 1 - q)
                sp.wait_ge(d_ready, CT * e + CT)
                load_down(e + 2, q)

            load_up(0, 0)
            load_up(1, 1)
            load_down(0, 0)
            load_down(1, 1)
            sp.wait_ge(w_split, 1)
            load_up(2, 0)
            with nc.sync.Fori(0, E // 2 - 2) as i:
                step(i, 0)
                step(i, 1)
            step(E // 2 - 2, 0)
            step(E // 2 - 2, 1, up=False)

        @block.gpsimd
        def _(pool):
            def gather(e, q):
                nc.gpsimd.tensor_copy(index[:, q, :], slot_token[:, ds(e, 1), :].rearrange("p a c -> p (a c)")).then_inc(index_ready, 1)
                hold(pool, index_ready, e + 1, held)
                for t in range(CT):
                    nc.gpsimd.indirect_dma_start(xg[:, q, t, :], None, rows_xn, bass.IndirectOffsetOnAxis(index[:, q, t:t + 1], 0),
                                                 bounds_check=B * T - 1).then_inc(gathered[q], 16)

            def step(i, q, more, first=False):
                e = 2 * i + q
                if not first or q:
                    hold(pool, added[1 - q], DONE * (i + q), held)
                if more:
                    hold(pool, x_T, KC * e + KC, held)
                    gather(e + 1, 1 - q)
                for t in range(CT):
                    hold(pool, d_taken, CT * e + t + 3, held)
                    nc.gpsimd.indirect_dma_start(rows_y, bass.IndirectOffsetOnAxis(index[:, q, t:t + 1], 0), eo[:, q, t, :], None,
                                                 bounds_check=B * T - 1, compute_op=ALU.add).then_inc(added[q], 16)

            gather(0, 0)
            step(0, 0, True, first=True)
            step(0, 1, True, first=True)
            with nc.gpsimd.Fori(1, E // 2 - 1) as i:
                step(i, 0, True)
                step(i, 1, True)
            step(E // 2 - 1, 0, True)
            step(E // 2 - 1, 1, False)
            for q in range(2):
                pool.wait_ge(added[q], DONE * (E // 2))

        @block.tensor
        def _(pe):
            def transpose_rows(i, q, e):
                pe.wait_ge(gathered[q], DONE * i + DONE)
                for k in range(KC):
                    for t in range(CT):
                        last = nc.tensor.transpose(ps_x[k][:, t * P:(t + 1) * P], xg[:, q, t, k * P:(k + 1) * P], ident[:, :])
                    last.then_inc(x_T, 1)

            def step(i, q, more):
                e = 2 * i + q
                pe.wait_ge(w_split, e + 1)
                pe.wait_ge(x_split, e + 1)
                hidden_pe(nc, pe, e, HB, *[[part[:, q, :, :] for part in parts] for parts in (xs, g, u)], ps_g, ps_u, gu_ready, h_ready)
                if more:
                    transpose_rows(i + q, 1 - q, e + 1)
                pe.wait_ge(down_in[q], 16 * i + 16)
                down_pe(nc, pe, e, HB, hT, dT[:, q, :, :], ps_d, h_ready, d_ready, d_taken)

            pe.sem_inc(x_T, KC)
            pe.wait_ge(ident_in, 16)
            transpose_rows(0, 0, 0)
            with nc.tensor.Fori(0, E // 2 - 1) as i:
                step(i, 0, True)
                step(i, 1, True)
            step(E // 2 - 1, 0, True)
            step(E // 2 - 1, 1, False)

        @block.scalar
        def _(act):
            def copy_rows(e, q):
                for k in range(KC):
                    act.wait_ge(x_T, KC * e + k + 1 + KC)
                    nc.scalar.copy(xT[:, q, k, :], ps_x[k][:, :]).then_inc(xT_ready, 1)

            def step(i, q, more):
                hidden_act(nc, act, 2 * i + q, HB, ps_g, gelu, gu_ready, h_ready, gelu_ready)
                if more:
                    copy_rows(2 * i + q + 1, 1 - q)

            copy_rows(0, 0)
            with nc.scalar.Fori(0, E // 2 - 1) as i:
                step(i, 0, True)
                step(i, 1, True)
            step(E // 2 - 1, 0, True)
            step(E // 2 - 1, 1, False)

        @block.vector
        def _(dve):
            dve.sem_inc(h_ready, 2)
            dve.sem_inc(d_taken, 2)

            PIECES = [(w, parts, k, slice(i, i + T)) for w, parts in ((gT, g), (uT, u)) for k in range(KC) for i in range(0, I_E, T)]
            LINKS = 3 * (len(PIECES) + KC)

            def split_w(ch, i, q, j):
                if j >= len(PIECES):
                    return
                if j == 0:
                    hold(dve, up_in[q], 32 * i + 32, held)
                w, parts, k, columns = PIECES[j]
                split_piece(nc, ch, masked[:, :], w[:, q, k, columns], *[part[:, q, k, columns] for part in parts])
                if j == len(PIECES) - 1:
                    dve.sem_inc(w_split, 1)

            def split_x(ch, e, q):
                hold(dve, xT_ready, KC * e + KC, held)
                for k in range(KC):
                    split_piece(nc, ch, masked[:, :], xT[:, q, k, :], *[part[:, q, k, :] for part in xs])
                dve.sem_inc(x_split, 1)

            def step(i, q, first=False, more=True):
                e = 2 * i + q
                ch = Chain(dve, chain, LINKS * e + LINKS)
                hidden_dve(nc, dve, e, HB, ps_u, gelu, hT, gelu_ready, h_ready, (lambda j: split_w(ch, i + q, 1 - q, j)) if more else (lambda j: None))
                if more:
                    split_x(ch, e + 1, 1 - q)
                if not first:
                    dve.wait_ge(added[q], DONE * i)
                for t in range(CT):
                    dve.wait_ge(d_ready, CT * e + t + 1)
                    nc.vector.tensor_tensor(eo[:, q, t, :], ps_d[t % 2][:, :],
                                            slot_weight[:, ds(e, 1), t:t + 1].rearrange("p a c -> p (a c)").to_broadcast([P, C]),
                                            ALU.mult).then_inc(d_taken, 1)

            ch = Chain(dve, chain)
            for j in range(len(PIECES)):
                split_w(ch, 0, 0, j)
            split_x(ch, 0, 0)
            step(0, 0, first=True)
            step(0, 1, first=True)
            with nc.vector.Fori(1, E // 2 - 1) as i:
                step(i, 0)
                step(i, 1)
            step(E // 2 - 1, 0)
            step(E // 2 - 1, 1, more=False)


def scores_later(order, lags):
    out = [x for x in order if x[0] != "scores"]
    for k, lag in enumerate(lags):
        place = sum(x[0] != "scores" for x in order[:order.index(("scores", k))]) + lag
        out.insert(min(place, len(order) - len(lags)) + k, ("scores", k))
    return out


WINDOW_ORDER = [
    ("out_T", 0), ("scores", 0), ("out_T", 1), ("scores", 1), ("out", 0), ("probs_T", 0), ("probs_T", 1), ("q", 0),
    ("scores", 2), ("q", 1), ("values", 0), ("probs_T", 2), ("values", 1), ("probs_T", 3), ("k", 0),
    ("scores", 3), ("k", 1), ("values", 2), ("probs_T", 4), ("v", 0), ("values", 3), ("q_T", 0), ("probs_T", 5),
    ("q_T", 1), ("values", 4), ("probs_T", 6), ("values", 5), ("k_T", 0), ("probs_T", 7), ("values", 6), ("k_T", 1),
    ("values", 7), ("v", 1),
]
WINDOW_SCALAR_ORDER = scores_later(WINDOW_ORDER, (1, 4, 4, 6))
NEXT = ("q", "k", "v", "q_T", "k_T")
PAST = ("out_T", "out")


def window_stage(nc, tag, const, x_d, xnT_d, wqT_d, wkT_d, wvT_d, woT_d, gamma_d, bias_d, y_d):
    CH = BC // P
    HALVES = 2
    HW = BC // HALVES
    with ExitStack() as ctx:
        s = Store(nc, ctx, tag)
        ident = s.sb("ident", [P, P])
        wT = {kind: [s.sb(f"w{kind}_{part}", [P, KC, BC], F32R) for part in ("high", "rest")] for kind in ("q", "k", "v")}
        woT = s.sb("woT", [P, CH, C])
        gamma = s.sb("gamma", [P, 2, BC])
        bias = s.sb("bias", [P, BH, 2 * P])
        minus_half = s.sb("minus_half", [P, 2])
        xT = s.sb("xT", [P, 2, KC, P])
        xs = [s.sb(f"x_{part}", [P, 2, KC, P], F32R) for part in ("high", "rest")]
        masked = s.sb("masked", [P, HW])
        x = s.sb("x", [P, 2, C])
        raw = s.sb("raw", [P, 2, BC])
        square = s.sb("square", [P, HW])
        ss = s.sb("ss", [P, 2, HALVES])
        ms = s.sb("ms", [P, 2])
        rrms = s.sb("rrms", [P, 2])
        normed = s.sb("normed", [P, 2, BC])
        qT = s.sb("qT", [P, 2, CH, P])
        kT = s.sb("kT", [P, CH, T])
        v = s.sb("v", [P, NT, BC])
        spare = {"q": kT[:, 0:CH // 2, :], "k": kT[:, CH // 2:, :], "v": v[:, 0:KC, :]}
        w_whole = {"q": spare["q"].rearrange("p c t -> p (c t)").rearrange("p (k i) -> p k i", k=KC),
                   "k": spare["k"].rearrange("p c t -> p (c t)").rearrange("p (k i) -> p k i", k=KC), "v": spare["v"]}
        score = s.sb("score", [P, 4, 2 * P])
        low = s.sb("low", [P, 4])
        prob = s.sb("prob", [P, 4, 2 * P])
        probT = s.sb("probT", [P, 2, 2, 2, P])
        rsum = s.sb("rsum", [P, 2, BH])
        rinv = s.sb("rinv", [P, 2, BH])
        o = s.sb("o", [P, 2, BC])
        oT = s.sb("oT", [P, CH, P])
        ps_s = [[s.ps(f"ps_s{q}{r}", [P, 2, 2 * P]) for r in range(2)] for q in range(2)]
        ps_p = [s.ps(f"ps_p{q}", [P, 2, 2, P]) for q in range(2)]
        ps_o = s.ps("ps_o", [P, HW])
        ps_w = s.ps("ps_w", [P, HW])
        w_in = {kind: s.sem(f"w_in_{kind}") for kind in ("q", "k", "v")}
        early_in = s.sem("early_in")
        late_in = s.sem("late_in")
        xT_in = [s.sem(f"xT_in{p}") for p in range(2)]
        x_in = [s.sem(f"x_in{p}") for p in range(2)]
        y_out = [s.sem(f"y_out{p}") for p in range(2)]
        chain = s.sem("chain")
        held = s.sem("held")
        half_set = s.sem("half_set")
        w_split = s.sem("w_split")
        x_split = s.sem("x_split")
        filled = s.sem("filled")
        emptied = s.sem("emptied")
        squared = s.sem("squared")
        ms_ready = s.sem("ms_ready")
        pow_ready = s.sem("pow_ready")
        normed_ready = s.sem("normed_ready")
        scored = s.sem("scored")
        biased = s.sem("biased")
        exped = s.sem("exped")
        transposed = s.sem("transposed")
        copied = s.sem("copied")
        valued = s.sem("valued")
        o_taken = s.sem("o_taken")
        block = ctx.enter_context(s.programs())

        PROLOGUE = 10
        UNIT = 13

        def sections_before(b, t):
            return PROLOGUE if isinstance(b, int) and b == 0 and t == 0 else UNIT * (NT * b + t) + PROLOGUE - 3

        def steps(b, t, first, last, order=WINDOW_ORDER):
            n = sections_before(b, t)
            for kind, k in order:
                if (kind in NEXT and last) or (kind in PAST and first):
                    continue
                yield kind, k, n
                if kind in NEXT or kind in PAST:
                    n = n + 1

        def units(engine, unit):
            for t in range(NT):
                unit(0, t, t == 0, False)
            with engine.Fori(1, B - 1) as b:
                for t in range(NT):
                    unit(b, t, False, False)
            for t in range(NT):
                unit(B - 1, t, False, t == NT - 1)

        def following(b, t):
            return (b, t + 1) if t < NT - 1 else (b + 1, 0)

        def preceding(b, t):
            return (b, t - 1) if t else (b - 1, NT - 1)

        def section_number(b, t, kind, k):
            early = isinstance(b, int) and b == 0 and t < 2
            place = [x for x in WINDOW_ORDER if x[0] in NEXT or (x[0] in PAST and not early)].index((kind, k))
            return place if early and t == 0 else sections_before(*preceding(b, t)) + place

        def first_tile():
            n = 0
            for kind, k in WINDOW_ORDER:
                if kind in NEXT:
                    yield kind, k, n
                    n += 1

        def last_tile():
            n = sections_before(B - 1, NT - 1) + UNIT - PROLOGUE
            for kind, k in (("out_T", 0), ("out_T", 1), ("out", 0)):
                yield kind, k, n
                n += 1

        def uses(b, t):
            return 2 * b + t // 2 + 1

        @block.sync
        def _(sp):
            def load_xT(b, t):
                sp.dma_start(xT[:, t % 2, :, :], xnT_d[ds(b, 1)].rearrange("a p k t -> p (a k) t")[:, :, t * P:(t + 1) * P]).then_inc(xT_in[t % 2], 16)

            def tokens(dram, b, t):
                return dram[ds(b, 1)].rearrange("a t c -> t (a c)")[t * P:(t + 1) * P, :]

            def store(b, t, done):
                hold(sp, emptied, done + 1, held)
                sp.dma_start(tokens(y_d, b, t), x[:, t % 2, :]).then_inc(y_out[t % 2], 16)

            def unit(b, t, first, last):
                static = isinstance(b, int)
                if not (static and b == B - 1 and t >= 2):
                    hold(sp, emptied, sections_before(b, t), held)
                    load_xT(b + (t + 2) // NT, (t + 2) % NT)
                if not (static and b == 0 and t < 2):
                    past = (b, t - 2) if t >= 2 else (b - 1, t + 2)
                    store(*past, sections_before(*following(*past)) + 2)
                    hold(sp, y_out[t % 2], 16 * (uses(b, t) - 1), held)
                sp.dma_start(x[:, t % 2, :], tokens(x_d, b, t)).then_inc(x_in[t % 2], 16)

            load_xT(0, 0)
            for tile, dram, sem in ((w_whole["q"], wqT_d, w_in["q"]), (ident, const["ident"], early_in), (gamma, gamma_d, early_in),
                                    (w_whole["k"], wkT_d, w_in["k"]), (w_whole["v"], wvT_d, w_in["v"]), (bias, bias_d, late_in), (woT, woT_d, late_in)):
                sp.dma_start(tile[tuple(slice(None) for _ in tile.shape)], dram).then_inc(sem, 16)
            load_xT(0, 1)
            units(nc.sync, unit)
            store(B - 1, NT - 2, sections_before(B - 1, NT - 1) + 2)
            store(B - 1, NT - 1, sections_before(B - 1, NT - 1) + 5)
            for p in range(2):
                sp.wait_ge(y_out[p], 16 * (NT * B // 2))

        @block.tensor
        def _(pe):
            pe.sem_inc(transposed, 2)
            pe.sem_inc(valued, 2)
            pe.wait_ge(early_in, 16 * 2)

            def section(kind, k, n, b, t):
                w = NT * b + t
                if not (isinstance(n, int) and n == 0):
                    pe.wait_ge(emptied, n)
                if kind in ("q", "k", "v"):
                    if kind == "q" and k == 0:
                        pe.wait_ge(x_split, w + 1)
                    if k == 0:
                        pe.wait_ge(w_split, 1 + ("q", "k", "v").index(kind))
                    terms = [(c, x_part, w_part) for c in range(KC) for x_part, w_part in ((1, 0), (0, 0), (0, 1))]
                    for c, x_part, w_part in terms:
                        last = nc.tensor.matmul(ps_w[:, :], xs[x_part][:, t % 2, c, :], wT[kind][w_part][:, c, k * HW:(k + 1) * HW],
                                                start=((c, x_part, w_part) == terms[0]), stop=((c, x_part, w_part) == terms[-1]))
                elif kind in ("q_T", "k_T"):
                    which = 0 if kind == "q_T" else 1
                    pe.wait_ge(normed_ready, 2 * w + which + 3)
                    for c in range(4):
                        last = nc.tensor.transpose(ps_w[:, c * P:(c + 1) * P], normed[:, which, (4 * k + c) * P:(4 * k + c + 1) * P], ident[:, :])
                elif kind == "out_T":
                    pe.wait_ge(o_taken, 2 * w + 3)
                    for c in range(4):
                        last = nc.tensor.transpose(ps_w[:, c * P:(c + 1) * P], o[:, t % 2, (4 * k + c) * P:(4 * k + c + 1) * P], ident[:, :])
                else:
                    for c in range(CH):
                        last = nc.tensor.matmul(ps_w[:, 0:C], oT[:, c, :], woT[:, c, :], start=(c == 0), stop=(c == CH - 1))
                last.then_inc(filled, 1)

            def unit(b, t, first, last):
                u = NT * b + t
                lo = 1 if t == 0 else 0
                if first:
                    pe.wait_ge(late_in, 16 * 2)
                for kind, k, n in steps(b, t, first, last):
                    if kind in NEXT:
                        section(kind, k, n, *following(b, t))
                    elif kind in PAST:
                        section(kind, k, n, *preceding(b, t))
                    elif kind == "scores":
                        if k == 0:
                            pe.wait_ge(emptied, section_number(b, t, "k_T", 0) + 1)
                        elif k == 1:
                            pe.wait_ge(emptied, sections_before(b, t))
                        pe.wait_ge(biased, 16 * u + 4 * k + 4)
                        for hh in range(4):
                            h = 4 * k + hh
                            r = slice(BD * (h % 2), BD * (h % 2) + BD)
                            mm = nc.tensor.matmul(ps_s[k % 2][hh % 2][:, hh // 2, lo * P:], qT[r, t % 2, h // 2, :],
                                                  kT[r, h // 2, (t - 1 + lo) * P:(t + 1) * P], start=True, stop=True)
                        mm.then_inc(scored, 1)
                    elif kind == "probs_T":
                        pe.wait_ge(exped, 16 * u + 2 * k + 6)
                        pe.wait_ge(copied, 8 * u + k + 1)
                        for r in range(2):
                            for c in range(lo, 2):
                                mm = nc.tensor.transpose(ps_p[k % 2][:, r, c, :], prob[:, 2 * (k % 2) + r, c * P:(c + 1) * P], ident[:, :])
                        mm.then_inc(transposed, 1)
                    else:
                        pe.wait_ge(copied, 8 * u + k + 3)
                        if k % 4 == 0:
                            pe.wait_ge(o_taken, 2 * u + k // 4 + 1)
                        for r in range(2):
                            h = 2 * k + r
                            for c in range(lo, 2):
                                mm = nc.tensor.matmul(ps_o[:, h % 8 * BD:(h % 8 + 1) * BD], probT[:, k % 2, r, c, :],
                                                      v[:, t - 1 + c, h * BD:(h + 1) * BD], start=(c == lo), stop=(c == 1))
                        mm.then_inc(valued, 1)

            for kind, k, n in first_tile():
                section(kind, k, n, 0, 0)
            units(nc.tensor, unit)
            for kind, k, n in last_tile():
                section(kind, k, n, B - 1, NT - 1)

        @block.scalar
        def _(act):
            act.sem_inc(exped, 4)

            def section(kind, k, n, b, t):
                if kind == "out":
                    return
                act.wait_ge(filled, n + 1)
                if kind in ("q", "k"):
                    which = 0 if kind == "q" else 1
                    nc.scalar.activation(square[:, :], ps_w[:, :], ACT.Square, accum_out=ss[:, which, k:k + 1]).then_inc(squared, 1)
                    return
                by_chunk = ps_w[:, :].rearrange("p (c t) -> p c t", t=P)
                if kind == "v":
                    copy = nc.scalar.copy(v[:, t, k * HW:(k + 1) * HW], ps_w[:, :])
                elif kind == "q_T":
                    copy = nc.scalar.copy(qT[:, t % 2, 4 * k:4 * k + 4, :], by_chunk)
                elif kind == "k_T":
                    copy = nc.scalar.copy(kT[:, 4 * k:4 * k + 4, t * P:(t + 1) * P], by_chunk)
                else:
                    copy = nc.scalar.copy(oT[:, 4 * k:4 * k + 4, :], by_chunk)
                copy.then_inc(emptied, 1)

            def unit(b, t, first, last):
                u = NT * b + t
                lo = 1 if t == 0 else 0
                for kind, k, n in steps(b, t, first, last, WINDOW_SCALAR_ORDER):
                    if kind in NEXT:
                        section(kind, k, n, *following(b, t))
                    elif kind in PAST:
                        section(kind, k, n, *preceding(b, t))
                    elif kind == "scores":
                        for hh in range(4):
                            h = 4 * k + hh
                            act.wait_ge(biased, 16 * u + h + 9)
                            if h % 2 == 0:
                                act.wait_ge(transposed, 8 * u + h // 2 + 1)
                            nc.scalar.activation(prob[:, hh, lo * P:], score[:, hh, lo * P:], ACT.Exp, bias=low[:, hh:hh + 1], scale=-1.0,
                                                 accum_out=rsum[:, t % 2, h:h + 1]).then_inc(exped, 1)

            for kind, k, n in first_tile():
                section(kind, k, n, 0, 0)
            units(nc.scalar, unit)
            for kind, k, n in last_tile():
                section(kind, k, n, B - 1, NT - 1)

        @block.gpsimd
        def _(pool):
            nc.gpsimd.memset(minus_half[:, :], -0.5).then_inc(half_set, 1)
            pool.sem_inc(normed_ready, 2)
            pool.wait_ge(half_set, 1)
            with nc.gpsimd.Fori(0, NT * B) as w:
                pool.wait_ge(ms_ready, w + 1)
                nc.gpsimd.tensor_tensor(rrms[:, :], ms[:, :], minus_half[:, :], ALU.pow).then_inc(pow_ready, 1)
                hold(pool, pow_ready, w + 1, held)
                for i in range(2):
                    nc.gpsimd.tensor_scalar(normed[:, i, :], raw[:, i, :], rrms[:, i:i + 1], 1.0, ALU.mult, ALU.mult).then_inc(normed_ready, 1)

        @block.vector
        def _(dve):
            dve.sem_inc(biased, 8)
            dve.sem_inc(copied, 2)
            dve.sem_inc(o_taken, 1)
            LINKS = 6

            def split_x(b, t, ch):
                hold(dve, xT_in[t % 2], 16 * uses(b, t), held)
                flat = lambda x: x[:, t % 2, :, :].rearrange("p k t -> p (k t)")
                split_piece(nc, ch, masked[:, 0:KC * P], flat(xT), *[flat(part) for part in xs])
                dve.sem_inc(x_split, 1)

            def section(kind, k, n, b, t, ch):
                w = NT * b + t
                if kind in ("q", "k"):
                    which = 0 if kind == "q" else 1
                    dve.wait_ge(squared, 4 * w + 2 * which + k + 1)
                    if kind == "q" and k == 0:
                        dve.wait_ge(normed_ready, 2 * w + 2)
                    half = slice(k * HW, (k + 1) * HW)
                    nc.vector.tensor_tensor(raw[:, which, half], ps_w[:, :], gamma[:, which, half], ALU.mult).then_inc(emptied, 1)
                    if kind == "k" and k == 1:
                        ch.link(nc.vector.tensor_tensor(ms[:, :], ss[:, :, 0], ss[:, :, 1], ALU.add))
                        nc.vector.tensor_scalar(ms[:, :], ms[:, :], 1.0 / BC, RMS_EPS, ALU.mult, ALU.add).then_inc(ms_ready, 1)
                elif kind == "out":
                    dve.wait_ge(x_in[t % 2], 16 * uses(b, t))
                    dve.wait_ge(filled, n + 1)
                    nc.vector.tensor_tensor(x[:, t % 2, :], x[:, t % 2, :], ps_w[:, 0:C], ALU.add).then_inc(emptied, 1)

            def unit(b, t, first, last):
                u = NT * b + t
                lo = 1 if t == 0 else 0
                ch = Chain(dve, chain, LINKS * u + START)
                if first:
                    dve.wait_ge(late_in, 16 * 2)
                if not last:
                    hold(dve, filled, sections_before(b, t), held)
                    split_x(*following(b, t), ch)
                for kind, k, n in steps(b, t, first, last):
                    if kind in NEXT:
                        section(kind, k, n, *following(b, t), ch)
                    elif kind in PAST:
                        section(kind, k, n, *preceding(b, t), ch)
                    elif kind == "scores":
                        dve.wait_ge(scored, 4 * u + k + 1)
                        for hh in range(4):
                            h = 4 * k + hh
                            hold(dve, exped, 16 * u + h + 1, held)
                            nc.vector.tensor_tensor_reduce(out=score[:, hh, lo * P:], in0=ps_s[k % 2][hh % 2][:, hh // 2, lo * P:],
                                                           in1=bias[:, h, lo * P:], scale=-B_SCALE, scalar=3.0e38, op0=ALU.add, op1=ALU.min,
                                                           accum_out=low[:, hh:hh + 1]).then_inc(biased, 1)
                    elif kind == "probs_T":
                        dve.wait_ge(transposed, 8 * u + k + 3)
                        dve.wait_ge(valued, 8 * u + k + 1)
                        nc.vector.tensor_copy(probT[:, k % 2, :, lo:, :], ps_p[k % 2][:, :, lo:, :]).then_inc(copied, 1)
                    elif k % 4 == 3:
                        half = k // 4
                        dve.wait_ge(valued, 8 * u + k + 3)
                        hs = slice(8 * half, 8 * half + 8)
                        ch.link(nc.vector.reciprocal(rinv[:, t % 2, hs], rsum[:, t % 2, hs]))
                        nc.vector.tensor_tensor(o[:, t % 2, half * HW:(half + 1) * HW].rearrange("p (h d) -> p h d", d=BD),
                                                ps_o[:, :].rearrange("p (h d) -> p h d", d=BD),
                                                rinv[:, t % 2, hs].unsqueeze(2).to_broadcast([P, 8, BD]), ALU.mult).then_inc(o_taken, 1)

            ch = Chain(dve, chain)
            split_x(0, 0, ch)
            for kind, parts in wT.items():
                dve.wait_ge(w_in[kind], 16)
                for c in range(KC):
                    for half in (slice(0, HW), slice(HW, BC)):
                        split_piece(nc, ch, masked[:, :], w_whole[kind][:, c, half], *[part[:, c, half] for part in parts])
                dve.sem_inc(w_split, 1)
            dve.wait_ge(early_in, 16 * 2)
            START = ch.n + 1
            for kind, k, n in first_tile():
                section(kind, k, n, 0, 0, ch)
            units(nc.vector, unit)
            for kind, k, n in last_tile():
                section(kind, k, n, B - 1, NT - 1, ch)


RELATIVE_ORDER = [
    ("scores", 0), ("q", 0), ("scores", 1), ("k", 0), ("scores", 2), ("v", 0), ("probs_T", 0), ("probs_T", 1),
    ("scores", 3), ("q_band", 0), ("probs_T", 2), ("probs_T", 3), ("k_band", 0), ("q_band", 1),
    ("scores", 4), ("probs_T", 4), ("k_band", 1), ("values", 0), ("probs_T", 5), ("q_band", 2),
    ("scores", 5), ("k_band", 2), ("probs_T", 6), ("probs_T", 7), ("q_band", 3),
    ("scores", 6), ("values", 1), ("probs_T", 8), ("k_band", 3), ("probs_T", 9), ("bins_T", 0), ("probs_T", 10),
    ("scores", 7), ("bins_T", 1), ("probs_T", 11), ("bins", 0), ("probs_T", 12), ("out", 0), ("q_stack", 0),
    ("values", 2), ("k_stack", 0), ("probs_T", 13), ("probs_T", 14), ("q_stack", 1), ("probs_T", 15), ("k_stack", 1),
    ("values", 3),
]


RELATIVE_SCALAR_ORDER = scores_later(RELATIVE_ORDER, (1, 1, 3, 6, 5, 5, 5, 2))
A_NEXT = ("q", "k", "v", "q_band", "k_band", "q_stack", "k_stack")
A_PAST = ("bins_T", "bins", "out")


def relative_stage(nc, tag, const, xnT_d, wT_d, rows_d, table_d, base_d, bins_d, bins_base_d, vbase_d, scratch, o_d):
    Q, K = 0, 1
    W4 = HG * WIN
    with ExitStack() as ctx:
        s = Store(nc, ctx, tag)
        ident = s.sb("ident", [P, P])
        lower = s.sb("lower", [P, P])
        upper = s.sb("upper", [P, P])
        wT = s.sb("wT", [P, 2, NG, KC, P])
        wv = s.sb("wv", [P, KC, C])
        diff = s.sb("diff", [P, 2, NG, HG, XB + 1])
        bins_w = s.sb("bins_w", [P, NG, 2, 64])
        vbase = s.sb("vbase", [P, 2, C])
        scale = s.sb("scale", [P, 4])
        shift = s.sb("shift", [P, 4])
        spread = s.sb("spread", [P, 2, 2, 2, P], F32R)
        xT = s.sb("xT", [P, KC, T])
        qk = s.sb("qk", [P, 2, T])
        masked = s.sb("masked", [P, T])
        high = s.sb("high", [P, 2, T], F32R)
        rest = s.sb("rest", [P, 2, T], F32R)
        q_stack = s.sb("q_stack", [P, 2, 2, T], F32R)
        k_stack = s.sb("k_stack", [P, 2, 2, 2, T], F32R)
        v = s.sb("v", [P, 2, 2, NT, HG, 32])
        band = s.sb("band", [P, 2, NT, HG, WIN])
        edge = s.sb("edge", [P, 2, 2, NT, HG])
        win = s.sb("win", [P, 2, 2, NT, HG, WIN])
        spare = win[:, :, :, :, :, :].rearrange("p a b c d e -> p (a b c d e)")
        taken = 0

        def in_spare(names, shape):
            nonlocal taken
            n = int(np.prod(shape))
            taken += n
            return spare[:, taken - n:taken].rearrange(f"p ({names}) -> p {names}", **dict(zip(names.split(), shape)))

        rows = in_spare("d g c", (2, NG, C))
        table = in_spare("d g h x", (2, NG, HG, XB + 1))
        base = in_spare("d g h x", (2, NG, HG, XB + 1))
        bins_b = in_spare("g r x", (NG, 2, 64))
        spread_in = in_spare("d k i x", (2, 2, 2, P))
        tri = s.sb("tri", [P, 2, HG, P])
        low = s.sb("low", [P, 2, 2])
        prob = s.sb("prob", [P, 2, HG, 32 + T + 32])
        probT = s.sb("probT", [P, 2, HG, T])
        rsum = s.sb("rsum", [P, 2, NT, HG])
        rinv = s.sb("rinv", [P, NT, HG])
        junk = s.sb("junk", [P, 2, P])
        below = s.sb("below", [P, 2, NT, HG])
        bins = s.sb("bins", [P, 2, NT, HG, XB])
        binsT = s.sb("binsT", [P, 2, NT, P])
        oT = s.sb("oT", [P, T])
        o = s.sb("o", [P, 2, NT, HG, AD])
        ps_s = [s.ps(f"ps_s{q}", [P, 2, T]) for q in range(2)]
        ps_p = [s.ps(f"ps_p{q}", [P, T]) for q in range(2)]
        ps_o = s.ps("ps_o", [P, T])
        ps_w = s.ps("ps_w", [P, T])
        const_in = s.sem("const_in")
        chain = s.sem("chain")
        pool_chain = s.sem("pool_chain")
        held = s.sem("held")
        folded = s.sem("folded")
        set_up = s.sem("set_up")
        xT_in = s.sem("xT_in")
        filled = s.sem("filled")
        emptied = s.sem("emptied")
        split = s.sem("split")
        band_out = [[s.sem(f"band_out{d}{t}") for t in range(NT)] for d in range(2)]
        win_in = [[s.sem(f"win_in{d}{t}") for t in range(NT)] for d in range(2)]
        win_ready = s.sem("win_ready")
        scored = s.sem("scored")
        maxed = s.sem("maxed")
        exped = s.sem("exped")
        transposed = s.sem("transposed")
        copied = [s.sem(f"copied{q}") for q in range(2)]
        valued = s.sem("valued")
        summed = s.sem("summed")
        prob_out = [s.sem(f"prob_out{q}") for q in range(2)]
        bins_in = [s.sem(f"bins_in{q}") for q in range(2)]
        bins_ready = s.sem("bins_ready")
        o_taken = s.sem("o_taken")
        o_ready = s.sem("o_ready")
        o_out = [s.sem(f"o_out{q}") for q in range(2)]
        loads = ((ident, const["ident"]), (lower, const["lower"]), (upper, const["upper"]), (wT, wT_d[0]), (wv, wT_d[1]), (rows, rows_d),
                 (table, table_d), (base, base_d), (bins_w, bins_d), (bins_b, bins_base_d), (vbase, vbase_d),
                 (scale, const["row_scale"]), (shift, const["row_shift"]), (spread_in, const["spread"]))
        block = ctx.enter_context(s.programs())

        PROLOGUE = sum(kind in A_NEXT for kind, _ in RELATIVE_ORDER)
        PAST = sum(kind in A_PAST for kind, _ in RELATIVE_ORDER)
        UNIT = PROLOGUE + PAST

        def sections_before(b, g):
            return PROLOGUE if isinstance(b, int) and b == 0 and g == 0 else UNIT * (NG * b + g) + PROLOGUE - PAST

        def steps(b, g, first, last, order=RELATIVE_ORDER):
            n = sections_before(b, g)
            for kind, k in order:
                if (kind in A_NEXT and last) or (kind in A_PAST and first):
                    continue
                yield kind, k, n
                if kind in A_NEXT or kind in A_PAST:
                    n = n + 1

        def units(engine, unit):
            for g in range(NG):
                unit(0, g, g == 0, False)
            with engine.Fori(1, B - 1) as b:
                for g in range(NG):
                    unit(b, g, False, False)
            for g in range(NG):
                unit(B - 1, g, False, g == NG - 1)

        def following(b, g):
            return (b, g + 1) if g < NG - 1 else (b + 1, 0)

        def preceding(b, g):
            return (b, g - 1) if g else (b - 1, NG - 1)

        def first_unit():
            n = 0
            for kind, k in RELATIVE_ORDER:
                if kind in A_NEXT:
                    yield kind, k, n
                    n += 1

        def last_unit():
            n = sections_before(B - 1, NG - 1) + UNIT - PROLOGUE
            for kind, k in RELATIVE_ORDER:
                if kind in A_PAST:
                    yield kind, k, n
                    n += 1

        def section_number(b, g, kind, k):
            early = isinstance(b, int) and b == 0 and g < 2
            place = [x for x in RELATIVE_ORDER if x[0] in A_NEXT or (x[0] in A_PAST and not early)].index((kind, k))
            return place if early and g == 0 else sections_before(*preceding(b, g)) + place

        def uses(b, g):
            return 2 * b + g // 2 + 1

        def window_columns(t):
            return max(0, t * P - 32), min(T, t * P + P + 32), 32 if t == 0 else 0

        @block.sync
        def _(sp):
            for tile, dram in loads:
                sp.dma_start(tile[tuple(slice(None) for _ in tile.shape)], dram).then_inc(const_in, 16)

            def next_unit(b, g):
                u = NG * b + g
                if g == 0:
                    if not (isinstance(b, int) and b == 0):
                        hold(sp, emptied, section_number(*preceding(b, g), "v", 0) + 1, held)
                    sp.dma_start(xT[:, :, :], by_channel(xnT_d, b)).then_inc(xT_in, 16)
                for step in range(NT + 1):
                    for d in range(2):
                        if step < NT:
                            hold(sp, emptied, section_number(b, g, ("q_band", "k_band")[d], step) + 1, held)
                            sp.dma_start(scratch["band"][d, g % 2, step], band[:, d, step, :, :].rearrange("p h x -> p (h x)")).then_inc(band_out[d][step], 16)
                        if step:
                            t = step - 1
                            hold(sp, band_out[d][t], 16 * u + 16, held)
                            rows_at = scratch["band"][d, g % 2, t]
                            skewed = bass.AP(rows_at.tensor, rows_at.offset, [[W4 - 1, P], [1, W4]])
                            sp.dma_start(win[:, g % 2, d, t, :, :].rearrange("p h x -> p (h x)"), skewed).then_inc(win_in[d][t], 16)

            def store(b, g):
                hold(sp, o_ready, NG * b + g + 1, held)
                out = o_d[ds(b, 1)].rearrange("a (t p) c -> p (a t) c", p=P)[:, :, g * HG * AD:(g + 1) * HG * AD]
                sp.dma_start(out, o[:, g % 2, :, :, :].rearrange("p t h d -> p t (h d)")).then_inc(o_out[g % 2], 16)

            def unit(b, g, first, last):
                if not last:
                    next_unit(*following(b, g))
                if not first:
                    store(*preceding(b, g))

            next_unit(0, 0)
            units(nc.sync, unit)
            store(B - 1, NG - 1)
            for q in range(2):
                sp.wait_ge(o_out[q], 16 * NG * B // 2)

        @block.tensor
        def _(pe):
            pe.sem_inc(transposed, 8)
            pe.sem_inc(valued, 2)
            pe.wait_ge(const_in, 16 * len(loads))
            for d in range(2):
                for end in range(2):
                    x = ((1, BUCKETS), (BUCKETS, 1))[d][end]
                    for g in range(NG):
                        for c in range(KC):
                            at = (((d * 2 + end) * NG + g) * KC + c) * HG
                            last = nc.tensor.matmul(ps_w[:, at:at + HG], rows[:, d, g, c * P:(c + 1) * P], table[:, d, g, :, x], start=True, stop=True)
            last.then_inc(folded, 1)
            pe.wait_ge(set_up, 1)

            def section(kind, k, n, b, g):
                if not (isinstance(n, int) and n == 0):
                    pe.wait_ge(emptied, n)
                if kind in ("q", "k"):
                    if kind == "q" and g == 0:
                        pe.wait_ge(xT_in, 16 * b + 16)
                    for c in range(KC):
                        last = nc.tensor.matmul(ps_w[:, :], wT[:, 0 if kind == "q" else 1, g, c, :], xT[:, c, :], start=(c == 0), stop=(c == KC - 1))
                elif kind == "v":
                    for t in range(NT):
                        for c in range(KC):
                            last = nc.tensor.matmul(ps_w[:, t * HG * AD:(t + 1) * HG * AD], xT[:, c, t * P:(t + 1) * P],
                                                    wv[:, c, g * HG * AD:(g + 1) * HG * AD], start=(c == 0), stop=(c == KC - 1))
                elif kind in ("q_band", "k_band"):
                    d = 0 if kind == "q_band" else 1
                    last = nc.tensor.matmul(ps_w[:, 0:HG * (XB + 1)], qk[:, d, k * P:(k + 1) * P],
                                            diff[:, d, g, :, :].rearrange("p h x -> p (h x)"), start=True, stop=True)
                elif kind in ("q_stack", "k_stack"):
                    d = 0 if kind == "q_stack" else 1
                    pe.wait_ge(split, 2 * (NG * b + g) + 1 + d)
                    nc.tensor.matmul(ps_w[:, :], spread[:, d, k, 0, :], high[:, d, :], start=True, stop=False)
                    last = nc.tensor.matmul(ps_w[:, :], spread[:, d, k, 1, :], rest[:, d, :], start=False, stop=True)
                elif kind == "bins_T":
                    if k == 0:
                        pe.wait_ge(bins_ready, NG * b + g + 1)
                    for m in range(4):
                        t, r = 2 * k + m % 2, m // 2
                        last = nc.tensor.transpose(ps_w[:, m * P:(m + 1) * P], bins[:, g % 2, t, 2 * r:2 * r + 2, :].rearrange("p h x -> p (h x)"), ident[:, :])
                elif kind == "bins":
                    for r in range(2):
                        last = nc.tensor.matmul(ps_w[64 * r:64 * r + 64, :], bins_w[:, g, r, :], binsT[:, r, :, :].rearrange("p t i -> p (t i)"), start=True, stop=True)
                else:
                    for t in range(NT):
                        last = nc.tensor.transpose(ps_w[:, t * P:(t + 1) * P], oT[:, t * P:(t + 1) * P], ident[:, :])
                last.then_inc(filled, 1)

            def unit(b, g, first, last):
                u = NG * b + g
                p = g % 2
                for kind, k, n in steps(b, g, first, last):
                    if kind in A_NEXT:
                        section(kind, k, n, *following(b, g))
                    elif kind in A_PAST:
                        section(kind, k, n, *preceding(b, g))
                    elif kind == "scores":
                        t = k // 2
                        if k == 0:
                            pe.wait_ge(emptied, section_number(b, g, "k_stack", 0) + 1)
                        elif k == 1:
                            pe.wait_ge(emptied, sections_before(b, g))
                        pe.wait_ge(win_ready, 8 * u + 2 * min(t + 1, NT - 1) + 2)
                        pe.wait_ge(exped, 16 * u + 2 * k + 2)
                        heads = [2 * (k % 2), 2 * (k % 2) + 1]
                        for h in heads:
                            r = slice(64 * (h % 2), 64 * (h % 2) + 64)
                            q_tile = q_stack[r, p, k % 2, t * P:(t + 1) * P]
                            bank = ps_s[k % 2][:, h % 2, :]
                            if t:
                                nc.tensor.matmul(bank[:, 0:t * P], q_tile, k_stack[r, p, 0, k % 2, 0:t * P], start=True, stop=False)
                            nc.tensor.matmul(bank[:, t * P:], q_tile, k_stack[r, p, 1, k % 2, t * P:], start=(t == 0), stop=False)
                        for h in heads:
                            bank = ps_s[k % 2][:, h % 2, :]
                            if t:
                                nc.tensor.matmul(bank[0:32, t * P - 32:t * P], win[96:P, p, K, t - 1, h, 160:192], ident[96:P, 96:P], start=False, stop=False)
                            if t < NT - 1:
                                nc.tensor.matmul(bank[96:P, (t + 1) * P:(t + 1) * P + 32], win[0:32, p, K, t + 1, h, 0:32], ident[0:32, 0:32], start=False, stop=False)
                            mm = nc.tensor.matmul(bank[:, t * P:(t + 1) * P], win[:, p, K, t, h, 32:160], ident[:, :], start=False, stop=True)
                        mm.then_inc(scored, 1)
                    elif kind == "probs_T":
                        t, h = k // HG, k % HG
                        pe.wait_ge(exped, 16 * u + k + 5)
                        pe.wait_ge(copied[k % 2], 8 * u + k // 2 + 1)
                        for c in range(NT):
                            mm = nc.tensor.transpose(ps_p[k % 2][:, c * P:(c + 1) * P], prob[:, t % 2, h, 32 + c * P:32 + (c + 1) * P], ident[:, :])
                        mm.then_inc(transposed, 1)
                    else:
                        t = k
                        for q in range(2):
                            pe.wait_ge(copied[q], 8 * u + 2 * t + 3)
                        if t == 0:
                            pe.wait_ge(o_taken, u + 1)
                        for c in range(NT):
                            for h in range(HG):
                                mm = nc.tensor.matmul(ps_o[32 * h:32 * h + 32, t * P:(t + 1) * P], v[:, p, 0 if c < t else 1, c, h, :],
                                                      probT[:, t % 2, h, c * P:(c + 1) * P], start=(c == 0), stop=(c == NT - 1))
                        mm.then_inc(valued, 1)

            for kind, k, n in first_unit():
                section(kind, k, n, 0, 0)
            units(nc.tensor, unit)
            for kind, k, n in last_unit():
                section(kind, k, n, B - 1, NG - 1)

        @block.scalar
        def _(act):
            act.sem_inc(exped, 4)
            act.sem_inc(copied[1], 1)
            act.wait_ge(const_in, 16 * len(loads))

            def section(kind, k, n, b, g):
                p = g % 2
                if kind in ("v", "bins", "out"):
                    return
                act.wait_ge(filled, n + 1)
                if kind in ("q", "k"):
                    i = 0 if kind == "q" else 1
                    last = nc.scalar.activation(qk[:, i, :], ps_w[:, :], ACT.Identity, bias=shift[:, i:i + 1], scale=scale[:, i:i + 1])
                elif kind == "q_stack":
                    last = nc.scalar.copy(q_stack[:, p, k, :], ps_w[:, :])
                elif kind == "k_stack":
                    for i in range(2):
                        last = nc.scalar.activation(k_stack[:, p, i, k, :], ps_w[:, :], ACT.Identity, bias=shift[:, 2 + i:3 + i], scale=scale[:, 2 + i:3 + i])
                elif kind in ("q_band", "k_band"):
                    d = 0 if kind == "q_band" else 1
                    if not (isinstance(b, int) and b == 0 and g == 0):
                        act.wait_ge(band_out[d][k], 16 * (NG * b + g))
                    got = ps_w[:, 0:HG * (XB + 1)].rearrange("p (h x) -> p h x", h=HG)
                    nc.scalar.copy(band[:, d, k, :, 0:XB], got[:, :, 0:XB])
                    last = nc.scalar.copy(edge[:, p, d, k, :].unsqueeze(2), got[:, :, XB:])
                else:
                    last = nc.scalar.copy(binsT[:, :, 2 * k:2 * k + 2, :].rearrange("p r t i -> p r (t i)"), ps_w[:, :].rearrange("p (r x) -> p r x", r=2))
                last.then_inc(emptied, 1)

            def bins_home(b, g, t):
                act.wait_ge(prob_out[t % 2], 16 * (2 * (NG * b + g) + t // 2 + 1))
                src = scratch["prob"][t % 2]
                skewed = bass.AP(src.tensor, src.offset, [[W4 + 1, P], [WIN, HG], [1, XB]])
                act.dma_start(bins[:, g % 2, t, :, :], skewed).then_inc(bins_in[t % 2], 16)

            def unit(b, g, first, last):
                u = NG * b + g
                p = g % 2
                for kind, k, n in steps(b, g, first, last, RELATIVE_SCALAR_ORDER):
                    if kind in A_NEXT:
                        section(kind, k, n, *following(b, g))
                    elif kind in A_PAST:
                        section(kind, k, n, *preceding(b, g))
                    elif kind == "scores":
                        t = k // 2
                        act.wait_ge(maxed, 8 * u + k + 1)
                        if k % 2 == 0:
                            act.wait_ge(transposed, 16 * u + 4 * t + 4)
                            act.wait_ge(summed, 16 * u + 4 * t + 4)
                            if not (first and t < 2):
                                act.wait_ge(prob_out[t % 2], 16 * (2 * u + t // 2))
                        for r in range(2):
                            h = 2 * (k % 2) + r
                            nc.scalar.activation(prob[:, t % 2, h, 32:32 + T], ps_s[k % 2][:, r, :], ACT.Exp, bias=low[:, k % 2, r:r + 1],
                                                 accum_out=rsum[:, p, t, h:h + 1]).then_inc(exped, 1)
                        if k % 2:
                            act.wait_ge(exped, 16 * u + 4 * t + 8)
                            if not (first and t < 2):
                                act.wait_ge(bins_in[t % 2], 16 * (2 * u + t // 2))
                            act.dma_start(scratch["prob"][t % 2].rearrange("p (h x) -> p h x", h=HG),
                                          prob[:, t % 2, :, t * P:t * P + WIN]).then_inc(prob_out[t % 2], 16)
                            if t:
                                bins_home(b, g, t - 1)
                            elif not first:
                                bins_home(*preceding(b, g), NT - 1)
                    elif kind == "probs_T" and k % 2:
                        act.wait_ge(transposed, 16 * u + k + 9)
                        act.wait_ge(valued, 4 * u + k // HG + 1)
                        nc.scalar.copy(probT[:, k // HG % 2, k % HG, :], ps_p[1][:, :]).then_inc(copied[1], 1)

            act.wait_ge(set_up, 1)
            for kind, k, n in first_unit():
                section(kind, k, n, 0, 0)
            units(nc.scalar, unit)
            bins_home(B - 1, NG - 1, NT - 1)
            for kind, k, n in last_unit():
                section(kind, k, n, B - 1, NG - 1)

        @block.gpsimd
        def _(pool):
            def next_unit(b, g):
                u = NG * b + g
                ch = Chain(pool, pool_chain, 8 * u)
                for t in range(NT):
                    if not (isinstance(u, int) and u + t == 0):
                        pool.wait_ge(win_ready, 8 * u + 2 * t)
                    pool.wait_ge(emptied, section_number(b, g, "k_band", t) + 1)
                    for d in range(2):
                        ch.mark(nc.gpsimd.tensor_tensor(tri[:, d, :, :], (lower, upper)[d][:, :].unsqueeze(1).to_broadcast([P, HG, P]),
                                                        edge[:, g % 2, d, t, :].unsqueeze(2).to_broadcast([P, HG, P]), ALU.mult))
                    ch.settle()
                    for d in range(2):
                        pool.wait_ge(win_in[d][t], 16 * u + 16)
                        square = win[:, g % 2, d, t, :, 32:160]
                        nc.gpsimd.tensor_tensor(square, square, tri[:, d, :, :], ALU.add).then_inc(win_ready, 1)

            def unit(b, g, first, last):
                if not last:
                    next_unit(*following(b, g))

            pool.wait_ge(const_in, 16 * len(loads))
            next_unit(0, 0)
            units(nc.gpsimd, unit)

        @block.vector
        def _(dve):
            SETUP = 3
            dve.sem_inc(copied[0], 1)
            dve.sem_inc(summed, 8)
            dve.sem_inc(o_taken, 1)
            ch = Chain(dve, chain)
            nc.vector.memset(v[:, :, :, :, :, AD:].rearrange("p a b t h d -> p (a b t h) d"), 0.0)
            ch.mark(nc.vector.memset(band[:, :, :, :, XB:].rearrange("p d t h x -> p (d t h) x"), 0.0))
            nc.vector.memset(prob[:, :, :, 0:32].rearrange("p t h x -> p (t h) x"), 0.0)
            ch.mark(nc.vector.memset(prob[:, :, :, 32 + T:].rearrange("p t h x -> p (t h) x"), 0.0))
            dve.wait_ge(const_in, 16 * len(loads))
            flat = lambda x: x[:, :, :, :, :].rearrange("p d g h x -> p (d g h x)")
            ch.mark(nc.vector.tensor_tensor(flat(diff), flat(table), flat(base), ALU.subtract))
            ch.settle()
            nc.vector.tensor_scalar(diff[:, K, :, :, :], diff[:, K, :, :, :], A_SCALE, None, ALU.mult)
            nc.vector.tensor_tensor(bins_w[:, :, :, :], bins_w[:, :, :, :], bins_b[:, :, :, :], ALU.subtract)
            nc.vector.tensor_copy(spread[:, :, :, :, :].rearrange("p d k i x -> p (d k i x)"), spread_in[:, :, :, :, :].rearrange("p d k i x -> p (d k i x)"))
            dve.wait_ge(folded, 1)
            for d in range(2):
                for end in range(2):
                    at = (d * 2 + end) * NG * KC * HG
                    last = nc.vector.tensor_copy(wT[:, d, :, :, :].rearrange("p g c (h r) -> p (g c) h r", r=32)[:, :, :, AD + 2 * d + end],
                                                 ps_w[:, at:at + NG * KC * HG].rearrange("p (m h) -> p m h", h=HG))
            last.then_inc(set_up, 1)

            def section(kind, k, n, b, g, ch):
                p = g % 2
                if kind == "v":
                    dve.wait_ge(filled, n + 1)
                    for i in range(2):
                        last = nc.vector.tensor_tensor(v[:, p, i, :, :, 0:AD], ps_w[:, 0:C].rearrange("p (t h d) -> p t h d", t=NT, h=HG),
                                                       vbase[:, i, g * HG * AD:(g + 1) * HG * AD].rearrange("p (h d) -> p h d", h=HG)
                                                       .unsqueeze(1).to_broadcast([P, NT, HG, AD]), ALU.add)
                    last.then_inc(emptied, 1)
                elif kind in ("q", "k"):
                    i = 0 if kind == "q" else 1
                    dve.wait_ge(emptied, n + 1)
                    if not (isinstance(b, int) and b == 0 and g + i == 0):
                        dve.wait_ge(split, 2 * (NG * b + g) + i)
                    ch.link(nc.vector.tensor_single_scalar(masked[:, :].bitcast(I32), qk[:, i, :].bitcast(I32), HIGH_BITS, ALU.bitwise_and))
                    nc.vector.tensor_copy(high[:, i, :], masked[:, :])
                    nc.vector.tensor_tensor(rest[:, i, :], qk[:, i, :], masked[:, :], ALU.subtract).then_inc(split, 1)
                elif kind == "bins":
                    ch.link(nc.vector.reciprocal(rinv[:, :, :], rsum[:, p, :, :]))
                    dve.wait_ge(filled, n + 1)
                    dve.wait_ge(o_taken, NG * b + g + 2)
                    nc.vector.tensor_tensor(oT[:, :], oT[:, :], ps_w[:, :], ALU.add).then_inc(emptied, 1)
                elif kind == "out":
                    dve.wait_ge(filled, n + 1)
                    if not (isinstance(b, int) and b == 0 and g < 2):
                        dve.wait_ge(o_out[p], 16 * (uses(b, g) - 1))
                    ch.link(nc.vector.tensor_tensor(o[:, p, :, :, :].rearrange("p t h d -> p (t h) d"), ps_w[:, :].rearrange("p (m r) -> p m r", r=32)[:, :, 0:AD],
                                                    rinv[:, :, :].rearrange("p t h -> p (t h)").unsqueeze(2).to_broadcast([P, NT * HG, AD]), ALU.mult))
                    dve.sem_inc(emptied, 1)
                    dve.sem_inc(o_ready, 1)
                elif kind == "bins_T" and k == 0:
                    for t in range(NT - 2, NT):
                        dve.wait_ge(bins_in[t % 2], 16 * (2 * (NG * b + g) + 2))
                    dve.wait_ge(summed, 16 * (NG * b + g) + 24)
                    nc.vector.tensor_copy(bins[:, p, :, :, 0], below[:, p, :, :]).then_inc(bins_ready, 1)

            def unit(b, g, first, last):
                u = NG * b + g
                p = g % 2
                ch = Chain(dve, chain, SETUP + 2 if isinstance(b, int) and u == 0 else 12 * u + SETUP)
                for kind, k, n in steps(b, g, first, last):
                    if kind in A_NEXT:
                        section(kind, k, n, *following(b, g), ch)
                    elif kind in A_PAST:
                        section(kind, k, n, *preceding(b, g), ch)
                    elif kind == "scores":
                        t = k // 2
                        c0, c1, x0 = window_columns(t)
                        h0 = 2 * (k % 2)
                        dve.wait_ge(win_ready, 8 * u + 2 * t + 1)
                        dve.wait_ge(scored, 8 * u + k + 1)
                        both = ps_s[k % 2]
                        ch.link(nc.vector.tensor_tensor(both[:, :, c0:c1], both[:, :, c0:c1], win[:, p, Q, t, h0:h0 + 2, x0:x0 + c1 - c0], ALU.add))
                        nc.vector.reduce_max(low[:, k % 2, :], both[:, :, :], AX.X, negate=True).then_inc(maxed, 1)
                    elif kind == "probs_T":
                        t, h = k // HG, k % HG
                        if k % 2 == 0:
                            dve.wait_ge(transposed, 16 * u + k + 9)
                            dve.wait_ge(valued, 4 * u + k // HG + 1)
                            nc.vector.tensor_copy(probT[:, k // HG % 2, k % HG, :], ps_p[0][:, :]).then_inc(copied[0], 1)
                        dve.wait_ge(summed, 16 * u + k + 7)
                        hold(dve, exped, 16 * u + k + 5, held)
                        nc.vector.tensor_tensor_reduce(out=junk[:, k % 2, :], in0=prob[:, t % 2, h, 32 + t * P:32 + (t + 1) * P], in1=lower[:, :],
                                                       scale=1.0, scalar=0.0, op0=ALU.mult, op1=ALU.add, accum_out=below[:, p, t, h:h + 1]).then_inc(summed, 1)
                    elif kind == "values" and k == NT - 1:
                        dve.wait_ge(valued, 4 * u + 6)
                        nc.vector.tensor_copy(oT[:, :], ps_o[:, :]).then_inc(o_taken, 1)

            for kind, k, n in first_unit():
                section(kind, k, n, 0, 0, ch)
            units(nc.vector, unit)
            ch = Chain(dve, chain, 12 * NG * B + SETUP - 2)
            for kind, k, n in last_unit():
                section(kind, k, n, B - 1, NG - 1, ch)


def hybrid_block(nc, ins, out):
    def scratch(name, shape):
        return nc.dram_tensor(name, shape, F32, kind="Internal").ap()

    with ExitStack() as ctx:
        scores = ctx.enter_context(nc.sbuf_tensor("scores", [P, NT, B, E], F32))
        slot_token = ctx.enter_context(nc.sbuf_tensor("slot_token", [P, E, CT], I32))
        slot_weight = ctx.enter_context(nc.sbuf_tensor("slot_weight", [P, E, CT], F32))
        xnT = scratch("xnT", (B, P, KC, T))
        xn = scratch("xn", (B, T, C))
        x1 = scratch("x1", (B, T, C))
        x2 = scratch("x2", (B, T, C))
        x3 = scratch("x3", (B, T, C))
        heads = scratch("heads", (B, T, C))
        trips = {"band": scratch("band", (2, 2, NT, P, HG * WIN)), "prob": scratch("prob", (2, P, HG * WIN))}
        ident = ins["ident"]

        def mixture(tag, x, y):
            with nc.sbuf_tensor(f"{tag}_st", [P, T], F32) as st, nc.sbuf_tensor(f"{tag}_thr", [P, 1], F32) as thr:
                shared_stage(nc, f"{tag}s", ins, scores, st, thr, xnT, x, ins["SgT"], ins["SuT"], ins["SdT"], y)
                route_stage(nc, f"{tag}r", ins, scores, st, thr, slot_token, slot_weight)
            expert_stage(nc, f"{tag}e", ident, xn, slot_token, slot_weight, ins["WgT"], ins["WuT"], ins["WdT"], y)

        norm_stage(nc, "n0", ident, ins["x"], xnT)
        relative_stage(nc, "a", ins, xnT, (ins["a_wT"], ins["a_wv"]), ins["a_rows"], ins["a_table"], ins["a_base"],
                       ins["a_bins"], ins["a_bins_base"], ins["a_vbase"], trips, heads)
        norm_stage(nc, "n1", ident, ins["x"], xnT, attn=(heads, ins["a_projT"], ins["a_bias"]), x1_d=x1, xn_d=xn, gate=ins["gateT"], scores=scores)
        mixture("f", x1, x2)
        norm_stage(nc, "n2", ident, x2, xnT)
        window_stage(nc, "b", ins, x2, xnT, ins["b_wqT"], ins["b_wkT"], ins["b_wvT"], ins["b_woT"], ins["b_gamma"], ins["b_bias"], x3)
        norm_stage(nc, "n3", ident, x3, xnT, xn_d=xn, gate=ins["gateT"], scores=scores)
        mixture("g", x3, out)



def constants():
    p = np.arange(P)
    f = np.float32
    row_scale, row_shift = np.zeros((P, 4), f), np.zeros((P, 4), f)
    for h in range(HG):
        o = 32 * h
        row_scale[o:o + AD + 2, 0] = A_SCALE
        row_shift[o + AD + 2:o + AD + 4, 0] = 1
        row_scale[o:o + AD, 1] = 1
        row_scale[o + AD + 2:o + AD + 4, 1] = A_SCALE
    spread = np.zeros((P, 2, 2, 2, P), f)
    for h in range(2):
        for j in range(3):
            o = 64 * h + A_ROWS * j
            for i in range(2):
                row_scale[o:o + AD, 2 + i] = 1
                row_scale[o + AD + 2 + i, 2 + i] = 1
                row_shift[o + AD + i, 2 + i] = STACKED[1][j] == 0
            for d in range(2):
                for pair in range(2):
                    for r in range(A_ROWS):
                        spread[32 * (2 * pair + h) + r, d, pair, STACKED[d][j], o + r] = 1
    m = np.arange(NT * B)
    slopes = np.array([2.0 ** (-8.0 / BH * (h + 1)) for h in range(BH)], f)
    dist = np.arange(2 * P)[None] - P - p[:, None]
    masked = (dist > 0) | (dist < -WINDOW)
    b_bias = np.where(masked[:, None], f(-1e9 / B_SCALE), slopes[None, :, None] * dist[:, None].astype(f) / f(B_SCALE))
    same = p[:, None] % E == p[None] % E
    return {
        "ident": np.eye(P, dtype=f),
        "lower": (p[None] < p[:, None]).astype(f),
        "upper": (p[None] > p[:, None]).astype(f),
        "row_scale": row_scale,
        "row_shift": row_shift,
        "spread": spread,
        "same": same.astype(f),
        "bits": np.tile(np.array(BITS, np.int32), (P, 1)),
        "before": (same & (p[:, None] // E < p[None] // E)).astype(f),
        "iota": np.tile(p.astype(f), (P, 1)),
        "token": ((m % B) * T + (m // B) * P + p[:, None]).astype(f),
        "b_bias": b_bias.astype(f),
    }


def by_chunk(w):
    return np.ascontiguousarray(w.T.reshape(w.shape[1] // P, P, w.shape[0]).transpose(1, 0, 2))


def relative_layout(w_qkv, q_table, k_table, v_table):
    wT = np.zeros((P, 2, NG, KC, P), w_qkv.dtype)
    rows = np.zeros((P, 2, NG, C), w_qkv.dtype)
    table = np.zeros((P, 2, NG, HG, XB + 1), k_table.dtype)
    base = np.zeros_like(table)
    bins = np.zeros((P, NG, 2, 64), v_table.dtype)
    bins_base = np.zeros_like(bins)
    last = BUCKETS - 1
    for d, tab in enumerate((k_table, q_table)):
        first_end, low_end, up_end = HALF + 1 + d, (0, last)[d], (last, 0)[d]
        for h in range(AH):
            g, r = h // HG, slice(32 * (h % HG), 32 * (h % HG) + AD)
            w = w_qkv[d * C + h * AD:d * C + (h + 1) * AD]
            rows[r, d, g] = w
            wT[:, d, g, :, r] = w.T.reshape(KC, P, AD).transpose(1, 0, 2)
            table[r, d, g, h % HG, 1:XB] = tab[h]
            base[r, d, g, h % HG, 1:first_end] = tab[h][:, 0:1]
            base[r, d, g, h % HG, first_end:XB] = tab[h][:, last:]
            table[r, d, g, h % HG, XB] = tab[h][:, low_end]
            base[r, d, g, h % HG, XB] = tab[h][:, up_end]
    for h in range(AH):
        g, r, x, c = h // HG, h % HG // 2, XB * (h % 2), slice(32 * (h % 2), 32 * (h % 2) + AD)
        bins[x, g, r, c] = v_table[h, 0]
        bins[x + 1:x + XB, g, r, c] = v_table[h]
        bins_base[x + 1:x + 1 + HALF, g, r, c] = v_table[h, 0]
        bins_base[x + 1 + HALF:x + XB, g, r, c] = v_table[h, last]
        bins_base[x, g, r, c] = v_table[h, last]
    ends = np.stack([v_table[:, 0].reshape(C), v_table[:, last].reshape(C)])
    return {
        "a_wT": wT, "a_wv": by_chunk(w_qkv[2 * C:]), "a_rows": rows, "a_table": table, "a_base": base,
        "a_bins": bins, "a_bins_base": bins_base, "a_vbase": np.tile(ends, (P, 1, 1)),
    }


def kernel(L0_attn_a_x, L0_attn_a_w_qkv, L0_attn_a_w_proj, L0_attn_a_b_proj, L0_attn_a_rpe_q_table, L0_attn_a_rpe_k_table,
           L0_attn_a_rpe_v_table, L0_attn_b_wq, L0_attn_b_wk, L0_attn_b_wv, L0_attn_b_wo, L0_attn_b_q_gamma, L0_attn_b_k_gamma,
           L0_ffn_gate_w, L0_ffn_Wg, L0_ffn_Wu, L0_ffn_Wd, L0_ffn_Sg, L0_ffn_Su, L0_ffn_Sd):
    import concourse.bacc as bacc
    from concourse.bass_utils import run_bass_kernel_spmd

    a = np.asarray
    arrays = {
        "x": a(L0_attn_a_x),
        "a_projT": by_chunk(a(L0_attn_a_w_proj)),
        "a_bias": np.tile(a(L0_attn_a_b_proj), (P, 1)),
        "b_wqT": by_chunk(a(L0_attn_b_wq)),
        "b_wkT": by_chunk(a(L0_attn_b_wk)),
        "b_wvT": by_chunk(a(L0_attn_b_wv)),
        "b_woT": by_chunk(a(L0_attn_b_wo)),
        "b_gamma": np.tile(np.stack([a(L0_attn_b_q_gamma), a(L0_attn_b_k_gamma)]), (P, 1, 1)),
        "gateT": by_chunk(a(L0_ffn_gate_w)),
        "WgT": np.stack([by_chunk(w) for w in a(L0_ffn_Wg)]),
        "WuT": np.stack([by_chunk(w) for w in a(L0_ffn_Wu)]),
        "WdT": np.stack([by_chunk(w) for w in a(L0_ffn_Wd)]),
        "SgT": by_chunk(a(L0_ffn_Sg)),
        "SuT": by_chunk(a(L0_ffn_Su)),
        "SdT": by_chunk(a(L0_ffn_Sd)),
        **relative_layout(a(L0_attn_a_w_qkv), a(L0_attn_a_rpe_q_table), a(L0_attn_a_rpe_k_table), a(L0_attn_a_rpe_v_table)),
        **constants(),
    }
    nc = bacc.Bacc("TRN2", target_bir_lowering=False, num_devices=1)
    ins = {name: nc.dram_tensor(f"in_{name}", x.shape, mybir.dt.from_np(x.dtype), kind="ExternalInput").ap() for name, x in arrays.items()}
    out = nc.dram_tensor("out", (B, T, C), F32, kind="ExternalOutput").ap()
    hybrid_block(nc, ins, out)
    result = run_bass_kernel_spmd(nc, [{f"in_{name}": np.ascontiguousarray(x) for name, x in arrays.items()}], core_ids=[0])
    return result.results[0]["out"]
```
